# Optimizing a Trainium2 kernel written in Bass

```python
import numpy as np
import jax
import jax.numpy as jnp

def _softmax(x, axis=-1):
    return jax.nn.softmax(x, axis=axis)

def _gelu(x):
    return jax.nn.gelu(x, approximate=True)

def _silu(x):
    return jax.nn.silu(x)

def _sigmoid(x):
    return jax.nn.sigmoid(x)

def _layernorm(x, axis=-1, eps=1e-05):
    m = jnp.mean(x, axis=axis, keepdims=True)
    v = jnp.var(x, axis=axis, keepdims=True)
    return (x - m) / jnp.sqrt(v + eps)

def _scatter_add(tgt, idx, src, axis=0):
    return tgt.at[idx].add(src)

def _segment_sum(src, seg, n):
    return jax.ops.segment_sum(src, seg, n)
kernel_name = 'mk_gnn_ffn_d2_gnn_r8_044769'

def setup_inputs(seed: int=0):
    np.random.seed(seed)
    _w = jnp.asarray

    def _rec_inputs():
        import jax
        import jax.numpy as jnp
        _gk = jax.random.key(seed)
        x = -0.0002117 + 1 * jax.random.normal(jax.random.fold_in(_gk, 1), (12500, 256), jnp.float32)
        _s = jax.random.randint(jax.random.fold_in(_gk, 2), (100000,), 0, 12500, jnp.int32)
        _d = jax.random.randint(jax.random.fold_in(_gk, 3), (100000,), 0, 12500, jnp.int32)
        _loop = jnp.arange(12500, dtype=jnp.int32)
        src = jnp.concatenate([_s, _d, _loop])
        dst = jnp.concatenate([_d, _s, _loop])
        _o = jnp.argsort(dst, stable=True)
        src = src[_o]
        dst = dst[_o]
        return (x, src, dst)
    x, src, dst = _rec_inputs()

    def _L0_gnn_setup():
        import jax, jax.numpy as jnp
        import numpy as np
        N_NODES = 12500
        N_EDGES = 400000
        IN_F = 256
        OUT_F = 256
        NEG_SLOPE = 0.2
        key = jax.random.key(seed)
        ks = jax.random.split(key, 8)
        x = jax.random.normal(ks[0], (N_NODES, IN_F), dtype=jnp.float32)
        Wv = jax.random.normal(ks[1], (IN_F, OUT_F), dtype=jnp.float32) / np.sqrt(IN_F)
        bv = jnp.zeros((OUT_F,), dtype=jnp.float32)
        wq = jax.random.normal(ks[2], (OUT_F,), dtype=jnp.float32) / np.sqrt(OUT_F)
        bq = jnp.zeros((), dtype=jnp.float32)
        wk = jax.random.normal(ks[3], (OUT_F,), dtype=jnp.float32) / np.sqrt(OUT_F)
        bk = jnp.zeros((), dtype=jnp.float32)
        src = jax.random.randint(ks[4], (N_EDGES,), 0, N_NODES, dtype=jnp.int32)
        dst = jax.random.randint(ks[5], (N_EDGES,), 0, N_NODES, dtype=jnp.int32)
        return {'x': x, 'Wv': Wv, 'bv': bv, 'wq': wq, 'bq': bq, 'wk': wk, 'bk': bk, 'src': src, 'dst': dst}
    _L0_gnn_all = _L0_gnn_setup()
    _L0_gnn_in = {k: v for k, v in _L0_gnn_all.items() if k in ('Wv', 'bv', 'wq', 'bq', 'wk', 'bk')}
    del _L0_gnn_all

    def _L0_ffn_setup():
        import math
        import jax, jax.numpy as jnp
        import numpy as np
        CAPACITY_FACTOR = 1.25
        TOP_K = 2
        LN_EPS = 1e-05

        def _layer_norm(x, gamma, beta):
            mu = jnp.mean(x, axis=-1, keepdims=True)
            var = jnp.var(x, axis=-1, keepdims=True)
            return (x - mu) * jax.lax.rsqrt(var + LN_EPS) * gamma + beta
        key = jax.random.key(seed)
        ks = jax.random.split(key, 4)
        B, S, D, F, E = (8, 512, 256, 512, 8)
        x = jax.random.normal(ks[0], (B, S, D), dtype=jnp.float32)
        Wr = jax.random.normal(ks[1], (D, E), dtype=jnp.float32) / np.sqrt(D)
        br = jnp.zeros((E,), jnp.float32)
        W1 = jax.random.normal(ks[2], (E, D, F), dtype=jnp.float32) / np.sqrt(D)
        b1 = jnp.zeros((E, F), jnp.float32)
        W2 = jax.random.normal(ks[3], (E, F, D), dtype=jnp.float32) / np.sqrt(F)
        b2 = jnp.zeros((E, D), jnp.float32)
        gamma = jnp.ones((D,), jnp.float32)
        beta = jnp.zeros((D,), jnp.float32)
        return {'x': x, 'Wr': Wr, 'br': br, 'W1': W1, 'b1': b1, 'W2': W2, 'b2': b2, 'gamma': gamma, 'beta': beta}
    _L0_ffn_all = _L0_ffn_setup()
    _L0_ffn_in = {k: v for k, v in _L0_ffn_all.items() if k in ('Wr', 'br', 'W1', 'b1', 'W2', 'b2', 'gamma', 'beta')}
    del _L0_ffn_all

    def _L1_gnn_setup():
        import jax, jax.numpy as jnp
        import numpy as np
        N_NODES = 1250
        N_EDGES = 40000
        DIM = 256
        NUM_HEADS = 8
        HEAD_DIM = DIM // NUM_HEADS
        key = jax.random.key(seed)
        ks = jax.random.split(key, 8)
        s = 1.0 / np.sqrt(DIM)
        x = jax.random.normal(ks[0], (N_NODES, DIM), dtype=jnp.float32)
        src = jax.random.randint(ks[1], (N_EDGES,), 0, N_NODES, dtype=jnp.int32)
        dst = jax.random.randint(ks[2], (N_EDGES,), 0, N_NODES, dtype=jnp.int32)
        Wq = jax.random.normal(ks[3], (DIM, DIM), dtype=jnp.float32) * s
        Wk = jax.random.normal(ks[4], (DIM, DIM), dtype=jnp.float32) * s
        Wv = jax.random.normal(ks[5], (DIM, DIM), dtype=jnp.float32) * s
        Wo = jax.random.normal(ks[6], (DIM, DIM), dtype=jnp.float32) * s
        z = jnp.zeros((DIM,), dtype=jnp.float32)
        return {'x': x, 'src': src, 'dst': dst, 'Wq': Wq, 'bq': z, 'Wk': Wk, 'bk': z, 'Wv': Wv, 'bv': z, 'Wo': Wo, 'bo': z}
    _L1_gnn_all = _L1_gnn_setup()
    _L1_gnn_in = {k: v for k, v in _L1_gnn_all.items() if k in ('Wq', 'bq', 'Wk', 'bk', 'Wv', 'bv', 'Wo', 'bo')}
    del _L1_gnn_all

    def _L1_ffn_setup():
        import jax, jax.numpy as jnp
        import numpy as np
        B, S, D = (8, 512, 256)
        H = 4 * D
        CAPACITY = 0.5
        key = jax.random.key(seed)
        ks = jax.random.split(key, 6)
        x = jax.random.normal(ks[0], (B, S, D), dtype=jnp.float32)
        attention_mask = jnp.zeros((B, 1, 1, S), dtype=jnp.float32)
        wr = jax.random.normal(ks[1], (D, 1), dtype=jnp.float32) * 0.02
        br = jnp.zeros((1,), dtype=jnp.float32)
        w1 = jax.random.normal(ks[2], (D, H), dtype=jnp.float32) * 0.02
        b1 = jnp.zeros((H,), dtype=jnp.float32)
        w2 = jax.random.normal(ks[3], (H, D), dtype=jnp.float32) * 0.02
        b2 = jnp.zeros((D,), dtype=jnp.float32)
        return {'x': x, 'attention_mask': attention_mask, 'wr': wr, 'br': br, 'w1': w1, 'b1': b1, 'w2': w2, 'b2': b2}
    _L1_ffn_all = _L1_ffn_setup()
    _L1_ffn_in = {k: v for k, v in _L1_ffn_all.items() if k in ('attention_mask', 'wr', 'br', 'w1', 'b1', 'w2', 'b2')}
    del _L1_ffn_all
    return {'x': x, 'src': src, 'dst': dst, 'L0_gnn_Wv': _L0_gnn_in['Wv'], 'L0_gnn_bv': _L0_gnn_in['bv'], 'L0_gnn_wq': _L0_gnn_in['wq'], 'L0_gnn_bq': _L0_gnn_in['bq'], 'L0_gnn_wk': _L0_gnn_in['wk'], 'L0_gnn_bk': _L0_gnn_in['bk'], 'L0_ffn_Wr': _L0_ffn_in['Wr'], 'L0_ffn_br': _L0_ffn_in['br'], 'L0_ffn_W1': _L0_ffn_in['W1'], 'L0_ffn_b1': _L0_ffn_in['b1'], 'L0_ffn_W2': _L0_ffn_in['W2'], 'L0_ffn_b2': _L0_ffn_in['b2'], 'L0_ffn_gamma': _L0_ffn_in['gamma'], 'L0_ffn_beta': _L0_ffn_in['beta'], 'L1_gnn_Wq': _L1_gnn_in['Wq'], 'L1_gnn_bq': _L1_gnn_in['bq'], 'L1_gnn_Wk': _L1_gnn_in['Wk'], 'L1_gnn_bk': _L1_gnn_in['bk'], 'L1_gnn_Wv': _L1_gnn_in['Wv'], 'L1_gnn_bv': _L1_gnn_in['bv'], 'L1_gnn_Wo': _L1_gnn_in['Wo'], 'L1_gnn_bo': _L1_gnn_in['bo'], 'L1_ffn_attention_mask': _L1_ffn_in['attention_mask'], 'L1_ffn_wr': _L1_ffn_in['wr'], 'L1_ffn_br': _L1_ffn_in['br'], 'L1_ffn_w1': _L1_ffn_in['w1'], 'L1_ffn_b1': _L1_ffn_in['b1'], 'L1_ffn_w2': _L1_ffn_in['w2'], 'L1_ffn_b2': _L1_ffn_in['b2']}

def reference(x, src, dst, L0_gnn_Wv, L0_gnn_bv, L0_gnn_wq, L0_gnn_bq, L0_gnn_wk, L0_gnn_bk, L0_ffn_Wr, L0_ffn_br, L0_ffn_W1, L0_ffn_b1, L0_ffn_W2, L0_ffn_b2, L0_ffn_gamma, L0_ffn_beta, L1_gnn_Wq, L1_gnn_bq, L1_gnn_Wk, L1_gnn_bk, L1_gnn_Wv, L1_gnn_bv, L1_gnn_Wo, L1_gnn_bo, L1_ffn_attention_mask, L1_ffn_wr, L1_ffn_br, L1_ffn_w1, L1_ffn_b1, L1_ffn_w2, L1_ffn_b2):
    import jax
    import jax.numpy as jnp

    def _L0_gnn_ref(x, Wv, bv, wq, bq, wk, bk, src, dst):
        import jax, jax.numpy as jnp
        import numpy as np
        N_NODES = 12500
        N_EDGES = 400000
        IN_F = 256
        OUT_F = 256
        NEG_SLOPE = 0.2
        n = x.shape[0]
        h = x @ Wv + bv
        q = h @ wq + bq
        k = h @ wk + bk
        e = q[src] + k[dst]
        c = jnp.where(e > 0, e, NEG_SLOPE * e)
        m = jax.ops.segment_max(c, dst, num_segments=n)
        ex = jnp.exp(c - m[dst])
        s = jax.ops.segment_sum(ex, dst, num_segments=n)
        attn = ex / s[dst]
        msg = h[src] * attn[:, None]
        out = jax.ops.segment_sum(msg, dst, num_segments=n)
        return out

    def _L0_ffn_ref(x, Wr, br, W1, b1, W2, b2, gamma, beta):
        import math
        import jax, jax.numpy as jnp
        import numpy as np
        CAPACITY_FACTOR = 1.25
        TOP_K = 2
        LN_EPS = 1e-05

        def _layer_norm(x, gamma, beta):
            mu = jnp.mean(x, axis=-1, keepdims=True)
            var = jnp.var(x, axis=-1, keepdims=True)
            return (x - mu) * jax.lax.rsqrt(var + LN_EPS) * gamma + beta
        B, S, D = x.shape
        E = Wr.shape[1]
        N = B * S
        K = TOP_K
        logits = jnp.mean(x, axis=1) @ Wr + br
        routing_weights = jax.nn.softmax(logits, axis=-1)
        capacity = float(math.ceil(N * CAPACITY_FACTOR / E))
        expected_loads = routing_weights.sum(axis=0) * (N / B)
        scale = jnp.where(expected_loads > capacity, capacity / expected_loads, 1.0)
        routing_weights = jax.nn.softmax(routing_weights * scale, axis=-1)
        rw_tok = jnp.broadcast_to(routing_weights[:, None, :], (B, S, E)).reshape(N, E)
        top_w, top_i = jax.lax.top_k(rw_tok, K)
        top_w = jax.nn.softmax(top_w, axis=-1)
        xf = x.reshape(N, D)
        h = jax.nn.gelu(jnp.einsum('nd,edf->enf', xf, W1) + b1[:, None, :], approximate=False)
        y = jnp.einsum('enf,efd->end', h, W2) + b2[:, None, :]
        w_dense = jnp.zeros((N, E), x.dtype).at[jnp.arange(N)[:, None], top_i].add(top_w)
        out = jnp.einsum('ne,end->nd', w_dense, y).reshape(B, S, D)
        out = _layer_norm(out + x, gamma, beta)
        return out

    def _L1_gnn_ref(x, src, dst, Wq, bq, Wk, bk, Wv, bv, Wo, bo):
        import jax, jax.numpy as jnp
        import numpy as np
        N_NODES = 1250
        N_EDGES = 40000
        DIM = 256
        NUM_HEADS = 8
        HEAD_DIM = DIM // NUM_HEADS
        N = x.shape[0]
        q = (x @ Wq.T + bq).reshape(N, NUM_HEADS, HEAD_DIM)
        k = (x @ Wk.T + bk).reshape(N, NUM_HEADS, HEAD_DIM)
        v = (x @ Wv.T + bv).reshape(N, NUM_HEADS, HEAD_DIM)
        score = jnp.einsum('ehd,ehd->eh', q[src], k[dst]) / np.sqrt(HEAD_DIM).astype(np.float32)
        attn = jax.nn.softmax(score, axis=1)
        m = v[src] * attn[:, :, None]
        h = jax.ops.segment_sum(m, dst, num_segments=N).reshape(N, DIM)
        out = h @ Wo.T + bo
        return out

    def _L1_ffn_ref(x, attention_mask, wr, br, w1, b1, w2, b2):
        import jax, jax.numpy as jnp
        import numpy as np
        B, S, D = (8, 512, 256)
        H = 4 * D
        CAPACITY = 0.5
        b, s, d = x.shape
        weights = (jnp.einsum('bsd,do->bso', x, wr) + br)[..., 0]
        k = max(1, int(CAPACITY * s))
        kk = k - 1 if k > 1 else 1
        _, idx = jax.lax.top_k(weights, k)
        sel_idx = idx[:, :kk]
        sel = jnp.take_along_axis(x, sel_idx[:, :, None], axis=1)
        h = jax.nn.gelu(jnp.einsum('bkd,dh->bkh', sel, w1) + b1)
        y = jnp.einsum('bkh,hd->bkd', h, w2) + b2
        w_sel = jnp.take_along_axis(weights, sel_idx, axis=1)
        y = y * w_sel[..., None]
        batch_idx = jnp.arange(b)[:, None]
        processed = jnp.zeros_like(x).at[batch_idx, sel_idx].set(y)
        return processed + x
    x = x + _L0_gnn_ref(_layernorm(x, axis=-1), L0_gnn_Wv, L0_gnn_bv, L0_gnn_wq, L0_gnn_bq, L0_gnn_wk, L0_gnn_bk, src, dst)
    x = x + _L0_ffn_ref(_layernorm(x, axis=-1)[None], L0_ffn_Wr, L0_ffn_br, L0_ffn_W1, L0_ffn_b1, L0_ffn_W2, L0_ffn_b2, L0_ffn_gamma, L0_ffn_beta)[0]
    x = x + _L1_gnn_ref(_layernorm(x, axis=-1), src, dst, L1_gnn_Wq, L1_gnn_bq, L1_gnn_Wk, L1_gnn_bk, L1_gnn_Wv, L1_gnn_bv, L1_gnn_Wo, L1_gnn_bo)
    x = x + _L1_ffn_ref(_layernorm(x, axis=-1)[None], L1_ffn_attention_mask, L1_ffn_wr, L1_ffn_br, L1_ffn_w1, L1_ffn_b1, L1_ffn_w2, L1_ffn_b2)[0]
    return x

_drawn_inputs = setup_inputs


def setup_inputs(seed=0):
    import zlib

    import numpy as np

    out = dict(_drawn_inputs(seed))
    spreads = {'L0_gnn_bv': (0.0, 0.1),
     'L0_ffn_br': (0.0, 0.1),
     'L0_ffn_b1': (0.0, 0.3),
     'L0_ffn_b2': (0.0, 0.1),
     'L0_ffn_gamma': (1.0, 0.2),
     'L0_ffn_beta': (0.0, 0.1),
     'L1_gnn_bq': (0.0, 0.274),
     'L1_gnn_bk': (0.0, 0.303),
     'L1_gnn_bv': (0.0, 0.1),
     'L1_gnn_bo': (0.0, 0.1),
     'L1_ffn_b1': (0.0, 0.8),
     'L1_ffn_b2': (0.0, 0.8)}
    factors = {'L1_ffn_wr': 7.047, 'L1_ffn_w1': 8.0, 'L1_ffn_w2': 7.608}
    for name, (base, spread) in spreads.items():
        noise = np.random.default_rng([zlib.crc32(name.encode()), seed]).standard_normal(out[name].shape)
        drawn = base * np.exp(spread * noise) if base else spread * noise
        out[name] = jnp.asarray(drawn.astype(out[name].dtype))
    for name, factor in factors.items():
        out[name] = (out[name] * factor).astype(out[name].dtype)
    return out
```

```python
from contextlib import ExitStack

import concourse.bass as bass
from concourse import mybir

F32 = mybir.dt.float32
BF16 = mybir.dt.bfloat16
I32 = mybir.dt.int32
ALU = mybir.AluOpType
ACT = mybir.ActivationFunctionType
X = mybir.AxisListType.X

P = 128
N = 12500
D = 256
TILES = (N + P - 1) // P
NPAD = TILES * P
LAST = N - (TILES - 1) * P
EDGES = 212500
EROW = 256
EROWS = (EDGES + EROW - 1) // EROW
ITEMS = EROWS + TILES - 1
GROUP = 4
GROUPS = ITEMS // GROUP
IBLOCKS = (ITEMS + P - 1) // P
IPAD = IBLOCKS * P
CH = EROW // P
COLS = GROUP * CH
HEADS = 8
HD = D // HEADS
EXPERTS = 8
HID = 1024
HB = HID // P
KD = D // P
EPS = 1e-5
BIG = 1e30
TOPK = N // 2 - 1
CAPACITY = float(-(-N * 5 // (4 * EXPERTS)))
QCOL, ONECOL, SCOL, HCOLS = D, D + 1, D + 2, D + 3
assert ITEMS % (2 * GROUP) == 0 and TILES % 2 == 0


def ds(start, size):
    return bass.ds(start, size)


def pairs(eng, n, body):
    for u in (0, 1):
        body(0, u)
    with eng.Fori(1, n // 2) as i:
        for u in (0, 1):
            body(i, u)


def before(i, u):
    if u == 1:
        return i, 0
    return None if isinstance(i, int) and i == 0 else (i - 1, 1)


def first(i):
    return isinstance(i, int) and i == 0


def linker(eng, sem, base):
    count = [0]

    def link(ins):
        count[0] += 1
        ins.then_inc(sem, 1)
        eng.wait_ge(sem, base + count[0])

    link.count = count
    return link


class Shared:
    pass


def constants(nc, s):
    sem_iota, sem_c = s.sem("c_iota"), s.sem("c_made")
    with nc.Block() as block:
        @block.gpsimd
        def _(g):
            g.iota(s.iota_i[:, :], pattern=[[1, IPAD]], base=0, channel_multiplier=0).then_inc(sem_iota, 1)
            g.iota(s.part_i[:, :], pattern=[[0, 1]], base=0, channel_multiplier=1).then_inc(sem_iota, 1)
            g.iota(s.node_i[:, :], pattern=[[P, TILES]], base=0, channel_multiplier=1).then_inc(sem_iota, 1)

        @block.vector
        def _(v):
            link = linker(v, sem_c, 0)
            v.memset(s.ones[:, :], 1.0)
            v.memset(s.half[:, :], -0.5)
            v.memset(s.acc[:, :, :], 0.0)
            v.wait_ge(sem_iota, 3)
            v.tensor_copy(s.iota[:, :], s.iota_i[:, :])
            v.tensor_copy(s.node[:, :], s.node_i[:, :])
            link(v.tensor_copy(s.part[:, :], s.part_i[:, :]))
            link(v.tensor_scalar(s.ident[:, :], s.iota[:, 0:P], s.part[:, 0:1], None, ALU.is_equal))


def item_tables(nc, s, src2, dst2):
    with ExitStack() as ctx:
        def sb(name, shape, dt):
            return ctx.enter_context(nc.sbuf_tensor(name, shape, dt))

        def ps(name, shape, dt=F32):
            return ctx.enter_context(nc.psum_tensor(name, shape, dt))

        first_i = sb("t_first_i", [1, EROWS], I32)
        first_f = sb("t_first_f", [1, EROWS], F32)
        below = sb("t_below", [P, EROWS], F32)
        cnt = sb("t_cnt", [P, 1], F32)
        begins = sb("t_begins", [P, 1], F32)
        bound = sb("t_bound", [P, 1], F32)
        valid = sb("t_valid", [P, P], BF16)
        vcol = sb("t_vcol", [P, 2], F32)
        step = sb("t_step", [P, IPAD], BF16)
        tcol = sb("t_tcol", [P, IBLOCKS], F32)
        tbase = sb("t_tbase", [P, IBLOCKS], F32)
        grow = sb("t_grow", [P, IBLOCKS], F32)
        growi = sb("t_growi", [P, IBLOCKS], I32)
        srcb = sb("t_srcb", [P, 2, EROW], I32)
        dstb = sb("t_dstb", [P, 2, EROW], I32)
        srcf = sb("t_srcf", [P, 2, EROW], F32)
        dloc = sb("t_dloc", [P, 2, EROW], F32)
        dlocb = sb("t_dlocb", [P, 2, EROW], BF16)
        seg = sb("t_seg", [P, 2, EROW + 1], F32)
        trep = sb("t_trep", [P, IPAD], F32)
        bc = [ps(f"t_bc{i}", [P, 512]) for i in range(2)]
        pt = [ps(f"t_pt{i}", [P, 512]) for i in range(2)]
        pc = ps("t_pc", [P, 512])
        px = [ps(f"t_px{i}", [P, 2, CH, P]) for i in range(2)]
        m_first, m_ff, m_bc, m_v = s.sem("t_first"), s.sem("t_ff"), s.sem("t_bc"), s.sem("t_v")
        m_step, m_t, m_idx = s.sem("t_step"), s.sem("t_t"), s.sem("t_idx")
        m_rows = [s.sem(f"t_rows{u}") for u in (0, 1)]
        m_loc, m_x, m_done = s.sem("t_loc"), s.sem("t_x"), s.sem("t_done")
        m_st = [s.sem(f"t_st{u}") for u in (0, 1)]
        half = EROWS // 2

        with nc.Block() as block:
            @block.sync
            def _(sp):
                with nc.allow_non_contiguous_dma(reason="one element of each edge row"):
                    sp.dma_start(first_i[:, :], dst2[:, 0:1].rearrange("r o -> o r")).then_inc(m_first, 16)
                for b in range(IBLOCKS):
                    u = b % 2
                    sp.wait_ge(m_loc, b + 1)
                    sp.dma_start(s.drow_d[b * P:(b + 1) * P, :], dlocb[:, u, :]).then_inc(m_st[u], 16)
                    sp.dma_start(s.seg_d[b * P:(b + 1) * P, :], seg[:, u, :]).then_inc(m_st[u], 16)
                for u in (0, 1):
                    sp.wait_ge(m_st[u], 32 * (IBLOCKS // 2))

            @block.tensor
            def _(pe):
                pe.wait_ge(m_ff, 1)
                pe.matmul(bc[0][:, 0:half], s.ones[0:1, :], first_f[:, 0:half], start=True, stop=True)
                pe.matmul(bc[1][:, 0:EROWS - half], s.ones[0:1, :], first_f[:, half:], start=True,
                          stop=True).then_inc(m_bc, 1)
                pe.wait_ge(m_step, 1)
                for k in range(2):
                    pe.matmul(pt[k][:, :], valid[:, :], step[:, k * 512:(k + 1) * 512], start=True, stop=True)
                for b in range(IBLOCKS):
                    last = pe.matmul(pc[:, b:b + 1], step[:, b * P:(b + 1) * P], valid[:, 0:1], start=True, stop=True)
                last.then_inc(m_t, 1)
                for b in range(IBLOCKS):
                    u = b % 2
                    pe.wait_ge(m_loc, b + 1)
                    if b >= 2:
                        pe.wait_ge(m_done, b - 1)
                    for c in range(CH):
                        pe.transpose(px[u][:, 0, c, :], srcf[:, u, c * P:(c + 1) * P], s.ident[:, :])
                        last = pe.transpose(px[u][:, 1, c, :], dloc[:, u, c * P:(c + 1) * P], s.ident[:, :])
                    last.then_inc(m_x, 1)

            @block.gpsimd
            def _(g):
                g.wait_ge(m_idx, 1)
                for b in range(IBLOCKS):
                    u = b % 2
                    if b >= 2:
                        g.wait_ge(m_loc, b - 1)
                    for buf, table in ((srcb, src2), (dstb, dst2)):
                        g.indirect_dma_start(buf[:, u, :], None, table,
                                             bass.IndirectOffsetOnAxis(ap=growi[:, b:b + 1], axis=0)
                                             ).then_inc(m_rows[u], 16)

            @block.vector
            def _(v):
                link = linker(v, m_v, 0)
                v.wait_ge(m_first, 16)
                v.tensor_copy(first_f[:, :], first_i[:, :]).then_inc(m_ff, 1)
                link(v.tensor_scalar(bound[:, :], s.part[:, :], float(P), None, ALU.mult))
                link(v.tensor_scalar(vcol[:, 0:1], s.part[:, :], 1.0, None, ALU.is_ge))
                link(v.tensor_scalar(vcol[:, 1:2], s.part[:, :], float(TILES), None, ALU.is_lt))
                link(v.tensor_tensor(vcol[:, 0:1], vcol[:, 0:1], vcol[:, 1:2], ALU.mult))
                link(v.tensor_scalar(valid[:, :], s.ones[:, :], vcol[:, 0:1], None, ALU.mult))
                v.wait_ge(m_bc, 1)
                link(v.tensor_scalar(below[:, 0:half], bc[0][:, 0:half], bound[:, 0:1], None, ALU.is_lt))
                link(v.tensor_scalar(below[:, half:], bc[1][:, 0:EROWS - half], bound[:, 0:1], None, ALU.is_lt))
                link(v.tensor_reduce(cnt[:, :], below[:, 1:EROWS], X, ALU.add))
                link(v.tensor_tensor(begins[:, :], cnt[:, :], s.part[:, :], ALU.add))
                link(v.tensor_scalar(step[:, :], s.iota[:, :], begins[:, 0:1], None, ALU.is_ge))
                v.sem_inc(m_step, 1)
                v.wait_ge(m_t, 1)
                for k in range(2):
                    v.tensor_copy(s.tile_i[:, k * 512:(k + 1) * 512], pt[k][0:1, :])
                    link(v.tensor_copy(trep[:, k * 512:(k + 1) * 512], pt[k][:, :]))
                link(v.memset(s.fresh[:, 0:1], 1.0))
                link(v.tensor_tensor(s.fresh[:, 1:IPAD], trep[:, 1:IPAD], trep[:, 0:IPAD - 1], ALU.not_equal))
                link(v.tensor_scalar(s.fresh[:, :], s.fresh[:, :], -BIG, None, ALU.mult))
                link(v.tensor_copy(tcol[:, :], pc[:, 0:IBLOCKS]))
                link(v.tensor_scalar(tbase[:, :], tcol[:, :], float(P), None, ALU.mult))
                link(v.tensor_scalar(grow[:, :], s.iota[:, 0:IPAD:P], s.part[:, 0:1], None, ALU.add))
                link(v.tensor_tensor(grow[:, :], grow[:, :], tcol[:, :], ALU.subtract))
                link(v.tensor_scalar(grow[:, :], grow[:, :], float(EROWS - 1), None, ALU.min))
                v.tensor_copy(growi[:, :], grow[:, :]).then_inc(m_idx, 1)
                link(v.memset(seg[:, :, :], 0.0))

                def tables(b):
                    u = b % 2
                    v.wait_ge(m_x, b + 1)
                    v.tensor_copy(s.src_t[:, b * P:(b + 1) * P, :], px[u][:, 0, :, :].rearrange("p c i -> p i c"))
                    v.tensor_copy(s.dst_t[:, b * P:(b + 1) * P, :],
                                  px[u][:, 1, :, :].rearrange("p c i -> p i c")).then_inc(m_done, 1)

                for b in range(IBLOCKS):
                    u = b % 2
                    v.wait_ge(m_rows[u], 32 * (b // 2 + 1))
                    if b >= 2:
                        v.wait_ge(m_st[u], 32 * (b // 2))
                        v.wait_ge(m_x, b - 1)
                    v.tensor_copy(srcf[:, u, :], srcb[:, u, :])
                    link(v.tensor_scalar(dloc[:, u, :], dstb[:, u, :], tbase[:, b:b + 1], None, ALU.subtract))
                    link(v.tensor_tensor(seg[:, u, 1:EROW], dstb[:, u, 1:EROW], dstb[:, u, 0:EROW - 1], ALU.not_equal))
                    link(v.tensor_scalar(seg[:, u, :], seg[:, u, :], -BIG, None, ALU.mult))
                    link(v.tensor_copy(dlocb[:, u, :], dloc[:, u, :]))
                    v.sem_inc(m_loc, 1)
                    if b >= 1:
                        tables(b - 1)
                tables(IBLOCKS - 1)


def norm_stats(v, link, passed, x, st, mv):
    link(v.bn_stats(st, x))
    v.sem_inc(passed, 1)
    link(v.bn_aggr(mv, st))


def project0(nc, s, x, Wv, bv, wq, bq, wk, bk):
    with ExitStack() as ctx:
        def sb(name, shape, dt=F32):
            return ctx.enter_context(nc.sbuf_tensor(name, shape, dt))

        w = sb("a_w", [P, KD, D])
        rows = sb("a_rows", [P, 3, D])
        bqk = sb("a_bqk", [P, 2])
        kcol = sb("a_kcol", [P, 2])
        xin = sb("a_xin", [P, 2, D])
        st = sb("a_st", [P, 2, 6])
        mv = sb("a_mv", [P, 2, 2])
        ve = sb("a_ve", [P, 2])
        rs = sb("a_rs", [P, 2])
        xn = sb("a_xn", [P, 2, D])
        xT = sb("a_xT", [P, 2, KD, P])
        hq = sb("a_hq", [P, 2, D + 1])
        junk = sb("a_junk", [P, 2, D])
        pT = [ctx.enter_context(nc.psum_tensor(f"a_pT{u}", [P, KD, P], F32)) for u in (0, 1)]
        pH = [ctx.enter_context(nc.psum_tensor(f"a_pH{u}", [P, D], F32)) for u in (0, 1)]
        m_w = s.sem("a_w")
        m_x = [s.sem(f"a_x{u}") for u in (0, 1)]
        m_v, m_var, m_rs, m_xn, m_T, m_xT, m_h, m_hq = (s.sem("a_" + n) for n in
                                                         ("v", "var", "rs", "xn", "T", "xT", "h", "hq"))
        m_st = [s.sem(f"a_st{u}") for u in (0, 1)]
        LINKS1, LINKS2 = 2, 4

        with nc.Block() as block:
            @block.sync
            def _(sp):
                sp.dma_start(w[:, :, :], Wv.rearrange("(k p) n -> p k n", p=P)).then_inc(m_w, 16)
                for j, row in enumerate((bv, wq, wk)):
                    sp.dma_start(rows[:, j, :], row.partition_broadcast(P)).then_inc(m_w, 16)
                for j, one in enumerate((bq, bk)):
                    sp.dma_start(bqk[:, j:j + 1], one.partition_broadcast(P)).then_inc(m_w, 16)

                def load(i, u):
                    if not first(i):
                        sp.wait_ge(m_xn, 2 * i + u - 1)
                    sp.dma_start(xin[:, u, :], x[ds((2 * i + u) * P, P), :]).then_inc(m_x[u], 16)

                pairs(sp, TILES, load)

            @block.gpsimd
            def _(g):
                def root(i, u):
                    g.wait_ge(m_var, 2 * i + u + 1)
                    g.tensor_tensor(rs[:, u:u + 1], ve[:, u:u + 1], s.half[:, :], ALU.pow).then_inc(m_rs, 1)

                pairs(g, TILES, root)

            @block.tensor
            def _(pe):
                pe.wait_ge(m_w, 16 * 6)

                def transposes(i, u):
                    pe.wait_ge(m_xn, 2 * i + u + 1)
                    if not first(i):
                        pe.wait_ge(m_xT, 2 * i + u - 1)
                    for k in range(KD):
                        last = pe.transpose(pT[u][:, k, :], xn[:, u, k * P:(k + 1) * P], s.ident[:, :])
                    last.then_inc(m_T, 1)

                def product(i, u):
                    pe.wait_ge(m_xT, 2 * i + u + 1)
                    if not first(i):
                        pe.wait_ge(m_hq, 2 * i + u - 1)
                    for k in range(KD):
                        last = pe.matmul(pH[u][:, :], xT[:, u, k, :], w[:, k, :], start=k == 0, stop=k == KD - 1)
                    last.then_inc(m_h, 1)

                def step(i, u):
                    transposes(i, u)
                    if before(i, u):
                        product(*before(i, u))

                pairs(pe, TILES, step)
                product(TILES // 2 - 1, 1)

            @block.scalar
            def _(act):
                def copy(i, u):
                    act.wait_ge(m_T, 2 * i + u + 1)
                    if not first(i):
                        act.wait_ge(m_h, 2 * i + u - 1)
                    act.copy(xT[:, u, :, :], pT[u][:, :, :]).then_inc(m_xT, 1)

                def store(i, u):
                    act.wait_ge(m_hq, 2 * i + u + 1)
                    act.dma_start(s.hq_d[ds((2 * i + u) * P, P), :], hq[:, u, :]).then_inc(m_st[u], 16)

                def step(i, u):
                    copy(i, u)
                    if before(i, u):
                        store(*before(i, u))

                pairs(act, TILES, step)
                store(TILES // 2 - 1, 1)
                for u in (0, 1):
                    act.wait_ge(m_st[u], 16 * (TILES // 2))

            @block.vector
            def _(v):
                v.wait_ge(m_w, 16 * 6)

                def normalise(i, u, base):
                    link = linker(v, m_v, base)
                    v.wait_ge(m_x[u], 16 * (i + 1))
                    norm_stats(v, link, s.passed, xin[:, u, :], st[:, u, :], mv[:, u, :])
                    v.tensor_scalar(ve[:, u:u + 1], mv[:, u, 1:2], EPS, None, ALU.add).then_inc(m_var, 1)
                    if not first(i):
                        v.wait_ge(m_T, 2 * i + u - 1)
                    v.wait_ge(m_rs, 2 * i + u + 1)
                    v.tensor_scalar(xn[:, u, :], xin[:, u, :], mv[:, u, 0:1], rs[:, u:u + 1], ALU.subtract,
                                    ALU.mult).then_inc(m_xn, 1)
                    assert link.count[0] == LINKS1

                def finish(i, u, base):
                    link = linker(v, m_v, base)
                    t = 2 * i + u
                    v.wait_ge(m_h, t + 1)
                    if not first(i):
                        v.wait_ge(m_st[u], 16 * i)
                    link(v.tensor_tensor(hq[:, u, 0:D], pH[u][:, :], rows[:, 0, :], ALU.add))
                    link(v.tensor_tensor_reduce(junk[:, 0, :], hq[:, u, 0:D], rows[:, 1, :], 1.0, 0.0, ALU.mult,
                                                ALU.add, hq[:, u, D:D + 1]))
                    link(v.tensor_tensor_reduce(junk[:, 1, :], hq[:, u, 0:D], rows[:, 2, :], 1.0, 0.0, ALU.mult,
                                                ALU.add, kcol[:, u:u + 1]))
                    link(v.tensor_scalar(s.k0[:, ds(t, 1)], kcol[:, u:u + 1], bqk[:, 1:2], None, ALU.add))
                    v.tensor_scalar(hq[:, u, D:D + 1], hq[:, u, D:D + 1], bqk[:, 0:1], None, ALU.add).then_inc(m_hq, 1)
                    assert link.count[0] == LINKS2

                def step(i, u):
                    t = 2 * i + u
                    normalise(i, u, t * LINKS1 + ((t - 1) * LINKS2 if before(i, u) else 0))
                    if before(i, u):
                        finish(*before(i, u), (t + 1) * LINKS1 + (t - 1) * LINKS2)

                pairs(v, TILES, step)
                finish(TILES // 2 - 1, 1, TILES * LINKS1 + (TILES - 1) * LINKS2)


def edges0(nc, s):
    with ExitStack() as ctx:
        def sb(name, shape, dt=F32):
            return ctx.enter_context(nc.sbuf_tensor(name, shape, dt))

        R = sb("e_R", [P, 2, GROUP, CH, HCOLS])
        idx = sb("e_idx", [P, 2, COLS], I32)
        drow = sb("e_drow", [P, 2, GROUP, EROW], BF16)
        seg = sb("e_seg", [GROUP, 2, EROW + 1])
        OHT = sb("e_OHT", [P, 2, GROUP, EROW])
        W = sb("e_W", [P, GROUP, CH, P])
        fwd = sb("e_fwd", [GROUP, EROW])
        bwd = sb("e_bwd", [GROUP, EROW])
        mx = sb("e_mx", [GROUP, EROW])
        dcol = sb("e_dcol", [P, COLS])
        kS = sb("e_kS", [P, GROUP, CH])
        z = sb("e_z", [P, 2, GROUP, CH])
        c = sb("e_c", [P, 2, GROUP, CH])
        dd = sb("e_dd", [P, COLS])
        w = sb("e_w", [P, COLS])
        ls = sb("e_ls", [P, 2, GROUP])
        rl = sb("e_rl", [P, GROUP])
        none = sb("e_none", [P, GROUP])
        sn = sb("e_sn", [P, GROUP])
        run = sb("e_run", [P, GROUP + 1])
        old = sb("e_old", [P, GROUP])
        dab = sb("e_dab", [P, 2, GROUP])
        ab = sb("e_ab", [P, 2, GROUP])
        tmp = sb("e_tmp", [P, GROUP, HCOLS])

        def ps(name, shape):
            return ctx.enter_context(nc.psum_tensor(name, shape, F32))

        pA = ps("e_pA", [P, GROUP, 512])
        pK = ps("e_pK", [P, 512])
        pQ = ps("e_pQ", [P, 512])
        pM = ps("e_pM", [P, 512])
        m_idx = s.sem("e_idx")
        m_g = [s.sem(f"e_g{u}") for u in (0, 1)]
        m_row = [s.sem(f"e_row{u}") for u in (0, 1)]
        (m_v, m_one, m_oht, m_k, m_q, m_mx, m_mxe, m_dd, m_w, m_W, m_agg, m_dab, m_ab, m_tmp, m_done) = (
            s.sem("e_" + n) for n in ("v", "one", "oht", "k", "q", "mx", "mxe", "dd", "w", "W", "agg", "dab", "ab",
                                      "tmp", "done"))
        LINKS = 17 + GROUP

        with nc.Block() as block:
            @block.gpsimd
            def _(g):
                def gather(i, u):
                    b = 2 * i + u
                    if not first(i):
                        g.wait_ge(m_agg, b - 1)
                    g.tensor_copy(idx[:, u, :], s.src_t[:, ds(b * GROUP, GROUP), :]).then_inc(m_idx, 1)
                    g.wait_ge(m_idx, b + 1)
                    g.sem_inc(s.passed, 1)
                    for n in range(COLS):
                        g.indirect_dma_start(R[:, u, n // CH, n % CH, 0:D + 1], None, s.hq_d[:, :],
                                             bass.IndirectOffsetOnAxis(ap=idx[:, u, n:n + 1], axis=0)
                                             ).then_inc(m_g[u], 16)

                g.wait_ge(m_one, 1)
                pairs(g, GROUPS, gather)

            @block.sync
            def _(sp):
                def load(i, u):
                    b = 2 * i + u
                    if not first(i):
                        sp.wait_ge(m_mx, b - 1)
                    sp.dma_start(drow[:, u, :, :], s.drow_d[ds(b * GROUP, GROUP), :].partition_broadcast(P)
                                 ).then_inc(m_row[u], 16)
                    sp.dma_start(seg[:, u, :], s.seg_d[ds(b * GROUP, GROUP), :]).then_inc(m_row[u], 16)

                pairs(sp, GROUPS, load)

            @block.tensor
            def _(pe):
                def group(i, u):
                    b = 2 * i + u
                    if before(i, u):
                        pe.wait_ge(m_dd, b)
                    pe.wait_ge(m_oht, b + 1)
                    for n in range(GROUP):
                        tile = pe.value_load(s.tile_i[0:1, ds(b * GROUP + n, 1)], min_val=0, max_val=TILES - 1)
                        for j in range(CH):
                            last = pe.matmul(pK[:, n * CH + j:n * CH + j + 1], OHT[:, u, n, j * P:(j + 1) * P],
                                             s.k0[:, ds(tile, 1)], start=True, stop=True)
                    last.then_inc(m_k, 1)
                    pe.wait_ge(m_g[u], 16 * COLS * (i + 1))
                    for j in range(CH):
                        last = pe.transpose(pQ[0:GROUP, j * P:(j + 1) * P], R[:, u, :, j, QCOL], s.ident[:, :])
                    last.then_inc(m_q, 1)
                    pe.wait_ge(m_mx, b + 1)
                    pe.sem_inc(s.passed, 1)
                    for j in range(CH):
                        last = pe.transpose(pM[:, j * GROUP:(j + 1) * GROUP], mx[:, j * P:(j + 1) * P],
                                            s.ident[0:GROUP, 0:GROUP])
                    last.then_inc(m_mxe, 1)
                    pe.wait_ge(m_W, b + 1)
                    if before(i, u):
                        pe.wait_ge(m_tmp, b)
                    for n in range(GROUP):
                        for j in range(CH):
                            last = pe.matmul(pA[:, n, 0:HCOLS], W[:, n, j, :], R[:, u, n, j, :],
                                             start=j == 0, stop=j == CH - 1)
                    last.then_inc(m_agg, 1)

                pairs(pe, GROUPS, group)

            @block.scalar
            def _(act):
                def group(i, u):
                    b = 2 * i + u
                    act.wait_ge(m_dd, b + 1)
                    act.activation(w[:, :], dd[:, :], ACT.Exp).then_inc(m_w, 1)
                    act.wait_ge(m_dab, b + 1)
                    act.activation(ab[:, :, :], dab[:, :, :], ACT.Exp).then_inc(m_ab, 1)
                    act.wait_ge(m_ab, b + 1)
                    if before(i, u):
                        act.wait_ge(m_done, b)
                    for n in range(GROUP):
                        last = act.activation(tmp[:, n, :], pA[:, n, 0:HCOLS], ACT.Copy, scale=ab[:, 1, n:n + 1])
                    last.then_inc(m_tmp, 1)

                pairs(act, GROUPS, group)

            @block.vector
            def _(v):
                v.memset(run[:, 0:1], -BIG)
                v.memset(R[:, :, :, :, ONECOL], 1.0).then_inc(m_one, 1)

                def group(i, u):
                    b = 2 * i + u
                    link = linker(v, m_v, b * LINKS)
                    v.wait_ge(m_row[u], 32 * (i + 1))
                    v.tensor_scalar(OHT[:, u, :, :], drow[:, u, :, :], s.part[:, 0:1], None,
                                    ALU.is_equal).then_inc(m_oht, 1)
                    link(v.tensor_copy(dcol[:, :], s.dst_t[:, ds(b * GROUP, GROUP), :]))
                    v.wait_ge(m_q, b + 1)
                    if before(i, u):
                        v.wait_ge(m_mxe, b)
                    link(v.tensor_tensor_scan(fwd[:, :], seg[:, u, 0:EROW], pQ[0:GROUP, 0:EROW], -BIG,
                                              ALU.add, ALU.max))
                    link(v.tensor_tensor_scan(bwd[:, ::-1], seg[:, u, 1:EROW + 1][:, ::-1],
                                              pQ[0:GROUP, 0:EROW][:, ::-1], -BIG, ALU.add, ALU.max))
                    v.tensor_tensor(mx[:, :], fwd[:, :], bwd[:, :], ALU.max).then_inc(m_mx, 1)
                    v.wait_ge(m_k, b + 1)
                    link(v.tensor_copy(kS[:, :, :], pK[:, 0:COLS].rearrange("p (n j) -> p n j", j=CH)))
                    v.wait_ge(m_mxe, b + 1)
                    link(v.tensor_tensor(z[:, 0, :, :], R[:, u, :, :, QCOL], kS[:, :, :], ALU.add))
                    link(v.tensor_tensor(z[:, 1, :, :], pM[:, 0:COLS].rearrange("p (j n) -> p n j", j=CH), kS[:, :, :],
                                         ALU.add))
                    link(v.scalar_tensor_tensor(c[:, :, :, :], z[:, :, :, :], 0.2, z[:, :, :, :], ALU.mult, ALU.max))
                    if before(i, u):
                        v.wait_ge(m_w, b)
                    v.tensor_tensor(dd[:, :], c[:, 0, :, :], c[:, 1, :, :], ALU.subtract).then_inc(m_dd, 1)
                    link(v.tensor_copy(R[:, u, :, :, SCOL], c[:, 1, :, :]))
                    v.wait_ge(m_w, b + 1)
                    if before(i, u):
                        v.wait_ge(m_agg, b)
                    for n in range(COLS):
                        last = v.tensor_scalar(W[:, n // CH, n % CH, :], s.iota[:, 0:P], dcol[:, n:n + 1],
                                               w[:, n:n + 1], ALU.is_equal, ALU.mult)
                    last.then_inc(m_W, 1)
                    v.wait_ge(m_agg, b + 1)
                    link(v.tensor_copy(ls[:, :, :], pA[:, :, ONECOL:SCOL + 1].rearrange("p n a -> p a n")))
                    link(v.tensor_scalar(rl[:, :], ls[:, 0, :], 1e-30, None, ALU.max))
                    link(v.reciprocal(rl[:, :], rl[:, :]))
                    link(v.tensor_scalar(none[:, :], ls[:, 0, :], 0.5, -BIG, ALU.is_lt, ALU.mult))
                    link(v.tensor_tensor(sn[:, :], ls[:, 1, :], rl[:, :], ALU.mult))
                    link(v.tensor_tensor(sn[:, :], sn[:, :], none[:, :], ALU.add))
                    link(v.tensor_tensor_scan(run[:, 1:GROUP + 1], s.fresh[:, ds(b * GROUP, GROUP)], sn[:, :],
                                              run[:, 0:1], ALU.add, ALU.max))
                    link(v.tensor_tensor(old[:, :], run[:, 0:GROUP], s.fresh[:, ds(b * GROUP, GROUP)], ALU.add))
                    v.tensor_tensor(dab[:, 0, :], old[:, :], run[:, 1:GROUP + 1], ALU.subtract)
                    v.tensor_tensor(dab[:, 1, :], sn[:, :], run[:, 1:GROUP + 1], ALU.subtract).then_inc(m_dab, 1)
                    link(v.tensor_copy(run[:, 0:1], run[:, GROUP:GROUP + 1]))
                    v.wait_ge(m_tmp, b + 1)
                    for n in range(GROUP):
                        tile = v.value_load(s.tile_i[0:1, ds(b * GROUP + n, 1)], min_val=0, max_val=TILES - 1)
                        a = s.acc[:, ds(tile, 1), :]
                        link(v.scalar_tensor_tensor(a, a, ab[:, 0, n:n + 1], tmp[:, n:n + 1, :], ALU.mult, ALU.add))
                    v.sem_inc(m_done, 1)
                    assert link.count[0] == LINKS, link.count

                pairs(v, GROUPS, group)


def finish0(nc, s, x):
    with ExitStack() as ctx:
        def sb(name, shape, dt=F32):
            return ctx.enter_context(nc.sbuf_tensor(name, shape, dt))

        xin = sb("f_xin", [P, 2, D])
        x1 = sb("f_x1", [P, 2, 2, D])
        den = sb("f_den", [P, 2])
        rd = sb("f_rd", [P, 2])
        st = sb("f_st", [P, 2, 6])
        mv = sb("f_mv", [P, 2, 2])
        ve = sb("f_ve", [P, 2])
        rs = sb("f_rs", [P, 2])
        m_x = [s.sem(f"f_x{u}") for u in (0, 1)]
        m_st = [s.sem(f"f_st{u}") for u in (0, 1)]
        m_v, m_x1, m_var, m_rs, m_xn = (s.sem("f_" + n) for n in ("v", "res", "var", "rs", "xn"))
        LINKS1, LINKS2 = 4, 2

        with nc.Block() as block:
            @block.sync
            def _(sp):
                def load(i, u):
                    if not first(i):
                        sp.wait_ge(m_x1, 2 * i + u - 1)
                    sp.dma_start(xin[:, u, :], x[ds((2 * i + u) * P, P), :]).then_inc(m_x[u], 16)

                pairs(sp, TILES, load)

            @block.scalar
            def _(act):
                def store(i, u):
                    act.wait_ge(m_xn, 2 * i + u + 1)
                    act.dma_start(s.x1_d[ds((2 * i + u) * P, P), :], x1[:, u, :, :]).then_inc(m_st[u], 16)

                pairs(act, TILES, store)
                for u in (0, 1):
                    act.wait_ge(m_st[u], 16 * (TILES // 2))

            @block.gpsimd
            def _(g):
                def root(i, u):
                    g.wait_ge(m_var, 2 * i + u + 1)
                    g.tensor_tensor(rs[:, u:u + 1], ve[:, u:u + 1], s.half[:, :], ALU.pow).then_inc(m_rs, 1)

                pairs(g, TILES, root)

            @block.vector
            def _(v):
                v.memset(s.xsum[:, :], 0.0)

                def residual(i, u, base):
                    t = 2 * i + u
                    link = linker(v, m_v, base)
                    link(v.tensor_scalar(den[:, u:u + 1], s.acc[:, ds(t, 1), ONECOL], 1e-30, None, ALU.max))
                    link(v.reciprocal(rd[:, u:u + 1], den[:, u:u + 1]))
                    v.wait_ge(m_x[u], 16 * (i + 1))
                    if not first(i):
                        v.wait_ge(m_st[u], 16 * i)
                    v.scalar_tensor_tensor(x1[:, u, 0:1, :], s.acc[:, ds(t, 1), 0:D], rd[:, u:u + 1],
                                           xin[:, u:u + 1, :], ALU.mult, ALU.add).then_inc(m_x1, 1)
                    v.wait_ge(m_x1, t + 1)
                    norm_stats(v, link, s.passed, x1[:, u, 0, :], st[:, u, :], mv[:, u, :])
                    v.tensor_scalar(ve[:, u:u + 1], mv[:, u, 1:2], EPS, None, ALU.add).then_inc(m_var, 1)
                    assert link.count[0] == LINKS1

                def normalise(i, u, base):
                    t = 2 * i + u
                    link = linker(v, m_v, base)
                    v.wait_ge(m_rs, t + 1)
                    link(v.tensor_scalar(x1[:, u, 1, :], x1[:, u, 0, :], mv[:, u, 0:1], rs[:, u:u + 1],
                                         ALU.subtract, ALU.mult))
                    v.sem_inc(m_xn, 1)
                    link(v.tensor_tensor(s.xsum[:, :], s.xsum[:, :], x1[:, u, 1, :], ALU.add))
                    assert link.count[0] == LINKS2

                def step(i, u):
                    t = 2 * i + u
                    residual(i, u, t * LINKS1 + ((t - 1) * LINKS2 if before(i, u) else 0))
                    if before(i, u):
                        normalise(*before(i, u), (t + 1) * LINKS1 + (t - 1) * LINKS2)

                pairs(v, TILES, step)
                normalise(TILES // 2 - 1, 1, TILES * LINKS1 + (TILES - 1) * LINKS2)


def route0(nc, s, a):
    with ExitStack() as ctx:
        def sb(name, shape, dt=F32):
            return ctx.enter_context(nc.sbuf_tensor(name, shape, dt))

        wr = sb("r_wr", [P, KD, EXPERTS])
        br = sb("r_br", [1, EXPERTS])
        mean = sb("r_mean", [P, KD])
        row = sb("r_row", [1, EXPERTS])
        ex = sb("r_ex", [1, EXPERTS])
        sc = sb("r_sc", [1, EXPERTS])
        eq = sb("r_eq", [1, EXPERTS])
        one = sb("r_one", [1, 8])
        top = sb("r_top", [1, 2])
        tex = sb("r_tex", [1, 2])
        wtop = sb("r_wtop", [1, 2])
        pm = ctx.enter_context(nc.psum_tensor("r_pm", [P, KD], F32))
        pl = ctx.enter_context(nc.psum_tensor("r_pl", [1, EXPERTS], F32))
        pw = ctx.enter_context(nc.psum_tensor("r_pw", [P, 2], F32))
        m_w, m_pe, m_v, m_a, m_go, m_mean, m_top = (s.sem("r_" + n) for n in
                                                    ("w", "pe", "v", "a", "go", "mean", "wtop"))

        with nc.Block() as block:
            @block.sync
            def _(sp):
                sp.dma_start(wr[:, :, :], a["L0_ffn_Wr"].rearrange("(k p) e -> p k e", p=P)).then_inc(m_w, 16)
                sp.dma_start(br[:, :], a["L0_ffn_br"].partition_broadcast(1)).then_inc(m_w, 16)

            @block.tensor
            def _(pe):
                for k in range(KD):
                    last = pe.matmul(pm[:, k:k + 1], s.xsum[:, k * P:(k + 1) * P], s.ones[:, 0:1], start=True, stop=True)
                last.then_inc(m_pe, 1)
                pe.wait_ge(m_w, 32)
                pe.wait_ge(m_mean, 1)
                for k in range(KD):
                    last = pe.matmul(pl[:, :], mean[:, k:k + 1], wr[:, k, :], start=k == 0, stop=k == KD - 1)
                last.then_inc(m_pe, 1)
                pe.wait_ge(m_top, 1)
                pe.matmul(pw[:, :], s.ones[0:1, :], wtop[:, :], start=True, stop=True).then_inc(m_pe, 1)

            @block.scalar
            def _(act):
                for n, (dst, src) in enumerate(((ex, row), (ex, row), (tex, top))):
                    act.wait_ge(m_go, n + 1)
                    act.activation(dst[:, :], src[:, :], ACT.Exp).then_inc(m_a, 1)

            @block.vector
            def _(v):
                link = linker(v, m_v, 0)
                exps = [0]

                def softmax(row_, ex_, out_):
                    link(v.tensor_reduce(one[:, 0:1], row_, X, ALU.max))
                    v.tensor_scalar(row_, row_, one[:, 0:1], None, ALU.subtract).then_inc(m_go, 1)
                    exps[0] += 1
                    v.wait_ge(m_a, exps[0])
                    link(v.tensor_reduce(one[:, 1:2], ex_, X, ALU.add))
                    link(v.reciprocal(one[:, 2:3], one[:, 1:2]))
                    return v.tensor_scalar(out_, ex_, one[:, 2:3], None, ALU.mult)

                v.wait_ge(m_pe, 1)
                v.tensor_scalar(mean[:, :], pm[:, :], 1.0 / N, None, ALU.mult).then_inc(m_mean, 1)
                v.wait_ge(m_pe, 2)
                link(v.tensor_tensor(row[:, :], pl[:, :], br[:, :], ALU.add))
                link(softmax(row[:, :], ex[:, :], row[:, :]))
                link(v.tensor_scalar(sc[:, :], row[:, :], float(N), None, ALU.mult))
                link(v.tensor_scalar(sc[:, :], sc[:, :], CAPACITY, None, ALU.max))
                link(v.reciprocal(sc[:, :], sc[:, :]))
                link(v.tensor_scalar(sc[:, :], sc[:, :], CAPACITY, None, ALU.mult))
                link(v.tensor_tensor(row[:, :], row[:, :], sc[:, :], ALU.mult))
                link(softmax(row[:, :], ex[:, :], row[:, :]))
                for j in range(2):
                    link(v.tensor_reduce(top[:, j:j + 1], row[:, :], X, ALU.max))
                    link(v.tensor_scalar(eq[:, :], row[:, :], top[:, j:j + 1], None, ALU.is_equal))
                    link(v.tensor_scalar(sc[:, :], s.iota[0:1, 0:EXPERTS], float(-EXPERTS), None, ALU.add))
                    link(v.tensor_tensor(sc[:, :], sc[:, :], eq[:, :], ALU.mult))
                    link(v.tensor_reduce(one[:, 3:4], sc[:, :], X, ALU.min))
                    link(v.tensor_scalar(one[:, 4:5], one[:, 3:4], float(EXPERTS), None, ALU.add))
                    link(v.tensor_copy(s.expert_i[:, j:j + 1], one[:, 4:5]))
                    link(v.tensor_scalar(eq[:, :], s.iota[0:1, 0:EXPERTS], one[:, 4:5], -2.0, ALU.is_equal, ALU.mult))
                    link(v.tensor_tensor(row[:, :], row[:, :], eq[:, :], ALU.add))
                softmax(top[:, :], tex[:, :], wtop[:, :]).then_inc(m_top, 1)
                v.wait_ge(m_pe, 3)
                v.tensor_copy(s.wexp[:, :], pw[:, :])


def feed_forward(nc, s, name, func, table, load_weights, prepare, finish, roots, store):
    with ExitStack() as ctx:
        def sb(n, shape, dt=F32):
            return ctx.enter_context(nc.sbuf_tensor(name + n, shape, dt))

        def ps(n, shape):
            return ctx.enter_context(nc.psum_tensor(name + n, shape, F32))

        f = Shared()
        f.w1 = sb("w1", [P, KD, HID])
        f.b1 = sb("b1", [P, HB])
        f.w2 = sb("w2", [P, HB, D])
        f.vec = sb("vec", [P, 4, D])
        f.xrow = sb("xrow", [P, 2, 2, D])
        f.o = sb("o", [P, 2, D])
        f.t1 = sb("t1", [P, 2, D])
        f.st, f.mv, f.ve, f.rs = sb("st", [P, 2, 6]), sb("mv", [P, 2, 2]), sb("ve", [P, 2]), sb("rs", [P, 2])
        xT = sb("xT", [P, 2, KD, P])
        h = sb("h", [P, HB, P])
        pT = ps("pT", [P, KD, P])
        pH = [ps(f"pH{n}", [P, 2, P]) for n in range(HB // 2)]
        f.pY = [ps(f"pY{n}", [P, D]) for n in (0, 1)]
        f.m_w, f.m_v, m_T, m_xT, m_h, m_g, f.m_y, f.m_o, m_set, f.m_var, f.m_rs, f.m_yr = (
            s.sem(name + n) for n in ("w", "v", "T", "xT", "h", "g", "y", "o", "set", "var", "rs", "yread"))
        m_row = [s.sem(f"{name}row{u}") for u in (0, 1)]
        f.m_st = [s.sem(f"{name}st{u}") for u in (0, 1)]

        with nc.Block() as block:
            @block.sync
            def _(sp):
                load_weights(sp, f)

                def rows(i, u):
                    if not first(i):
                        sp.wait_ge(f.m_o, 2 * i + u - 1)
                    sp.dma_start(f.xrow[:, u, :, :], table[ds((2 * i + u) * P, P), :]).then_inc(m_row[u], 16)

                pairs(sp, TILES, rows)

            if roots:
                @block.gpsimd
                def _(g):
                    def root(i, u):
                        g.wait_ge(f.m_var, 2 * i + u + 1)
                        g.tensor_tensor(f.rs[:, u:u + 1], f.ve[:, u:u + 1], s.half[:, :], ALU.pow).then_inc(f.m_rs, 1)

                    pairs(g, TILES, root)

            @block.tensor
            def _(pe):
                def transposes(i, u):
                    pe.wait_ge(m_row[u], 16 * (i + 1))
                    if before(i, u):
                        pe.wait_ge(m_xT, 2 * i + u)
                    for k in range(KD):
                        last = pe.transpose(pT[:, k, :], f.xrow[:, u, 1, k * P:(k + 1) * P], s.ident[:, :])
                    last.then_inc(m_T, 1)

                def hidden(i, u):
                    pe.wait_ge(m_xT, 2 * i + u + 1)
                    for n in range(HB):
                        for k in range(KD):
                            last = pe.matmul(pH[n // 2][:, n % 2, :], f.w1[:, k, n * P:(n + 1) * P], xT[:, u, k, :],
                                             start=k == 0, stop=k == KD - 1)
                        if n % 2:
                            last.then_inc(m_h, 1)

                def output(i, u):
                    if not first(i):
                        pe.wait_ge(f.m_yr, 2 * i + u - 1)
                    for n in range(HB):
                        pe.wait_ge(m_g, (2 * i + u) * HB + n + 1)
                        last = pe.matmul(f.pY[u][:, :], h[:, n, :], f.w2[:, n, :], start=n == 0, stop=n == HB - 1)
                    last.then_inc(f.m_y, 1)

                def step(i, u):
                    if before(i, u):
                        hidden(*before(i, u))
                    transposes(i, u)
                    if before(i, u):
                        output(*before(i, u))

                pe.wait_ge(m_set, 1)
                pairs(pe, TILES, step)
                hidden(TILES // 2 - 1, 1)
                output(TILES // 2 - 1, 1)

            @block.scalar
            def _(act):
                def turned(i, u):
                    act.wait_ge(m_T, 2 * i + u + 1)
                    if not first(i):
                        act.wait_ge(m_h, (2 * i + u - 1) * (HB // 2))
                    act.copy(xT[:, u, :, :], pT[:, :, :]).then_inc(m_xT, 1)

                def hidden(i, u):
                    t = 2 * i + u
                    for n in range(HB):
                        if n % 2 == 0:
                            act.wait_ge(m_h, t * (HB // 2) + n // 2 + 1)
                        if n == 0 and before(i, u):
                            act.wait_ge(f.m_y, t)
                        act.activation(h[:, n, :], pH[n // 2][:, n % 2, :], func, bias=f.b1[:, n:n + 1]).then_inc(m_g, 1)

                def step(i, u):
                    if before(i, u):
                        hidden(*before(i, u))
                    turned(i, u)
                    if before(i, u) and before(*before(i, u)):
                        store(act, f, *before(*before(i, u)), False)

                act.wait_ge(m_set, 1)
                pairs(act, TILES, step)
                hidden(TILES // 2 - 1, 1)
                store(act, f, TILES // 2 - 1, 0, False)
                store(act, f, TILES // 2 - 1, 1, True)
                for u in (0, 1):
                    act.wait_ge(f.m_st[u], 16 * (TILES // 2))

            @block.vector
            def _(v):
                base = prepare(v, f)
                v.sem_inc(m_set, 1)
                pairs(v, TILES, lambda i, u: finish(v, f, i, u, base))


def feed_forward0(nc, s, a):
    EH = HID // 2

    def load(sp, f):
        experts = [sp.value_load(s.expert_i[0:1, j:j + 1], min_val=0, max_val=EXPERTS - 1) for j in (0, 1)]
        with nc.allow_non_contiguous_dma(reason="biases, one to a partition"):
            for j, e in enumerate(experts):
                sp.dma_start(f.w1[:, :, j * EH:(j + 1) * EH],
                             a["L0_ffn_W1"][ds(e, 1), :, :].rearrange("o (k p) f -> p (o k) f", p=P)).then_inc(f.m_w, 16)
                sp.dma_start(f.w2[:, j * HB // 2:(j + 1) * HB // 2, :],
                             a["L0_ffn_W2"][ds(e, 1), :, :].rearrange("o (n p) d -> p (o n) d", p=P)).then_inc(f.m_w, 16)
                sp.dma_start(f.b1[:, j * HB // 2:(j + 1) * HB // 2],
                             a["L0_ffn_b1"][ds(e, 1), :].rearrange("o (n p) -> p (o n)", p=P)).then_inc(f.m_w, 16)
                sp.dma_start(f.vec[:, j, :], a["L0_ffn_b2"][ds(e, 1), :].partition_broadcast(P)).then_inc(f.m_w, 16)
        for j, n in enumerate(("L0_ffn_gamma", "L0_ffn_beta")):
            sp.dma_start(f.vec[:, 2 + j, :], a[n].partition_broadcast(P)).then_inc(f.m_w, 16)

    def prepare(v, f):
        link = linker(v, f.m_v, 0)
        v.wait_ge(f.m_w, 16 * 10)
        for j in (0, 1):
            w2 = f.w2[:, j * HB // 2:(j + 1) * HB // 2, :]
            link(v.tensor_scalar(w2, w2, s.wexp[:, j:j + 1], None, ALU.mult))
            link(v.tensor_scalar(f.vec[:, j, :], f.vec[:, j, :], s.wexp[:, j:j + 1], None, ALU.mult))
        link(v.tensor_tensor(f.vec[:, 0, :], f.vec[:, 0, :], f.vec[:, 1, :], ALU.add))
        return link.count[0]

    LINKS = 7

    def finish(v, f, i, u, base):
        t = 2 * i + u
        link = linker(v, f.m_v, base + t * LINKS)
        t1 = f.t1[:, u, :]
        v.wait_ge(f.m_y, t + 1)
        v.tensor_tensor(t1, f.pY[u][:, :], f.vec[:, 0, :], ALU.add).then_inc(f.m_yr, 1)
        v.wait_ge(f.m_yr, t + 1)
        link(v.tensor_tensor(t1, t1, f.xrow[:, u, 1, :], ALU.add))
        norm_stats(v, link, s.passed, t1, f.st[:, u, :], f.mv[:, u, :])
        v.tensor_scalar(f.ve[:, u:u + 1], f.mv[:, u, 1:2], EPS, None, ALU.add).then_inc(f.m_var, 1)
        v.wait_ge(f.m_rs, t + 1)
        link(v.tensor_scalar(t1, t1, f.mv[:, u, 0:1], f.rs[:, u:u + 1], ALU.subtract, ALU.mult))
        link(v.tensor_tensor(t1, t1, f.vec[:, 2, :], ALU.mult))
        link(v.tensor_tensor(t1, t1, f.vec[:, 3, :], ALU.add))
        if not first(i):
            v.wait_ge(f.m_st[u], 16 * i)
        link(v.tensor_tensor(f.o[:, u, :], t1, f.xrow[:, u, 0, :], ALU.add))
        v.sem_inc(f.m_o, 1)
        assert link.count[0] == LINKS, link.count

    def store(act, f, i, u, last):
        act.wait_ge(f.m_o, 2 * i + u + 1)
        act.dma_start(s.x2_d[ds((2 * i + u) * P, P), :], f.o[:, u, :]).then_inc(f.m_st[u], 16)

    feed_forward(nc, s, "g", ACT.Gelu, s.x1_d, load, prepare, finish, True, store)


def feed_forward1(nc, s, a, out):
    def load(sp, f):
        sp.dma_start(f.w1[:, :, :], a["L1_ffn_w1"].rearrange("(k p) f -> p k f", p=P)).then_inc(f.m_w, 16)
        sp.dma_start(f.w2[:, :, :], a["L1_ffn_w2"].rearrange("(n p) d -> p n d", p=P)).then_inc(f.m_w, 16)
        with nc.allow_non_contiguous_dma(reason="biases, one to a partition"):
            sp.dma_start(f.b1[:, :], a["L1_ffn_b1"].rearrange("(n p) -> p n", p=P)).then_inc(f.m_w, 16)
        sp.dma_start(f.vec[:, 0, :], a["L1_ffn_b2"].partition_broadcast(P)).then_inc(f.m_w, 16)

    def prepare(v, f):
        v.wait_ge(f.m_w, 16 * 4)
        return 0

    LINKS = 2

    def finish(v, f, i, u, base):
        t = 2 * i + u
        link = linker(v, f.m_v, base + t * LINKS)
        v.wait_ge(f.m_y, t + 1)
        v.tensor_tensor(f.t1[:, u, :], f.pY[u][:, :], f.vec[:, 0, :], ALU.add).then_inc(f.m_yr, 1)
        v.wait_ge(f.m_yr, t + 1)
        link(v.scalar_tensor_tensor(f.t1[:, u, :], f.t1[:, u, :], s.wcol[:, ds(t, 1)], f.xrow[:, u, 1, :],
                                    ALU.mult, ALU.add))
        if not first(i):
            v.wait_ge(f.m_st[u], 16 * i)
        link(v.tensor_tensor(f.o[:, u, :], f.t1[:, u, :], f.xrow[:, u, 0, :], ALU.add))
        v.sem_inc(f.m_o, 1)
        assert link.count[0] == LINKS

    def store(act, f, i, u, last):
        act.wait_ge(f.m_o, 2 * i + u + 1)
        rows = LAST if last else P
        act.dma_start(out[ds((2 * i + u) * P, rows), :], f.o[0:rows, u, :]).then_inc(f.m_st[u], 16)

    feed_forward(nc, s, "j", ACT.Gelu_apprx_tanh, s.x3_d, load, prepare, finish, False, store)


def project1(nc, s, a):
    with ExitStack() as ctx:
        def sb(name, shape, dt=F32):
            return ctx.enter_context(nc.sbuf_tensor(name, shape, dt))

        w = sb("p_w", [P, KD, 3 * D])
        bias = sb("p_bias", [P, 3 * D])
        xin = sb("p_xin", [P, 2, D])
        st, mv, ve, rs = sb("p_st", [P, 2, 6]), sb("p_mv", [P, 2, 2]), sb("p_ve", [P, 2]), sb("p_rs", [P, 2])
        xn = sb("p_xn", [P, 2, D])
        xT = sb("p_xT", [P, 2, KD, P])
        qvk = sb("p_qvk", [P, 2, 3 * D])
        pT = [ctx.enter_context(nc.psum_tensor(f"p_pT{u}", [P, KD, P], F32)) for u in (0, 1)]
        pQV = [ctx.enter_context(nc.psum_tensor(f"p_pQV{u}", [P, 2 * D], F32)) for u in (0, 1)]
        pKK = [ctx.enter_context(nc.psum_tensor(f"p_pKK{u}", [P, D], F32)) for u in (0, 1)]
        m_w = s.sem("p_w")
        m_x = [s.sem(f"p_x{u}") for u in (0, 1)]
        m_v, m_var, m_rs, m_xn, m_T, m_xT, m_h, m_o = (s.sem("p_" + n) for n in
                                                        ("v", "var", "rs", "xn", "T", "xT", "h", "o"))
        m_st = [s.sem(f"p_st{u}") for u in (0, 1)]
        LINKS = 2

        with nc.Block() as block:
            @block.sync
            def _(sp):
                for j, n in enumerate(("q", "v", "k")):
                    sp.dma_start(w[:, :, j * D:(j + 1) * D],
                                 a["L1_gnn_W" + n].rearrange("(k p) n -> p k n", p=P)).then_inc(m_w, 16)
                    sp.dma_start(bias[:, j * D:(j + 1) * D], a["L1_gnn_b" + n].partition_broadcast(P)).then_inc(m_w, 16)

                def load(i, u):
                    if not first(i):
                        sp.wait_ge(m_xn, 2 * i + u - 1)
                    sp.dma_start(xin[:, u, :], s.x2_d[ds((2 * i + u) * P, P), :]).then_inc(m_x[u], 16)

                pairs(sp, TILES, load)

            @block.gpsimd
            def _(g):
                def root(i, u):
                    g.wait_ge(m_var, 2 * i + u + 1)
                    g.tensor_tensor(rs[:, u:u + 1], ve[:, u:u + 1], s.half[:, :], ALU.pow).then_inc(m_rs, 1)

                pairs(g, TILES, root)

            @block.tensor
            def _(pe):
                def transposes(i, u):
                    pe.wait_ge(m_xn, 2 * i + u + 1)
                    if not first(i):
                        pe.wait_ge(m_xT, 2 * i + u - 1)
                    for k in range(KD):
                        last = pe.transpose(pT[u][:, k, :], xn[:, u, k * P:(k + 1) * P], s.ident[:, :])
                    last.then_inc(m_T, 1)

                def product(i, u):
                    pe.wait_ge(m_xT, 2 * i + u + 1)
                    if not first(i):
                        pe.wait_ge(m_o, 2 * i + u - 1)
                    for k in range(KD):
                        pe.matmul(pQV[u][:, :], xT[:, u, k, :], w[:, k, 0:2 * D], start=k == 0, stop=k == KD - 1)
                    for k in range(KD):
                        last = pe.matmul(pKK[u][:, :], xT[:, u, k, :], w[:, k, 2 * D:], start=k == 0, stop=k == KD - 1)
                    last.then_inc(m_h, 1)

                def step(i, u):
                    transposes(i, u)
                    if before(i, u):
                        product(*before(i, u))

                pe.wait_ge(m_w, 16 * 6)
                pairs(pe, TILES, step)
                product(TILES // 2 - 1, 1)

            @block.scalar
            def _(act):
                def turned(i, u):
                    act.wait_ge(m_T, 2 * i + u + 1)
                    if not first(i):
                        act.wait_ge(m_h, 2 * i + u - 1)
                    act.copy(xT[:, u, :, :], pT[u][:, :, :]).then_inc(m_xT, 1)

                def store(i, u):
                    act.wait_ge(m_o, 2 * i + u + 1)
                    rows = ds((2 * i + u) * P, P)
                    act.dma_start(s.qv_d[rows, :], qvk[:, u, 0:2 * D]).then_inc(m_st[u], 16)
                    act.dma_start(s.k_d[rows, :], qvk[:, u, 2 * D:]).then_inc(m_st[u], 16)

                def step(i, u):
                    turned(i, u)
                    if before(i, u):
                        store(*before(i, u))

                pairs(act, TILES, step)
                store(TILES // 2 - 1, 1)
                for u in (0, 1):
                    act.wait_ge(m_st[u], 32 * (TILES // 2))

            @block.vector
            def _(v):
                def normalise(i, u):
                    t = 2 * i + u
                    link = linker(v, m_v, t * LINKS)
                    v.wait_ge(m_x[u], 16 * (i + 1))
                    norm_stats(v, link, s.passed, xin[:, u, :], st[:, u, :], mv[:, u, :])
                    v.tensor_scalar(ve[:, u:u + 1], mv[:, u, 1:2], EPS, None, ALU.add).then_inc(m_var, 1)
                    if not first(i):
                        v.wait_ge(m_T, t - 1)
                    v.wait_ge(m_rs, t + 1)
                    v.tensor_scalar(xn[:, u, :], xin[:, u, :], mv[:, u, 0:1], rs[:, u:u + 1], ALU.subtract,
                                    ALU.mult).then_inc(m_xn, 1)

                def finish(i, u):
                    v.wait_ge(m_h, 2 * i + u + 1)
                    if not first(i):
                        v.wait_ge(m_st[u], 32 * i)
                    v.tensor_tensor(qvk[:, u, 0:2 * D], pQV[u][:, :], bias[:, 0:2 * D], ALU.add)
                    v.tensor_tensor(qvk[:, u, 2 * D:], pKK[u][:, :], bias[:, 2 * D:], ALU.add).then_inc(m_o, 1)

                def step(i, u):
                    normalise(i, u)
                    if before(i, u):
                        finish(*before(i, u))

                v.wait_ge(m_w, 16 * 6)
                v.memset(s.acc[:, :, 0:D], 0.0)
                pairs(v, TILES, step)
                finish(TILES // 2 - 1, 1)


def edges1(nc, s):
    with ExitStack() as ctx:
        def sb(name, shape, dt=F32):
            return ctx.enter_context(nc.sbuf_tensor(name, shape, dt))

        R = sb("h_R", [P, 2, GROUP, CH, 2 * D])
        idx = sb("h_idx", [P, 2, COLS], I32)
        drow = sb("h_drow", [P, 2, GROUP, EROW], BF16)
        kt = sb("h_kt", [P, 2, GROUP, D])
        OHT = sb("h_OHT", [P, 2, GROUP, EROW])
        OH = sb("h_OH", [P, GROUP, CH, P])
        dcol = sb("h_dcol", [P, COLS])
        prod = sb("h_prod", [P, CH, D])
        sc = sb("h_sc", [P, COLS, HEADS])
        smax = sb("h_smax", [P, COLS])
        ex = sb("h_ex", [P, COLS, HEADS])
        ssum = sb("h_ssum", [P, COLS])
        at = sb("h_at", [P, COLS, HEADS])
        pK = [ctx.enter_context(nc.psum_tensor(f"h_pK{n}", [P, CH, D], F32)) for n in range(GROUP)]
        pA = ctx.enter_context(nc.psum_tensor("h_pA", [P, GROUP, 512], F32))
        m_idx = s.sem("h_idx")
        m_g = [s.sem(f"h_g{u}") for u in (0, 1)]
        m_row = [s.sem(f"h_row{u}") for u in (0, 1)]
        m_v, m_oht, m_k, m_pr, m_d, m_ex, m_V, m_agg, m_done = (
            s.sem("h_" + n) for n in ("v", "oht", "k", "pr", "d", "ex", "V", "agg", "done"))
        LINKS = 2 * GROUP + 4 + GROUP + 1

        with nc.Block() as block:
            @block.gpsimd
            def _(g):
                def gather(i, u):
                    b = 2 * i + u
                    if not first(i):
                        g.wait_ge(m_agg, b - 1)
                    g.tensor_copy(idx[:, u, :], s.src_t[:, ds(b * GROUP, GROUP), :]).then_inc(m_idx, 1)
                    g.wait_ge(m_idx, b + 1)
                    g.sem_inc(s.passed, 1)
                    for n in range(COLS):
                        g.indirect_dma_start(R[:, u, n // CH, n % CH, :], None, s.qv_d[:, :],
                                             bass.IndirectOffsetOnAxis(ap=idx[:, u, n:n + 1], axis=0)
                                             ).then_inc(m_g[u], 16)

                pairs(g, GROUPS, gather)

            @block.sync
            def _(sp):
                def load(i, u):
                    b = 2 * i + u
                    if not first(i):
                        sp.wait_ge(m_k, (b - 1) * GROUP)
                    sp.dma_start(drow[:, u, :, :], s.drow_d[ds(b * GROUP, GROUP), :].partition_broadcast(P)
                                 ).then_inc(m_row[u], 16)
                    for n in range(GROUP):
                        tile = sp.value_load(s.tile_i[0:1, ds(b * GROUP + n, 1)], min_val=0, max_val=TILES - 1)
                        sp.dma_start(kt[:, u, n, :], s.k_d[ds(tile * P, P), :]).then_inc(m_row[u], 16)

                pairs(sp, GROUPS, load)

            @block.tensor
            def _(pe):
                def expand(i, u):
                    b = 2 * i + u
                    pe.wait_ge(m_row[u], 16 * (1 + GROUP) * (i + 1))
                    pe.wait_ge(m_oht, b + 1)
                    for n in range(GROUP):
                        if before(i, u):
                            pe.wait_ge(m_pr, (b - 1) * GROUP + n + 1)
                        for j in range(CH):
                            last = pe.matmul(pK[n][:, j, :], OHT[:, u, n, j * P:(j + 1) * P], kt[:, u, n, :],
                                             start=True, stop=True)
                        last.then_inc(m_k, 1)

                def collect(i, u):
                    b = 2 * i + u
                    for n in range(GROUP):
                        pe.wait_ge(m_V, b * GROUP + n + 1)
                        if before(i, u):
                            pe.wait_ge(m_done, b)
                        for j in range(CH):
                            last = pe.matmul(pA[:, n, 0:D], OH[:, n, j, :], R[:, u, n, j, D:], start=j == 0,
                                             stop=j == CH - 1)
                    last.then_inc(m_agg, 1)

                def step(i, u):
                    expand(i, u)
                    if before(i, u):
                        collect(*before(i, u))

                pairs(pe, GROUPS, step)
                collect(GROUPS // 2 - 1, 1)

            @block.scalar
            def _(act):
                def group(i, u):
                    b = 2 * i + u
                    act.wait_ge(m_d, b + 1)
                    act.activation(ex[:, :, :], sc[:, :, :], ACT.Exp, scale=float(HD) ** -0.5).then_inc(m_ex, 1)

                pairs(act, GROUPS, group)

            @block.vector
            def _(v):
                def select(i, u):
                    b = 2 * i + u
                    v.wait_ge(m_row[u], 16 * (1 + GROUP) * (i + 1))
                    if not first(i):
                        v.wait_ge(m_k, (b - 1) * GROUP)
                    v.tensor_scalar(OHT[:, u, :, :], drow[:, u, :, :], s.part[:, 0:1], None,
                                    ALU.is_equal).then_inc(m_oht, 1)

                def scores(i, u):
                    b = 2 * i + u
                    link = linker(v, m_v, b * LINKS)
                    link(v.tensor_copy(dcol[:, :], s.dst_t[:, ds(b * GROUP, GROUP), :]))
                    v.wait_ge(m_g[u], 16 * COLS * (i + 1))
                    for n in range(GROUP):
                        v.wait_ge(m_k, b * GROUP + n + 1)
                        link(v.tensor_tensor(prod[:, :, :], pK[n][:, :, :], R[:, u, n, :, 0:D], ALU.mult))
                        v.sem_inc(m_pr, 1)
                        link(v.tensor_reduce(sc[:, n * CH:(n + 1) * CH, :],
                                             prod[:, :, :].rearrange("p c (h d) -> p (c h) d", d=HD), X, ALU.add))
                    link(v.tensor_reduce(smax[:, :], sc[:, :, :], X, ALU.max))
                    v.tensor_tensor(sc[:, :, :], sc[:, :, :], smax[:, :].unsqueeze(2).to_broadcast([P, COLS, HEADS]),
                                    ALU.subtract).then_inc(m_d, 1)
                    for n in range(COLS):
                        if n == 0 and before(i, u):
                            v.wait_ge(m_agg, b)
                        v.tensor_scalar(OH[:, n // CH, n % CH, :], s.iota[:, 0:P], dcol[:, n:n + 1], None, ALU.is_equal)
                    v.wait_ge(m_ex, b + 1)
                    link(v.tensor_reduce(ssum[:, :], ex[:, :, :], X, ALU.add))
                    link(v.reciprocal(ssum[:, :], ssum[:, :]))
                    link(v.tensor_tensor(at[:, :, :], ex[:, :, :], ssum[:, :].unsqueeze(2).to_broadcast([P, COLS, HEADS]),
                                         ALU.mult))
                    for n in range(GROUP):
                        rv = R[:, u, n, :, D:].rearrange("p c (h d) -> p c h d", d=HD)
                        v.tensor_tensor(rv, rv, at[:, n * CH:(n + 1) * CH, :].unsqueeze(3)
                                        .to_broadcast([P, CH, HEADS, HD]), ALU.mult).then_inc(m_V, 1)
                    v.wait_ge(m_agg, b + 1)
                    for n in range(GROUP):
                        tile = v.value_load(s.tile_i[0:1, ds(b * GROUP + n, 1)], min_val=0, max_val=TILES - 1)
                        acc = s.acc[:, ds(tile, 1), 0:D]
                        link(v.tensor_tensor(acc, acc, pA[:, n:n + 1, 0:D], ALU.add))
                    v.sem_inc(m_done, 1)
                    assert link.count[0] == LINKS, link.count

                select(0, 0)
                select(0, 1)
                scores(0, 0)
                select(1, 0)
                scores(0, 1)
                with v.Fori(1, GROUPS // 2 - 1) as i:
                    select(i, 1)
                    scores(i, 0)
                    select(i + 1, 0)
                    scores(i, 1)
                select(GROUPS // 2 - 1, 1)
                scores(GROUPS // 2 - 1, 0)
                scores(GROUPS // 2 - 1, 1)


def finish1(nc, s, a):
    with ExitStack() as ctx:
        def sb(name, shape, dt=F32):
            return ctx.enter_context(nc.sbuf_tensor(name, shape, dt))

        w = sb("o_w", [P, KD, D])
        rows = sb("o_rows", [P, 2, D])
        br = sb("o_br", [P, 1])
        g = sb("o_g", [P, 2, D])
        gT = sb("o_gT", [P, 2, KD, P])
        xin = sb("o_xin", [P, 2, D])
        o = sb("o_o", [P, 2, 2, D])
        junk = sb("o_junk", [P, D])
        dot = sb("o_dot", [P, 2])
        st, mv, ve, rs = sb("o_st", [P, 2, 6]), sb("o_mv", [P, 2, 2]), sb("o_ve", [P, 2]), sb("o_rs", [P, 2])
        pT = [ctx.enter_context(nc.psum_tensor(f"o_pT{u}", [P, KD, P], F32)) for u in (0, 1)]
        pO = [ctx.enter_context(nc.psum_tensor(f"o_pO{u}", [P, D], F32)) for u in (0, 1)]
        m_w = s.sem("o_w")
        m_x = [s.sem(f"o_x{u}") for u in (0, 1)]
        m_st = [s.sem(f"o_st{u}") for u in (0, 1)]
        m_v, m_g, m_T, m_gT, m_p, m_pr, m_var, m_rs, m_o = (
            s.sem("o_" + n) for n in ("v", "g", "T", "gT", "p", "pr", "var", "rs", "out"))
        LINKS = 5

        with nc.Block() as block:
            @block.sync
            def _(sp):
                sp.dma_start(w[:, :, :], a["L1_gnn_Wo"].rearrange("(k p) n -> p k n", p=P)).then_inc(m_w, 16)
                sp.dma_start(rows[:, 0, :], a["L1_gnn_bo"].partition_broadcast(P)).then_inc(m_w, 16)
                sp.dma_start(rows[:, 1, :], a["L1_ffn_wr"].rearrange("d o -> (d o)").partition_broadcast(P)).then_inc(m_w, 16)
                sp.dma_start(br[:, :], a["L1_ffn_br"].partition_broadcast(P)).then_inc(m_w, 16)

                def load(i, u):
                    if not first(i):
                        sp.wait_ge(m_var, 2 * i + u - 1)
                    sp.dma_start(xin[:, u, :], s.x2_d[ds((2 * i + u) * P, P), :]).then_inc(m_x[u], 16)

                pairs(sp, TILES, load)

            @block.gpsimd
            def _(gp):
                def root(i, u):
                    gp.wait_ge(m_var, 2 * i + u + 1)
                    gp.tensor_tensor(rs[:, u:u + 1], ve[:, u:u + 1], s.half[:, :], ALU.pow).then_inc(m_rs, 1)

                pairs(gp, TILES, root)

            @block.tensor
            def _(pe):
                def transposes(i, u):
                    pe.wait_ge(m_g, 2 * i + u + 1)
                    if not first(i):
                        pe.wait_ge(m_gT, 2 * i + u - 1)
                    for k in range(KD):
                        last = pe.transpose(pT[u][:, k, :], g[:, u, k * P:(k + 1) * P], s.ident[:, :])
                    last.then_inc(m_T, 1)

                def product(i, u):
                    pe.wait_ge(m_gT, 2 * i + u + 1)
                    if not first(i):
                        pe.wait_ge(m_pr, 2 * i + u - 1)
                    for k in range(KD):
                        last = pe.matmul(pO[u][:, :], gT[:, u, k, :], w[:, k, :], start=k == 0, stop=k == KD - 1)
                    last.then_inc(m_p, 1)

                def step(i, u):
                    transposes(i, u)
                    if before(i, u):
                        product(*before(i, u))

                pe.wait_ge(m_w, 16 * 4)
                pairs(pe, TILES, step)
                product(TILES // 2 - 1, 1)

            @block.scalar
            def _(act):
                def stage(i, u):
                    if not first(i):
                        act.wait_ge(m_T, 2 * i + u - 1)
                    act.copy(g[:, u:u + 1, :], s.acc[:, ds(2 * i + u, 1), 0:D]).then_inc(m_g, 1)

                def turned(i, u):
                    act.wait_ge(m_T, 2 * i + u + 1)
                    if not first(i):
                        act.wait_ge(m_p, 2 * i + u - 1)
                    act.copy(gT[:, u, :, :], pT[u][:, :, :]).then_inc(m_gT, 1)

                def store(i, u):
                    act.wait_ge(m_o, 2 * i + u + 1)
                    act.dma_start(s.x3_d[ds((2 * i + u) * P, P), :], o[:, u, :, :]).then_inc(m_st[u], 16)

                def step(i, u):
                    stage(i, u)
                    turned(i, u)
                    if before(i, u) and before(*before(i, u)):
                        store(*before(*before(i, u)))

                pairs(act, TILES, step)
                store(TILES // 2 - 1, 0)
                store(TILES // 2 - 1, 1)
                for u in (0, 1):
                    act.wait_ge(m_st[u], 16 * (TILES // 2))

            @block.vector
            def _(v):
                v.wait_ge(m_w, 16 * 4)

                def finish(i, u):
                    t = 2 * i + u
                    link = linker(v, m_v, t * LINKS)
                    v.wait_ge(m_p, t + 1)
                    if not first(i):
                        v.wait_ge(m_st[u], 16 * i)
                    v.tensor_tensor(o[:, u, 0, :], pO[u][:, :], rows[:, 0, :], ALU.add).then_inc(m_pr, 1)
                    v.wait_ge(m_pr, t + 1)
                    v.wait_ge(m_x[u], 16 * (i + 1))
                    link(v.tensor_tensor(o[:, u, 0, :], o[:, u, 0, :], xin[:, u, :], ALU.add))
                    norm_stats(v, link, s.passed, o[:, u, 0, :], st[:, u, :], mv[:, u, :])
                    v.tensor_scalar(ve[:, u:u + 1], mv[:, u, 1:2], EPS, None, ALU.add).then_inc(m_var, 1)
                    v.wait_ge(m_rs, t + 1)
                    link(v.tensor_scalar(o[:, u, 1, :], o[:, u, 0, :], mv[:, u, 0:1], rs[:, u:u + 1], ALU.subtract,
                                         ALU.mult))
                    v.sem_inc(m_o, 1)
                    link(v.tensor_tensor_reduce(junk[:, :], o[:, u, 1, :], rows[:, 1, :], 1.0, 0.0, ALU.mult,
                                                ALU.add, dot[:, u:u + 1]))
                    v.tensor_scalar(s.wcol[:, ds(t, 1)], dot[:, u:u + 1], br[:, 0:1], None, ALU.add)
                    assert link.count[0] == LINKS

                pairs(v, TILES, finish)


def select1(nc, s):
    with ExitStack() as ctx:
        def sb(name, shape, dt=F32):
            return ctx.enter_context(nc.sbuf_tensor(name, shape, dt))

        bits = sb("s_bits", [P, TILES], I32)
        hi_i = sb("s_hi_i", [P, TILES], I32)
        lo_i = sb("s_lo_i", [P, TILES], I32)
        hi, lo, neg, tmp = sb("s_hi", [P, TILES]), sb("s_lo", [P, TILES]), sb("s_neg", [P, TILES]), sb("s_tmp", [P, TILES])
        real, chosen = sb("s_real", [P, TILES]), sb("s_chosen", [P, TILES])
        need, low, cand, bit, cnt, got = (sb("s_" + n, [P, 1]) for n in ("need", "low", "cand", "bit", "cnt", "got"))
        pc = ctx.enter_context(nc.psum_tensor("s_pc", [P, 1], F32))
        m_v, m_cnt, m_sum = s.sem("s_v"), s.sem("s_cnt"), s.sem("s_sum")
        BITS = (16, 16, 14)
        sums = sum(BITS) + 2

        with nc.Block() as block:
            @block.tensor
            def _(pe):
                with pe.Fori(0, sums) as i:
                    pe.wait_ge(m_cnt, i + 1)
                    pe.matmul(pc[:, :], s.ones[:, :], cnt[:, :], start=True, stop=True).then_inc(m_sum, 1)

            @block.vector
            def _(v):
                link = linker(v, m_v, 0)
                link(v.tensor_copy(bits[:, :], s.wcol[:, :].bitcast(I32)))
                link(v.tensor_scalar(hi_i[:, :], bits[:, :], 16, 0xFFFF, ALU.logical_shift_right, ALU.bitwise_and))
                link(v.tensor_scalar(lo_i[:, :], bits[:, :], 0xFFFF, None, ALU.bitwise_and))
                link(v.tensor_copy(hi[:, :], hi_i[:, :]))
                link(v.tensor_copy(lo[:, :], lo_i[:, :]))
                link(v.tensor_scalar(neg[:, :], hi[:, :], 32768.0, None, ALU.is_ge))
                link(v.tensor_scalar(tmp[:, :], lo[:, :], -2.0, 65535.0, ALU.mult, ALU.add))
                link(v.tensor_tensor(tmp[:, :], tmp[:, :], neg[:, :], ALU.mult))
                link(v.tensor_tensor(lo[:, :], lo[:, :], tmp[:, :], ALU.add))
                link(v.tensor_scalar(tmp[:, :], hi[:, :], -2.0, 32767.0, ALU.mult, ALU.add))
                link(v.tensor_tensor(tmp[:, :], tmp[:, :], neg[:, :], ALU.mult))
                link(v.tensor_scalar(hi[:, :], hi[:, :], 32768.0, None, ALU.add))
                link(v.tensor_tensor(hi[:, :], hi[:, :], tmp[:, :], ALU.add))
                link(v.tensor_scalar(real[:, :], s.node[:, :], float(N), None, ALU.is_lt))

                def masked(digit, mask):
                    link(v.tensor_scalar(digit, digit, 1.0, None, ALU.add))
                    link(v.tensor_tensor(digit, digit, mask, ALU.mult))
                    link(v.tensor_scalar(digit, digit, -1.0, None, ALU.add))

                masked(hi[:, :], real[:, :])
                link(v.memset(need[:, :], float(TOPK)))
                link(v.memset(chosen[:, :], 0.0))
                at, summed = link.count[0], 0

                def search(digit, nbits):
                    v.memset(low[:, :], 0.0).then_inc(m_v, 1)
                    v.memset(bit[:, :], float(2 ** (nbits - 1))).then_inc(m_v, 1)
                    v.wait_ge(m_v, at + 2)
                    with v.Fori(0, nbits) as i:
                        step = linker(v, m_v, i * 5 + (at + 2))
                        step(v.tensor_tensor(cand[:, :], low[:, :], bit[:, :], ALU.add))
                        step(v.tensor_scalar(tmp[:, :], digit, cand[:, 0:1], None, ALU.is_ge))
                        v.tensor_reduce(cnt[:, :], tmp[:, :], X, ALU.add).then_inc(m_cnt, 1)
                        v.wait_ge(m_sum, i + (summed + 1))
                        step(v.tensor_tensor(got[:, :], pc[:, :], need[:, :], ALU.is_ge))
                        step(v.scalar_tensor_tensor(low[:, :], got[:, :], bit[:, 0:1], low[:, :], ALU.mult, ALU.add))
                        step(v.tensor_scalar(bit[:, :], bit[:, :], 0.5, None, ALU.mult))
                    return at + 2 + 5 * nbits, summed + nbits

                def settle(digit, following):
                    step = linker(v, m_v, at)
                    step(v.tensor_scalar(tmp[:, :], digit, low[:, 0:1], None, ALU.is_gt))
                    step(v.tensor_tensor(chosen[:, :], chosen[:, :], tmp[:, :], ALU.add))
                    v.tensor_reduce(cnt[:, :], tmp[:, :], X, ALU.add).then_inc(m_cnt, 1)
                    v.wait_ge(m_sum, summed + 1)
                    step(v.tensor_tensor(need[:, :], need[:, :], pc[:, :], ALU.subtract))
                    step(v.tensor_scalar(tmp[:, :], digit, low[:, 0:1], None, ALU.is_equal))
                    step(v.tensor_scalar(following, following, 1.0, None, ALU.add))
                    step(v.tensor_tensor(following, following, tmp[:, :], ALU.mult))
                    step(v.tensor_scalar(following, following, -1.0, None, ALU.add))
                    return at + step.count[0], summed + 1

                at, summed = search(hi[:, :], BITS[0])
                at, summed = settle(hi[:, :], lo[:, :])
                at, summed = search(lo[:, :], BITS[1])
                v.tensor_scalar(neg[:, :], s.node[:, :], -1.0, float(2 ** BITS[2] - 1), ALU.mult, ALU.add).then_inc(m_v, 1)
                at += 1
                v.wait_ge(m_v, at)
                at, summed = settle(lo[:, :], neg[:, :])
                at, summed = search(neg[:, :], BITS[2])
                step = linker(v, m_v, at)
                step(v.tensor_scalar(tmp[:, :], neg[:, :], low[:, 0:1], None, ALU.is_ge))
                step(v.tensor_tensor(chosen[:, :], chosen[:, :], tmp[:, :], ALU.add))
                step(v.tensor_tensor(s.wcol[:, :], s.wcol[:, :], chosen[:, :], ALU.mult))


def build(nc, x, src2, dst2, a, out):
    with ExitStack() as ctx:
        s = Shared()

        def sb(name, shape, dt=F32):
            return ctx.enter_context(nc.sbuf_tensor(name, shape, dt))

        s.sem = lambda name: ctx.enter_context(nc.semaphore(name))
        s.passed = s.sem("passed")
        s.acc = sb("acc", [P, TILES, HCOLS])
        s.iota_i = sb("iota_i", [P, IPAD], I32)
        s.iota = sb("iota", [P, IPAD])
        s.part_i = sb("part_i", [P, 1], I32)
        s.part = sb("part", [P, 1])
        s.node_i = sb("node_i", [P, TILES], I32)
        s.node = sb("node", [P, TILES])
        s.ones = sb("ones", [P, P])
        s.half = sb("half", [P, 1])
        s.ident = sb("ident", [P, P])
        s.tile_i = sb("tile_i", [1, IPAD], I32)
        s.fresh = sb("fresh", [P, IPAD])
        s.src_t = sb("src_t", [P, IPAD, CH], I32)
        s.dst_t = sb("dst_t", [P, IPAD, CH])
        s.k0 = sb("k0", [P, TILES])
        s.xsum = sb("xsum", [P, D])
        s.expert_i = sb("expert_i", [1, 2], I32)
        s.wexp = sb("wexp", [P, 2])
        s.wcol = sb("wcol", [P, TILES])
        s.drow_d = nc.dram_tensor("drow_d", [IPAD, EROW], BF16).ap()
        s.seg_d = nc.dram_tensor("seg_d", [IPAD, EROW + 1], F32).ap()
        s.hq_d = nc.dram_tensor("hq_d", [NPAD, D + 1], F32).ap()
        s.qv_d = nc.dram_tensor("qv_d", [NPAD, 2 * D], F32).ap()
        s.k_d = nc.dram_tensor("k_d", [NPAD, D], F32).ap()
        s.x1_d = nc.dram_tensor("x1_d", [NPAD, 2 * D], F32).ap()
        s.x2_d = nc.dram_tensor("x2_d", [NPAD, D], F32).ap()
        s.x3_d = nc.dram_tensor("x3_d", [NPAD, 2 * D], F32).ap()
        constants(nc, s)
        item_tables(nc, s, src2, dst2)
        project0(nc, s, x, a["L0_gnn_Wv"], a["L0_gnn_bv"], a["L0_gnn_wq"], a["L0_gnn_bq"], a["L0_gnn_wk"], a["L0_gnn_bk"])
        edges0(nc, s)
        finish0(nc, s, x)
        route0(nc, s, a)
        feed_forward0(nc, s, a)
        project1(nc, s, a)
        edges1(nc, s)
        finish1(nc, s, a)
        select1(nc, s)
        feed_forward1(nc, s, a, out)


_WEIGHTS = ['L0_gnn_Wv', 'L0_gnn_bv', 'L0_gnn_wq', 'L0_gnn_bq', 'L0_gnn_wk', 'L0_gnn_bk', 'L0_ffn_Wr', 'L0_ffn_br',
            'L0_ffn_W1', 'L0_ffn_b1', 'L0_ffn_W2', 'L0_ffn_b2', 'L0_ffn_gamma', 'L0_ffn_beta', 'L1_gnn_Wq', 'L1_gnn_bq',
            'L1_gnn_Wk', 'L1_gnn_bk', 'L1_gnn_Wv', 'L1_gnn_bv', 'L1_gnn_Wo', 'L1_gnn_bo', 'L1_ffn_wr', 'L1_ffn_br',
            'L1_ffn_w1', 'L1_ffn_b1', 'L1_ffn_w2', 'L1_ffn_b2']


def kernel(**inputs):
    import numpy as np
    import concourse.bacc as bacc
    from concourse.bass_utils import run_bass_kernel_spmd

    nc = bacc.Bacc("TRN2", target_bir_lowering=False, num_devices=1)
    arrays, args = {}, {}
    laid = {"x": np.pad(np.asarray(inputs["x"]), ((0, NPAD - N), (0, 0)))}
    laid["src2"] = np.pad(np.asarray(inputs["src"]), (0, EROWS * EROW - EDGES)).reshape(EROWS, EROW)
    laid["dst2"] = np.pad(np.asarray(inputs["dst"]), (0, EROWS * EROW - EDGES),
                          constant_values=2 * NPAD).reshape(EROWS, EROW)
    for name in _WEIGHTS:
        w = np.asarray(inputs[name])
        if name in ("L1_gnn_Wq", "L1_gnn_Wk", "L1_gnn_Wv", "L1_gnn_Wo"):
            w = w.T
        laid[name] = w.reshape(1) if w.ndim == 0 else w
    for name, value in laid.items():
        value = np.ascontiguousarray(value)
        arrays["in_" + name] = value
        args[name] = nc.dram_tensor("in_" + name, value.shape, mybir.dt.from_np(value.dtype), kind="ExternalInput").ap()
    out = nc.dram_tensor("out", (N, D), F32, kind="ExternalOutput").ap()
    build(nc, args.pop("x"), args.pop("src2"), args.pop("dst2"), args, out)
    return run_bass_kernel_spmd(nc, [arrays], core_ids=[0]).results[0]["out"]
```

```python
from contextlib import ExitStack

import concourse.bass as bass
from concourse import mybir

F32 = mybir.dt.float32
BF16 = mybir.dt.bfloat16
I32 = mybir.dt.int32
ALU = mybir.AluOpType
ACT = mybir.ActivationFunctionType
ENGINE = mybir.EngineType
X = mybir.AxisListType.X

P = 128
N = 12500
D = 256
TILES = (N + P - 1) // P
NPAD = TILES * P
LAST = N - (TILES - 1) * P
EDGES = 212500
EROW = 256
EROWS = (EDGES + EROW - 1) // EROW
ITEMS = EROWS + TILES - 1
GROUP = 4
GROUPS = ITEMS // GROUP
IBLOCKS = (ITEMS + P - 1) // P
IPAD = IBLOCKS * P
CH = EROW // P
COLS = GROUP * CH
RING = 4
LAST_TURN = (GROUPS // RING - 1, RING - 1)
KPARTS = 3
HEADS = 8
HD = D // HEADS
EXPERTS = 8
HID = 1024
HB = HID // P
KD = D // P
EPS = 1e-5
BIG = 1e30
TOPK = N // 2 - 1
CAPACITY = float(-(-N * 5 // (4 * EXPERTS)))
QCOL, ONECOL, SCOL, HCOLS = D, D + 1, D + 2, D + 3
ACOLS = D + 1
assert ITEMS % (RING * GROUP) == 0 and TILES % 2 == 0


def ds(start, size):
    return bass.ds(start, size)


def pairs(eng, n, body):
    for u in (0, 1):
        body(0, u)
    with eng.Fori(1, n // 2) as i:
        for u in (0, 1):
            body(i, u)


def turns(eng, n, width, body, peel_last=False, open_round=None):
    def run(i, peeled):
        more = {"opened": open_round(i)} if open_round else {}
        for u in range(width):
            if peeled:
                more["left"] = width - 1 - u
            body(i, u, **more)

    run(0, False)
    with eng.Fori(1, n // width - int(peel_last)) as i:
        run(i, False)
    if peel_last:
        run(n // width - 1, True)


def before(i, u, width=2):
    if u:
        return i, u - 1
    return None if isinstance(i, int) and i == 0 else (i - 1, width - 1)


def after(i, u, width, steps=1):
    return (i, u + steps) if u + steps < width else (i + 1, u + steps - width)


def load_tiles(nc, s, engine, b, groups=1):
    return nc.values_load_multi_w_load_instructions(s.tile_i[0:1, ds(b * GROUP, groups * GROUP)], engines=(engine,),
                                                    min_val=0, max_val=TILES - 1)[1]


def first(i):
    return isinstance(i, int) and i == 0


def linker(eng, sem, base):
    count = [0]

    def link(ins):
        count[0] += 1
        ins.then_inc(sem, 1)
        eng.wait_ge(sem, base + count[0])

    link.count = count
    return link


class Shared:
    pass


def constants(nc, s):
    sem_iota, sem_c = s.sem("c_iota"), s.sem("c_made")
    with nc.Block() as block:
        @block.gpsimd
        def _(g):
            g.iota(s.iota_i[:, :], pattern=[[1, IPAD]], base=0, channel_multiplier=0).then_inc(sem_iota, 1)
            g.iota(s.part_i[:, :], pattern=[[0, 1]], base=0, channel_multiplier=1).then_inc(sem_iota, 1)
            g.iota(s.node_i[:, :], pattern=[[P, TILES]], base=0, channel_multiplier=1).then_inc(sem_iota, 1)

        @block.vector
        def _(v):
            link = linker(v, sem_c, 0)
            v.memset(s.ones[:, :], 1.0)
            v.memset(s.half[:, :], -0.5)
            v.memset(s.acc[:, :, :], 0.0)
            v.wait_ge(sem_iota, 3)
            v.tensor_copy(s.item_no[:, :], s.iota_i[:, :])
            v.tensor_copy(s.iota[:, :], s.iota_i[:, 0:P])
            v.tensor_copy(s.iota_b[:, :], s.iota_i[:, 0:P])
            v.tensor_copy(s.node[:, :], s.node_i[:, :])
            link(v.tensor_copy(s.part[:, :], s.part_i[:, :]))
            link(v.tensor_scalar(s.ident[:, :], s.iota[:, :], s.part[:, 0:1], None, ALU.is_equal))


def item_tables(nc, s, src2, dst2):
    with ExitStack() as ctx:
        def sb(name, shape, dt):
            return ctx.enter_context(nc.sbuf_tensor(name, shape, dt))

        def ps(name, shape, dt=F32):
            return ctx.enter_context(nc.psum_tensor(name, shape, dt))

        first_i = sb("t_first_i", [1, EROWS], I32)
        first_f = sb("t_first_f", [1, EROWS], F32)
        below = sb("t_below", [P, EROWS], F32)
        cnt = sb("t_cnt", [P, 1], F32)
        begins = sb("t_begins", [P, 1], F32)
        bound = sb("t_bound", [P, 1], F32)
        valid = sb("t_valid", [P, P], BF16)
        vcol = sb("t_vcol", [P, 2], F32)
        step = sb("t_step", [P, IPAD], BF16)
        tcol = sb("t_tcol", [P, IBLOCKS], F32)
        tbase = sb("t_tbase", [P, IBLOCKS], F32)
        grow = sb("t_grow", [P, IBLOCKS], F32)
        growi = sb("t_growi", [P, IBLOCKS], I32)
        srcb = sb("t_srcb", [P, 2, EROW], I32)
        dstb = sb("t_dstb", [P, 2, EROW], I32)
        srcf = sb("t_srcf", [P, 2, EROW], F32)
        dloc = sb("t_dloc", [P, 2, EROW], F32)
        dlocb = sb("t_dlocb", [P, 2, EROW], BF16)
        seg = sb("t_seg", [P, 2, EROW + 1], F32)
        trep = sb("t_trep", [P, IPAD], F32)
        bc = [ps(f"t_bc{i}", [P, 512]) for i in range(2)]
        pt = [ps(f"t_pt{i}", [P, 512]) for i in range(2)]
        pc = ps("t_pc", [P, 512])
        px = [ps(f"t_px{i}", [P, 2, CH, P]) for i in range(2)]
        m_first, m_ff, m_bc, m_v = s.sem("t_first"), s.sem("t_ff"), s.sem("t_bc"), s.sem("t_v")
        m_step, m_t, m_idx = s.sem("t_step"), s.sem("t_t"), s.sem("t_idx")
        m_rows = [s.sem(f"t_rows{u}") for u in (0, 1)]
        m_loc, m_x, m_done = s.sem("t_loc"), s.sem("t_x"), s.sem("t_done")
        m_st = [s.sem(f"t_st{u}") for u in (0, 1)]
        half = EROWS // 2

        with nc.Block() as block:
            @block.sync
            def _(sp):
                with nc.allow_non_contiguous_dma(reason="one element of each edge row"):
                    sp.dma_start(first_i[:, :], dst2[:, 0:1].rearrange("r o -> o r")).then_inc(m_first, 16)
                for b in range(IBLOCKS):
                    u = b % 2
                    sp.wait_ge(m_loc, b + 1)
                    sp.dma_start(s.drow_d[b * P:(b + 1) * P, :], dlocb[:, u, :]).then_inc(m_st[u], 16)
                    sp.dma_start(s.seg_d[b * P:(b + 1) * P, :], seg[:, u, :]).then_inc(m_st[u], 16)
                for u in (0, 1):
                    sp.wait_ge(m_st[u], 32 * (IBLOCKS // 2))

            @block.tensor
            def _(pe):
                pe.wait_ge(m_ff, 1)
                pe.matmul(bc[0][:, 0:half], s.ones[0:1, :], first_f[:, 0:half], start=True, stop=True)
                pe.matmul(bc[1][:, 0:EROWS - half], s.ones[0:1, :], first_f[:, half:], start=True,
                          stop=True).then_inc(m_bc, 1)
                pe.wait_ge(m_step, 1)
                for k in range(2):
                    pe.matmul(pt[k][:, :], valid[:, :], step[:, k * 512:(k + 1) * 512], start=True, stop=True)
                for b in range(IBLOCKS):
                    last = pe.matmul(pc[:, b:b + 1], step[:, b * P:(b + 1) * P], valid[:, 0:1], start=True, stop=True)
                last.then_inc(m_t, 1)
                for b in range(IBLOCKS):
                    u = b % 2
                    pe.wait_ge(m_loc, b + 1)
                    if b >= 2:
                        pe.wait_ge(m_done, b - 1)
                    for c in range(CH):
                        pe.transpose(px[u][:, 0, c, :], srcf[:, u, c * P:(c + 1) * P], s.ident[:, :])
                        last = pe.transpose(px[u][:, 1, c, :], dloc[:, u, c * P:(c + 1) * P], s.ident[:, :])
                    last.then_inc(m_x, 1)

            @block.gpsimd
            def _(g):
                g.wait_ge(m_idx, 1)
                for b in range(IBLOCKS):
                    u = b % 2
                    if b >= 2:
                        g.wait_ge(m_loc, b - 1)
                    for buf, table in ((srcb, src2), (dstb, dst2)):
                        g.indirect_dma_start(buf[:, u, :], None, table,
                                             bass.IndirectOffsetOnAxis(ap=growi[:, b:b + 1], axis=0)
                                             ).then_inc(m_rows[u], 16)

            @block.vector
            def _(v):
                link = linker(v, m_v, 0)
                v.wait_ge(m_first, 16)
                v.tensor_copy(first_f[:, :], first_i[:, :]).then_inc(m_ff, 1)
                link(v.tensor_scalar(bound[:, :], s.part[:, :], float(P), None, ALU.mult))
                link(v.tensor_scalar(vcol[:, 0:1], s.part[:, :], 1.0, None, ALU.is_ge))
                link(v.tensor_scalar(vcol[:, 1:2], s.part[:, :], float(TILES), None, ALU.is_lt))
                link(v.tensor_tensor(vcol[:, 0:1], vcol[:, 0:1], vcol[:, 1:2], ALU.mult))
                link(v.tensor_scalar(valid[:, :], s.ones[:, :], vcol[:, 0:1], None, ALU.mult))
                v.wait_ge(m_bc, 1)
                link(v.tensor_scalar(below[:, 0:half], bc[0][:, 0:half], bound[:, 0:1], None, ALU.is_lt))
                link(v.tensor_scalar(below[:, half:], bc[1][:, 0:EROWS - half], bound[:, 0:1], None, ALU.is_lt))
                link(v.tensor_reduce(cnt[:, :], below[:, 1:EROWS], X, ALU.add))
                link(v.tensor_tensor(begins[:, :], cnt[:, :], s.part[:, :], ALU.add))
                link(v.tensor_scalar(step[:, :], s.item_no[:, :], begins[:, 0:1], None, ALU.is_ge))
                v.sem_inc(m_step, 1)
                v.wait_ge(m_t, 1)
                for k in range(2):
                    v.tensor_copy(s.tile_i[:, k * 512:(k + 1) * 512], pt[k][0:1, :])
                    link(v.tensor_copy(trep[:, k * 512:(k + 1) * 512], pt[k][:, :]))
                link(v.memset(s.fresh[:, 0:1], 1.0))
                link(v.tensor_tensor(s.fresh[:, 1:IPAD], trep[:, 1:IPAD], trep[:, 0:IPAD - 1], ALU.not_equal))
                link(v.tensor_scalar(s.fresh[:, :], s.fresh[:, :], -BIG, None, ALU.mult))
                link(v.tensor_copy(tcol[:, :], pc[:, 0:IBLOCKS]))
                link(v.tensor_scalar(tbase[:, :], tcol[:, :], float(P), None, ALU.mult))
                link(v.tensor_scalar(grow[:, :], s.item_no[:, 0:IPAD:P], s.part[:, 0:1], None, ALU.add))
                link(v.tensor_tensor(grow[:, :], grow[:, :], tcol[:, :], ALU.subtract))
                link(v.tensor_scalar(grow[:, :], grow[:, :], float(EROWS - 1), None, ALU.min))
                v.tensor_copy(growi[:, :], grow[:, :]).then_inc(m_idx, 1)
                link(v.memset(seg[:, :, :], 0.0))

                def tables(b):
                    u = b % 2
                    v.wait_ge(m_x, b + 1)
                    v.tensor_copy(s.src_t[:, b * P:(b + 1) * P, :], px[u][:, 0, :, :].rearrange("p c i -> p i c"))
                    v.tensor_copy(s.dst_t[:, b * P:(b + 1) * P, :],
                                  px[u][:, 1, :, :].rearrange("p c i -> p i c")).then_inc(m_done, 1)

                for b in range(IBLOCKS):
                    u = b % 2
                    v.wait_ge(m_rows[u], 32 * (b // 2 + 1))
                    if b >= 2:
                        v.wait_ge(m_st[u], 32 * (b // 2))
                        v.wait_ge(m_x, b - 1)
                    v.tensor_copy(srcf[:, u, :], srcb[:, u, :])
                    link(v.tensor_scalar(dloc[:, u, :], dstb[:, u, :], tbase[:, b:b + 1], None, ALU.subtract))
                    link(v.tensor_tensor(seg[:, u, 1:EROW], dstb[:, u, 1:EROW], dstb[:, u, 0:EROW - 1], ALU.not_equal))
                    link(v.tensor_scalar(seg[:, u, :], seg[:, u, :], -BIG, None, ALU.mult))
                    link(v.tensor_copy(dlocb[:, u, :], dloc[:, u, :]))
                    v.sem_inc(m_loc, 1)
                    if b >= 1:
                        tables(b - 1)
                tables(IBLOCKS - 1)


def norm_stats(v, link, passed, x, st, mv):
    link(v.bn_stats(st, x))
    v.sem_inc(passed, 1)
    link(v.bn_aggr(mv, st))


def project0(nc, s, x, Wv, bv, wq, bq, wk, bk):
    with ExitStack() as ctx:
        def sb(name, shape, dt=F32):
            return ctx.enter_context(nc.sbuf_tensor(name, shape, dt))

        w = sb("a_w", [P, KD, D])
        rows = sb("a_rows", [P, 3, D])
        bqk = sb("a_bqk", [P, 2])
        kcol = sb("a_kcol", [P, 2])
        xin = sb("a_xin", [P, 2, D])
        st = sb("a_st", [P, 2, 6])
        mv = sb("a_mv", [P, 2, 2])
        ve = sb("a_ve", [P, 2])
        rs = sb("a_rs", [P, 2])
        xn = sb("a_xn", [P, 2, D])
        xT = sb("a_xT", [P, 2, KD, P])
        hq = sb("a_hq", [P, 2, D + 1])
        junk = sb("a_junk", [P, 2, D])
        pT = [ctx.enter_context(nc.psum_tensor(f"a_pT{u}", [P, KD, P], F32)) for u in (0, 1)]
        pH = [ctx.enter_context(nc.psum_tensor(f"a_pH{u}", [P, D], F32)) for u in (0, 1)]
        m_w = s.sem("a_w")
        m_x = [s.sem(f"a_x{u}") for u in (0, 1)]
        m_v, m_var, m_rs, m_xn, m_T, m_xT, m_h, m_hq = (s.sem("a_" + n) for n in
                                                         ("v", "var", "rs", "xn", "T", "xT", "h", "hq"))
        m_st = [s.sem(f"a_st{u}") for u in (0, 1)]
        LINKS1, LINKS2 = 2, 4

        with nc.Block() as block:
            @block.sync
            def _(sp):
                sp.dma_start(w[:, :, :], Wv.rearrange("(k p) n -> p k n", p=P)).then_inc(m_w, 16)
                for j, row in enumerate((bv, wq, wk)):
                    sp.dma_start(rows[:, j, :], row.partition_broadcast(P)).then_inc(m_w, 16)
                for j, one in enumerate((bq, bk)):
                    sp.dma_start(bqk[:, j:j + 1], one.partition_broadcast(P)).then_inc(m_w, 16)

                def load(i, u):
                    if not first(i):
                        sp.wait_ge(m_xn, 2 * i + u - 1)
                    sp.dma_start(xin[:, u, :], x[ds((2 * i + u) * P, P), :]).then_inc(m_x[u], 16)

                pairs(sp, TILES, load)

            @block.gpsimd
            def _(g):
                def root(i, u):
                    g.wait_ge(m_var, 2 * i + u + 1)
                    g.tensor_tensor(rs[:, u:u + 1], ve[:, u:u + 1], s.half[:, :], ALU.pow).then_inc(m_rs, 1)

                pairs(g, TILES, root)

            @block.tensor
            def _(pe):
                pe.wait_ge(m_w, 16 * 6)

                def transposes(i, u):
                    pe.wait_ge(m_xn, 2 * i + u + 1)
                    if not first(i):
                        pe.wait_ge(m_xT, 2 * i + u - 1)
                    for k in range(KD):
                        last = pe.transpose(pT[u][:, k, :], xn[:, u, k * P:(k + 1) * P], s.ident[:, :])
                    last.then_inc(m_T, 1)

                def product(i, u):
                    pe.wait_ge(m_xT, 2 * i + u + 1)
                    if not first(i):
                        pe.wait_ge(m_hq, 2 * i + u - 1)
                    for k in range(KD):
                        last = pe.matmul(pH[u][:, :], xT[:, u, k, :], w[:, k, :], start=k == 0, stop=k == KD - 1)
                    last.then_inc(m_h, 1)

                def step(i, u):
                    transposes(i, u)
                    if before(i, u):
                        product(*before(i, u))

                pairs(pe, TILES, step)
                product(TILES // 2 - 1, 1)

            @block.scalar
            def _(act):
                def copy(i, u):
                    act.wait_ge(m_T, 2 * i + u + 1)
                    if not first(i):
                        act.wait_ge(m_h, 2 * i + u - 1)
                    act.copy(xT[:, u, :, :], pT[u][:, :, :]).then_inc(m_xT, 1)

                def store(i, u):
                    act.wait_ge(m_hq, 2 * i + u + 1)
                    act.dma_start(s.hq_d[ds((2 * i + u) * P, P), :], hq[:, u, :]).then_inc(m_st[u], 16)

                def step(i, u):
                    copy(i, u)
                    if before(i, u):
                        store(*before(i, u))

                pairs(act, TILES, step)
                store(TILES // 2 - 1, 1)
                for u in (0, 1):
                    act.wait_ge(m_st[u], 16 * (TILES // 2))

            @block.vector
            def _(v):
                v.wait_ge(m_w, 16 * 6)

                def normalise(i, u, base):
                    link = linker(v, m_v, base)
                    v.wait_ge(m_x[u], 16 * (i + 1))
                    norm_stats(v, link, s.passed, xin[:, u, :], st[:, u, :], mv[:, u, :])
                    v.tensor_scalar(ve[:, u:u + 1], mv[:, u, 1:2], EPS, None, ALU.add).then_inc(m_var, 1)
                    if not first(i):
                        v.wait_ge(m_T, 2 * i + u - 1)
                    v.wait_ge(m_rs, 2 * i + u + 1)
                    v.tensor_scalar(xn[:, u, :], xin[:, u, :], mv[:, u, 0:1], rs[:, u:u + 1], ALU.subtract,
                                    ALU.mult).then_inc(m_xn, 1)
                    assert link.count[0] == LINKS1

                def finish(i, u, base):
                    link = linker(v, m_v, base)
                    t = 2 * i + u
                    v.wait_ge(m_h, t + 1)
                    if not first(i):
                        v.wait_ge(m_st[u], 16 * i)
                    link(v.tensor_tensor(hq[:, u, 0:D], pH[u][:, :], rows[:, 0, :], ALU.add))
                    link(v.tensor_tensor_reduce(junk[:, 0, :], hq[:, u, 0:D], rows[:, 1, :], 1.0, 0.0, ALU.mult,
                                                ALU.add, hq[:, u, D:D + 1]))
                    link(v.tensor_tensor_reduce(junk[:, 1, :], hq[:, u, 0:D], rows[:, 2, :], 1.0, 0.0, ALU.mult,
                                                ALU.add, kcol[:, u:u + 1]))
                    link(v.tensor_scalar(s.kf[:, ds(t, 1)], kcol[:, u:u + 1], bqk[:, 1:2], None, ALU.add))
                    v.tensor_scalar(hq[:, u, D:D + 1], hq[:, u, D:D + 1], bqk[:, 0:1], None, ALU.add).then_inc(m_hq, 1)
                    assert link.count[0] == LINKS2

                def step(i, u):
                    t = 2 * i + u
                    normalise(i, u, t * LINKS1 + ((t - 1) * LINKS2 if before(i, u) else 0))
                    if before(i, u):
                        finish(*before(i, u), (t + 1) * LINKS1 + (t - 1) * LINKS2)

                pairs(v, TILES, step)
                finish(TILES // 2 - 1, 1, TILES * LINKS1 + (TILES - 1) * LINKS2)
                link = linker(v, m_v, TILES * (LINKS1 + LINKS2))
                v.wait_ge(m_hq, TILES)
                link(v.tensor_copy(s.k0[:, :, 0], s.kf[:, :]))
                for c in range(1, KPARTS):
                    link(v.tensor_tensor(s.kf[:, :], s.kf[:, :], s.k0[:, :, c - 1], ALU.subtract))
                    link(v.tensor_copy(s.k0[:, :, c], s.kf[:, :]))


def edges0(nc, s):
    with ExitStack() as ctx:
        def sb(name, shape, dt=F32):
            return ctx.enter_context(nc.sbuf_tensor(name, shape, dt))

        R = sb("e_R", [P, RING, GROUP, CH, HCOLS])
        idx = sb("e_idx", [P, RING, COLS], I32)
        drow = sb("e_drow", [P, 2, GROUP, EROW], BF16)
        seg = sb("e_seg", [GROUP, 2, EROW + 1])
        OHT = sb("e_OHT", [P, 2, GROUP, EROW], BF16)
        OH = sb("e_OH", [P, 2, COLS, P], BF16)
        W = sb("e_W", [P, 2, COLS, P])
        fwd = sb("e_fwd", [GROUP, EROW])
        bwd = sb("e_bwd", [GROUP, EROW])
        mx = sb("e_mx", [GROUP, EROW])
        dcol = sb("e_dcol", [P, 2, COLS])
        kS = sb("e_kS", [P, GROUP, CH])
        z = sb("e_z", [P, 2, GROUP, CH])
        c = sb("e_c", [P, 2, GROUP, CH])
        dd = sb("e_dd", [P, COLS])
        w = sb("e_w", [P, 2, COLS])
        rl = sb("e_rl", [P, GROUP])
        ltmp = sb("e_ltmp", [P, 2, GROUP])
        none = sb("e_none", [P, GROUP])
        sn = sb("e_sn", [P, GROUP])
        run = sb("e_run", [P, GROUP + 1])
        old = sb("e_old", [P, GROUP])
        dab = sb("e_dab", [P, 2, GROUP])
        ab = sb("e_ab", [P, 2, 2, GROUP])
        tmp = sb("e_tmp", [P, 2, GROUP, ACOLS])

        pA = ctx.enter_context(nc.psum_tensor("e_pA", [P, 2, GROUP // 2, 2, D], F32))
        pL = ctx.enter_context(nc.psum_tensor("e_pL", [P, GROUP, 2], F32))
        pS = ctx.enter_context(nc.psum_tensor("e_pS", [P, 512], F32))
        pK = pS[:, 0:COLS * KPARTS]
        pM = ctx.enter_context(nc.psum_tensor("e_pM", [P, 512], F32))[:, 0:COLS]
        pQ = pS[0:GROUP, 128:128 + EROW]
        m_idx = s.sem("e_idx")
        m_g = [s.sem(f"e_g{u}") for u in range(RING)]
        m_row = [s.sem(f"e_row{u}") for u in (0, 1)]
        (m_v, m_one, m_oh, m_oht, m_q, m_mx, m_mxe, m_dd, m_w, m_W, m_l, m_sum, m_dab, m_ab, m_tmp, m_done, m_old) = (
            s.sem("e_" + n) for n in ("v", "one", "oh", "oht", "q", "mx", "mxe", "dd", "w", "W", "l", "sum", "dab",
                                      "ab", "tmp", "done", "old"))
        LINKS_S, LINKS_Z, LINKS_M, LINKS_C = 3, 3, 7, 1 + GROUP
        LINKS = LINKS_S + LINKS_Z + LINKS_M + LINKS_C

        with nc.Block() as block:
            @block.gpsimd
            def _(g):
                def gather(i, u):
                    b = RING * i + u
                    if not first(i):
                        g.wait_ge(m_sum, 2 * (b - RING + 1))
                    g.tensor_copy(idx[:, u, :], s.src_t[:, ds(b * GROUP, GROUP), :]).then_inc(m_idx, 1)
                    g.wait_ge(m_idx, b + 1)
                    g.sem_inc(s.passed, 1)
                    for n in range(COLS):
                        g.indirect_dma_start(R[:, u, n // CH, n % CH, 0:D + 1], None, s.hq_d[:, :],
                                             bass.IndirectOffsetOnAxis(ap=idx[:, u, n:n + 1], axis=0)
                                             ).then_inc(m_g[u], 16)

                g.wait_ge(m_one, 1)
                turns(g, GROUPS, RING, gather)

            @block.sync
            def _(sp):
                def load(i, u):
                    b = 2 * i + u
                    if not first(i):
                        sp.wait_ge(m_mx, b - 1)
                    sp.dma_start(drow[:, u, :, :], s.drow_d[ds(b * GROUP, GROUP), :].partition_broadcast(P)
                                 ).then_inc(m_row[u], 16)
                    sp.dma_start(seg[:, u, :], s.seg_d[ds(b * GROUP, GROUP), :]).then_inc(m_row[u], 16)

                turns(sp, GROUPS, 2, load)

            @block.tensor
            def _(pe):
                def edge_values(i, u, tiles):
                    b = RING * i + u
                    if before(i, u, RING):
                        pe.wait_ge(m_dd, b)
                    pe.wait_ge(m_oht, b + 1)
                    for n in range(COLS):
                        pe.matmul(pK[:, n * KPARTS:(n + 1) * KPARTS],
                                  OHT[:, u % 2, n // CH, (n % CH) * P:(n % CH + 1) * P],
                                  s.k0[:, ds(tiles[n // CH], 1), :], start=True, stop=True)
                    pe.wait_ge(m_g[u], 16 * COLS * (i + 1))
                    for j in range(CH):
                        last = pe.transpose(pQ[:, j * P:(j + 1) * P], R[:, u, :, j, QCOL], s.ident[:, :])
                    last.then_inc(m_q, 1)

                def turn_maxima(i, u):
                    pe.wait_ge(m_mx, RING * i + u + 1)
                    pe.sem_inc(s.passed, 1)
                    for j in range(CH):
                        last = pe.transpose(pM[:, j * GROUP:(j + 1) * GROUP], mx[:, j * P:(j + 1) * P],
                                            s.ident[0:GROUP, 0:GROUP])
                    last.then_inc(m_mxe, 1)

                def totals(i, u):
                    b = RING * i + u
                    for n in range(COLS):
                        pe.wait_ge(m_W, COLS * b + n + 1)
                        if n == 0 and before(i, u, RING):
                            pe.wait_ge(m_dab, b)
                        last = pe.matmul(pL[:, n // CH, :], W[:, u % 2, n, :], R[:, u, n // CH, n % CH, ONECOL:HCOLS],
                                         start=n % CH == 0, stop=n % CH == CH - 1)
                    last.then_inc(m_l, 1)

                def sums(i, u, half):
                    b = RING * i + u
                    if not first(i) or u >= 2:
                        pe.wait_ge(m_tmp, (b - 2) * GROUP + 2 * half + 2)
                    for n in (2 * half, 2 * half + 1):
                        for j in range(CH):
                            last = pe.matmul(pA[:, u % 2, half, n % 2, :], W[:, u % 2, n * CH + j, :],
                                             R[:, u, n, j, 0:D], start=j == 0, stop=j == CH - 1)
                    last.then_inc(m_sum, 1)

                def step(i, u, opened, left=None):
                    if left != 0:
                        edge_values(*after(i, u, RING), opened[u * GROUP:(u + 1) * GROUP])
                    totals(i, u)
                    sums(i, u, 0)
                    if left != 0:
                        turn_maxima(*after(i, u, RING))
                    sums(i, u, 1)

                edge_values(0, 0, load_tiles(nc, s, ENGINE.PE, 0))
                turn_maxima(0, 0)
                turns(pe, GROUPS, RING, step, peel_last=True,
                      open_round=lambda i: load_tiles(nc, s, ENGINE.PE, RING * i + 1, RING))

            @block.scalar
            def _(act):
                def weights(i, u):
                    b = RING * i + u
                    act.wait_ge(m_dd, b + 1)
                    if not first(i) or u >= 2:
                        act.wait_ge(m_sum, 2 * (b - 1))
                    act.activation(w[:, u % 2, :], dd[:, :], ACT.Exp).then_inc(m_w, 1)
                    act.wait_ge(m_w, b + 1)
                    act.wait_ge(m_oh, b + 1)
                    for n in range(COLS):
                        act.activation(W[:, u % 2, n, :], OH[:, u % 2, n, :], ACT.Copy, scale=w[:, u % 2, n:n + 1]
                                       ).then_inc(m_W, 1)

                def factors(i, u):
                    b = RING * i + u
                    act.wait_ge(m_dab, b + 1)
                    if not first(i) or u >= 2:
                        act.wait_ge(m_done, b - 1)
                    act.activation(ab[:, u % 2, :, :], dab[:, :, :], ACT.Exp).then_inc(m_ab, 1)

                def rescale(i, u):
                    b = RING * i + u
                    act.wait_ge(m_ab, b + 1)
                    for n in range(GROUP):
                        if n % 2 == 0:
                            act.wait_ge(m_sum, 2 * b + n // 2 + 1)
                        act.activation(tmp[:, u % 2, n, 0:D], pA[:, u % 2, n // 2, n % 2, :], ACT.Copy,
                                       scale=ab[:, u % 2, 1, n:n + 1]
                                       ).then_inc(m_tmp, 1)

                def step(i, u, left=None):
                    factors(i, u)
                    if left != 0:
                        weights(*after(i, u, RING))
                    rescale(i, u)

                weights(0, 0)
                turns(act, GROUPS, RING, step, peel_last=True)

            @block.vector
            def _(v):
                v.memset(run[:, 0:1], -BIG)
                v.memset(R[:, :, :, :, ONECOL], 1.0).then_inc(m_one, 1)

                def select(i, u):
                    b = RING * i + u
                    h = u % 2
                    v.tensor_copy(dcol[:, h, :], s.dst_t[:, ds(b * GROUP, GROUP), :]).then_inc(m_old, 1)
                    v.wait_ge(m_row[h], 32 * (i * (RING // 2) + u // 2 + 1))
                    if not first(i) or u >= 2:
                        v.wait_ge(m_q, b - 1)
                        v.wait_ge(m_W, COLS * (b - 1))
                    v.tensor_scalar(OHT[:, h, :, :], drow[:, h, :, :], s.part[:, 0:1], None,
                                    ALU.is_equal).then_inc(m_oht, 1)
                    v.wait_ge(m_old, b + 1)

                def select_columns(i, u, columns):
                    for n in columns:
                        last = v.tensor_scalar(OH[:, u % 2, n, :], s.iota_b[:, :], dcol[:, u % 2, n:n + 1], None,
                                               ALU.is_equal)
                    if n == COLS - 1:
                        last.then_inc(m_oh, 1)

                def scans(i, u, base):
                    b = RING * i + u
                    h = u % 2
                    link = linker(v, m_v, base)
                    v.wait_ge(m_q, b + 1)
                    v.tensor_tensor_scan(fwd[:, :], seg[:, h, 0:EROW], pQ, -BIG, ALU.add, ALU.max)
                    link(v.tensor_tensor_scan(bwd[:, ::-1], seg[:, h, 1:EROW + 1][:, ::-1], pQ[:, ::-1], -BIG,
                                              ALU.add, ALU.max))
                    v.tensor_tensor(mx[:, :], fwd[:, :], bwd[:, :], ALU.max).then_inc(m_mx, 1)
                    link(v.tensor_reduce(kS[:, :, :], pK.rearrange("p (n j c) -> p n j c", j=CH, c=KPARTS), X, ALU.add))
                    link(v.tensor_tensor(z[:, 0, :, :], R[:, u, :, :, QCOL], kS[:, :, :], ALU.add))
                    assert link.count[0] == LINKS_S, link.count

                def shifts(i, u, base):
                    b = RING * i + u
                    link = linker(v, m_v, base)
                    v.wait_ge(m_mxe, b + 1)
                    link(v.tensor_tensor(z[:, 1, :, :], pM.rearrange("p (j n) -> p n j", j=CH), kS[:, :, :], ALU.add))
                    link(v.scalar_tensor_tensor(c[:, :, :, :], z[:, :, :, :], 0.2, z[:, :, :, :], ALU.mult, ALU.max))
                    v.tensor_copy(R[:, u, :, :, SCOL], c[:, 1, :, :])
                    v.tensor_tensor(dd[:, :], c[:, 0, :, :], c[:, 1, :, :], ALU.subtract).then_inc(m_v, 1)
                    link.count[0] += 1
                    v.wait_ge(m_v, base + LINKS_Z)
                    v.sem_inc(m_dd, 1)
                    assert link.count[0] == LINKS_Z, link.count

                def maxima(i, u, base):
                    b = RING * i + u
                    link = linker(v, m_v, base)
                    v.wait_ge(m_l, b + 1)
                    link(v.tensor_scalar(rl[:, :], pL[:, :, 0], 1e-30, None, ALU.max))
                    link(v.reciprocal(rl[:, :], rl[:, :]))
                    v.tensor_scalar(none[:, :], pL[:, :, 0], 0.5, -BIG, ALU.is_lt, ALU.mult)
                    link(v.tensor_tensor(sn[:, :], pL[:, :, 1], rl[:, :], ALU.mult))
                    link(v.tensor_tensor(sn[:, :], sn[:, :], none[:, :], ALU.add))
                    link(v.tensor_tensor_scan(run[:, 1:GROUP + 1], s.fresh[:, ds(b * GROUP, GROUP)], sn[:, :],
                                              run[:, 0:1], ALU.add, ALU.max))
                    link(v.tensor_tensor(old[:, :], run[:, 0:GROUP], s.fresh[:, ds(b * GROUP, GROUP)], ALU.add))
                    v.tensor_copy(ltmp[:, u % 2, :], pL[:, :, 0])
                    v.tensor_tensor(dab[:, 0, :], old[:, :], run[:, 1:GROUP + 1], ALU.subtract)
                    v.tensor_tensor(dab[:, 1, :], sn[:, :], run[:, 1:GROUP + 1], ALU.subtract).then_inc(m_dab, 1)
                    link(v.tensor_copy(run[:, 0:1], run[:, GROUP:GROUP + 1]))
                    assert link.count[0] == LINKS_M, link.count

                def merge(i, u, base, tiles, between=None):
                    b = RING * i + u
                    h = u % 2
                    link = linker(v, m_v, base)
                    v.wait_ge(m_ab, b + 1)
                    link(v.tensor_tensor(tmp[:, h, :, D], ltmp[:, h, :], ab[:, h, 1, :], ALU.mult))
                    for n in range(GROUP):
                        v.wait_ge(m_tmp, b * GROUP + n + 1)
                        if n:
                            v.wait_ge(m_v, base + 1 + n)
                        a = s.acc[:, ds(tiles[n], 1), :]
                        v.scalar_tensor_tensor(a, a, ab[:, h, 0, n:n + 1], tmp[:, h, n:n + 1, :], ALU.mult,
                                               ALU.add).then_inc(m_v, 1)
                        if between:
                            between(n)
                    v.wait_ge(m_v, base + LINKS_C)
                    v.sem_inc(m_done, 1)

                def step(i, u, opened, left=None):
                    b = RING * i + u
                    past = before(i, u, RING)
                    base = LINKS_S + LINKS_Z + b * (LINKS_S + LINKS_Z + LINKS_M) + ((b - 1) * LINKS_C if past else 0)
                    if left != 0:
                        scans(*after(i, u, RING), base)
                        base = base + LINKS_S
                    maxima(i, u, base)
                    base = base + LINKS_M
                    if left != 0:
                        shifts(*after(i, u, RING), base)
                        base = base + LINKS_Z
                    ahead = left is None or left > 1
                    if ahead:
                        select(*after(i, u, RING, 2))
                    if past:
                        def between(n):
                            if ahead:
                                select_columns(*after(i, u, RING, 2), range(n * CH, (n + 1) * CH))
                        merge(*past, base, opened[u * GROUP:(u + 1) * GROUP], between)
                    else:
                        select_columns(*after(i, u, RING, 2), range(COLS))

                def open_round(i):
                    if first(i):
                        return (None,) * GROUP + tuple(load_tiles(nc, s, ENGINE.DVE, 0, RING - 1))
                    return load_tiles(nc, s, ENGINE.DVE, RING * i - 1, RING)

                for u in (0, 1):
                    select(0, u)
                    select_columns(0, u, range(COLS))
                scans(0, 0, 0)
                shifts(0, 0, LINKS_S)
                turns(v, GROUPS, RING, step, peel_last=True, open_round=open_round)
                merge(*LAST_TURN, (GROUPS - 1) * LINKS + LINKS_S + LINKS_Z + LINKS_M,
                      load_tiles(nc, s, ENGINE.DVE, GROUPS - 1))


def finish0(nc, s, x):
    with ExitStack() as ctx:
        def sb(name, shape, dt=F32):
            return ctx.enter_context(nc.sbuf_tensor(name, shape, dt))

        xin = sb("f_xin", [P, 2, D])
        x1 = sb("f_x1", [P, 2, 2, D])
        den = sb("f_den", [P, 2])
        rd = sb("f_rd", [P, 2])
        st = sb("f_st", [P, 2, 6])
        mv = sb("f_mv", [P, 2, 2])
        ve = sb("f_ve", [P, 2])
        rs = sb("f_rs", [P, 2])
        m_x = [s.sem(f"f_x{u}") for u in (0, 1)]
        m_st = [s.sem(f"f_st{u}") for u in (0, 1)]
        m_v, m_x1, m_var, m_rs, m_xn = (s.sem("f_" + n) for n in ("v", "res", "var", "rs", "xn"))
        LINKS1, LINKS2 = 4, 2

        with nc.Block() as block:
            @block.sync
            def _(sp):
                def load(i, u):
                    if not first(i):
                        sp.wait_ge(m_x1, 2 * i + u - 1)
                    sp.dma_start(xin[:, u, :], x[ds((2 * i + u) * P, P), :]).then_inc(m_x[u], 16)

                pairs(sp, TILES, load)

            @block.scalar
            def _(act):
                def store(i, u):
                    act.wait_ge(m_xn, 2 * i + u + 1)
                    act.dma_start(s.x1_d[ds((2 * i + u) * P, P), :], x1[:, u, :, :]).then_inc(m_st[u], 16)

                pairs(act, TILES, store)
                for u in (0, 1):
                    act.wait_ge(m_st[u], 16 * (TILES // 2))

            @block.gpsimd
            def _(g):
                def root(i, u):
                    g.wait_ge(m_var, 2 * i + u + 1)
                    g.tensor_tensor(rs[:, u:u + 1], ve[:, u:u + 1], s.half[:, :], ALU.pow).then_inc(m_rs, 1)

                pairs(g, TILES, root)

            @block.vector
            def _(v):
                v.memset(s.xsum[:, :], 0.0)

                def residual(i, u, base):
                    t = 2 * i + u
                    link = linker(v, m_v, base)
                    link(v.tensor_scalar(den[:, u:u + 1], s.acc[:, ds(t, 1), D], 1e-30, None, ALU.max))
                    link(v.reciprocal(rd[:, u:u + 1], den[:, u:u + 1]))
                    v.wait_ge(m_x[u], 16 * (i + 1))
                    if not first(i):
                        v.wait_ge(m_st[u], 16 * i)
                    v.scalar_tensor_tensor(x1[:, u, 0:1, :], s.acc[:, ds(t, 1), 0:D], rd[:, u:u + 1],
                                           xin[:, u:u + 1, :], ALU.mult, ALU.add).then_inc(m_x1, 1)
                    v.wait_ge(m_x1, t + 1)
                    norm_stats(v, link, s.passed, x1[:, u, 0, :], st[:, u, :], mv[:, u, :])
                    v.tensor_scalar(ve[:, u:u + 1], mv[:, u, 1:2], EPS, None, ALU.add).then_inc(m_var, 1)
                    assert link.count[0] == LINKS1

                def normalise(i, u, base):
                    t = 2 * i + u
                    link = linker(v, m_v, base)
                    v.wait_ge(m_rs, t + 1)
                    link(v.tensor_scalar(x1[:, u, 1, :], x1[:, u, 0, :], mv[:, u, 0:1], rs[:, u:u + 1],
                                         ALU.subtract, ALU.mult))
                    v.sem_inc(m_xn, 1)
                    link(v.tensor_tensor(s.xsum[:, :], s.xsum[:, :], x1[:, u, 1, :], ALU.add))
                    assert link.count[0] == LINKS2

                def step(i, u):
                    t = 2 * i + u
                    residual(i, u, t * LINKS1 + ((t - 1) * LINKS2 if before(i, u) else 0))
                    if before(i, u):
                        normalise(*before(i, u), (t + 1) * LINKS1 + (t - 1) * LINKS2)

                pairs(v, TILES, step)
                normalise(TILES // 2 - 1, 1, TILES * LINKS1 + (TILES - 1) * LINKS2)


def route0(nc, s, a):
    with ExitStack() as ctx:
        def sb(name, shape, dt=F32):
            return ctx.enter_context(nc.sbuf_tensor(name, shape, dt))

        wr = sb("r_wr", [P, KD, EXPERTS])
        br = sb("r_br", [1, EXPERTS])
        mean = sb("r_mean", [P, KD])
        row = sb("r_row", [1, EXPERTS])
        ex = sb("r_ex", [1, EXPERTS])
        sc = sb("r_sc", [1, EXPERTS])
        eq = sb("r_eq", [1, EXPERTS])
        one = sb("r_one", [1, 8])
        top = sb("r_top", [1, 2])
        tex = sb("r_tex", [1, 2])
        wtop = sb("r_wtop", [1, 2])
        pm = ctx.enter_context(nc.psum_tensor("r_pm", [P, KD], F32))
        pl = ctx.enter_context(nc.psum_tensor("r_pl", [1, EXPERTS], F32))
        pw = ctx.enter_context(nc.psum_tensor("r_pw", [P, 2], F32))
        m_w, m_pe, m_v, m_a, m_go, m_mean, m_top = (s.sem("r_" + n) for n in
                                                    ("w", "pe", "v", "a", "go", "mean", "wtop"))

        with nc.Block() as block:
            @block.sync
            def _(sp):
                sp.dma_start(wr[:, :, :], a["L0_ffn_Wr"].rearrange("(k p) e -> p k e", p=P)).then_inc(m_w, 16)
                sp.dma_start(br[:, :], a["L0_ffn_br"].partition_broadcast(1)).then_inc(m_w, 16)

            @block.tensor
            def _(pe):
                for k in range(KD):
                    last = pe.matmul(pm[:, k:k + 1], s.xsum[:, k * P:(k + 1) * P], s.ones[:, 0:1], start=True, stop=True)
                last.then_inc(m_pe, 1)
                pe.wait_ge(m_w, 32)
                pe.wait_ge(m_mean, 1)
                for k in range(KD):
                    last = pe.matmul(pl[:, :], mean[:, k:k + 1], wr[:, k, :], start=k == 0, stop=k == KD - 1)
                last.then_inc(m_pe, 1)
                pe.wait_ge(m_top, 1)
                pe.matmul(pw[:, :], s.ones[0:1, :], wtop[:, :], start=True, stop=True).then_inc(m_pe, 1)

            @block.scalar
            def _(act):
                for n, (dst, src) in enumerate(((ex, row), (ex, row), (tex, top))):
                    act.wait_ge(m_go, n + 1)
                    act.activation(dst[:, :], src[:, :], ACT.Exp).then_inc(m_a, 1)

            @block.vector
            def _(v):
                link = linker(v, m_v, 0)
                exps = [0]

                def softmax(row_, ex_, out_):
                    link(v.tensor_reduce(one[:, 0:1], row_, X, ALU.max))
                    v.tensor_scalar(row_, row_, one[:, 0:1], None, ALU.subtract).then_inc(m_go, 1)
                    exps[0] += 1
                    v.wait_ge(m_a, exps[0])
                    link(v.tensor_reduce(one[:, 1:2], ex_, X, ALU.add))
                    link(v.reciprocal(one[:, 2:3], one[:, 1:2]))
                    return v.tensor_scalar(out_, ex_, one[:, 2:3], None, ALU.mult)

                v.wait_ge(m_pe, 1)
                v.tensor_scalar(mean[:, :], pm[:, :], 1.0 / N, None, ALU.mult).then_inc(m_mean, 1)
                v.wait_ge(m_pe, 2)
                link(v.tensor_tensor(row[:, :], pl[:, :], br[:, :], ALU.add))
                link(softmax(row[:, :], ex[:, :], row[:, :]))
                link(v.tensor_scalar(sc[:, :], row[:, :], float(N), None, ALU.mult))
                link(v.tensor_scalar(sc[:, :], sc[:, :], CAPACITY, None, ALU.max))
                link(v.reciprocal(sc[:, :], sc[:, :]))
                link(v.tensor_scalar(sc[:, :], sc[:, :], CAPACITY, None, ALU.mult))
                link(v.tensor_tensor(row[:, :], row[:, :], sc[:, :], ALU.mult))
                link(softmax(row[:, :], ex[:, :], row[:, :]))
                for j in range(2):
                    link(v.tensor_reduce(top[:, j:j + 1], row[:, :], X, ALU.max))
                    link(v.tensor_scalar(eq[:, :], row[:, :], top[:, j:j + 1], None, ALU.is_equal))
                    link(v.tensor_scalar(sc[:, :], s.iota[0:1, 0:EXPERTS], float(-EXPERTS), None, ALU.add))
                    link(v.tensor_tensor(sc[:, :], sc[:, :], eq[:, :], ALU.mult))
                    link(v.tensor_reduce(one[:, 3:4], sc[:, :], X, ALU.min))
                    link(v.tensor_scalar(one[:, 4:5], one[:, 3:4], float(EXPERTS), None, ALU.add))
                    link(v.tensor_copy(s.expert_i[:, j:j + 1], one[:, 4:5]))
                    link(v.tensor_scalar(eq[:, :], s.iota[0:1, 0:EXPERTS], one[:, 4:5], -2.0, ALU.is_equal, ALU.mult))
                    link(v.tensor_tensor(row[:, :], row[:, :], eq[:, :], ALU.add))
                softmax(top[:, :], tex[:, :], wtop[:, :]).then_inc(m_top, 1)
                v.wait_ge(m_pe, 3)
                v.tensor_copy(s.wexp[:, :], pw[:, :])


def feed_forward(nc, s, name, func, table, load_weights, prepare, finish, roots, store):
    with ExitStack() as ctx:
        def sb(n, shape, dt=F32):
            return ctx.enter_context(nc.sbuf_tensor(name + n, shape, dt))

        def ps(n, shape):
            return ctx.enter_context(nc.psum_tensor(name + n, shape, F32))

        f = Shared()
        f.w1 = sb("w1", [P, KD, HID])
        f.b1 = sb("b1", [P, HB])
        f.w2 = sb("w2", [P, HB, D])
        f.vec = sb("vec", [P, 4, D])
        f.xrow = sb("xrow", [P, 2, 2, D])
        f.o = sb("o", [P, 2, D])
        f.t1 = sb("t1", [P, 2, D])
        f.st, f.mv, f.ve, f.rs = sb("st", [P, 2, 6]), sb("mv", [P, 2, 2]), sb("ve", [P, 2]), sb("rs", [P, 2])
        xT = sb("xT", [P, 2, KD, P])
        h = sb("h", [P, HB, P])
        pT = ps("pT", [P, KD, P])
        pH = [ps(f"pH{n}", [P, 2, P]) for n in range(HB // 2)]
        f.pY = [ps(f"pY{n}", [P, D]) for n in (0, 1)]
        f.m_w, f.m_v, m_T, m_xT, m_h, m_g, f.m_y, f.m_o, m_set, f.m_var, f.m_rs, f.m_yr = (
            s.sem(name + n) for n in ("w", "v", "T", "xT", "h", "g", "y", "o", "set", "var", "rs", "yread"))
        m_row = [s.sem(f"{name}row{u}") for u in (0, 1)]
        f.m_st = [s.sem(f"{name}st{u}") for u in (0, 1)]

        with nc.Block() as block:
            @block.sync
            def _(sp):
                load_weights(sp, f)

                def rows(i, u):
                    if not first(i):
                        sp.wait_ge(f.m_o, 2 * i + u - 1)
                    sp.dma_start(f.xrow[:, u, :, :], table[ds((2 * i + u) * P, P), :]).then_inc(m_row[u], 16)

                pairs(sp, TILES, rows)

            if roots:
                @block.gpsimd
                def _(g):
                    def root(i, u):
                        g.wait_ge(f.m_var, 2 * i + u + 1)
                        g.tensor_tensor(f.rs[:, u:u + 1], f.ve[:, u:u + 1], s.half[:, :], ALU.pow).then_inc(f.m_rs, 1)

                    pairs(g, TILES, root)

            @block.tensor
            def _(pe):
                def transposes(i, u):
                    pe.wait_ge(m_row[u], 16 * (i + 1))
                    if before(i, u):
                        pe.wait_ge(m_xT, 2 * i + u)
                    for k in range(KD):
                        last = pe.transpose(pT[:, k, :], f.xrow[:, u, 1, k * P:(k + 1) * P], s.ident[:, :])
                    last.then_inc(m_T, 1)

                def hidden(i, u):
                    pe.wait_ge(m_xT, 2 * i + u + 1)
                    for n in range(HB):
                        for k in range(KD):
                            last = pe.matmul(pH[n // 2][:, n % 2, :], f.w1[:, k, n * P:(n + 1) * P], xT[:, u, k, :],
                                             start=k == 0, stop=k == KD - 1)
                        if n % 2:
                            last.then_inc(m_h, 1)

                def output(i, u):
                    if not first(i):
                        pe.wait_ge(f.m_yr, 2 * i + u - 1)
                    for n in range(HB):
                        pe.wait_ge(m_g, (2 * i + u) * HB + n + 1)
                        last = pe.matmul(f.pY[u][:, :], h[:, n, :], f.w2[:, n, :], start=n == 0, stop=n == HB - 1)
                    last.then_inc(f.m_y, 1)

                def step(i, u):
                    if before(i, u):
                        hidden(*before(i, u))
                    transposes(i, u)
                    if before(i, u):
                        output(*before(i, u))

                pe.wait_ge(m_set, 1)
                pairs(pe, TILES, step)
                hidden(TILES // 2 - 1, 1)
                output(TILES // 2 - 1, 1)

            @block.scalar
            def _(act):
                def turned(i, u):
                    act.wait_ge(m_T, 2 * i + u + 1)
                    if not first(i):
                        act.wait_ge(m_h, (2 * i + u - 1) * (HB // 2))
                    act.copy(xT[:, u, :, :], pT[:, :, :]).then_inc(m_xT, 1)

                def hidden(i, u):
                    t = 2 * i + u
                    for n in range(HB):
                        if n % 2 == 0:
                            act.wait_ge(m_h, t * (HB // 2) + n // 2 + 1)
                        if n == 0 and before(i, u):
                            act.wait_ge(f.m_y, t)
                        act.activation(h[:, n, :], pH[n // 2][:, n % 2, :], func, bias=f.b1[:, n:n + 1]).then_inc(m_g, 1)

                def step(i, u):
                    if before(i, u):
                        hidden(*before(i, u))
                    turned(i, u)
                    if before(i, u) and before(*before(i, u)):
                        store(act, f, *before(*before(i, u)), False)

                act.wait_ge(m_set, 1)
                pairs(act, TILES, step)
                hidden(TILES // 2 - 1, 1)
                store(act, f, TILES // 2 - 1, 0, False)
                store(act, f, TILES // 2 - 1, 1, True)
                for u in (0, 1):
                    act.wait_ge(f.m_st[u], 16 * (TILES // 2))

            @block.vector
            def _(v):
                base = prepare(v, f)
                v.sem_inc(m_set, 1)
                pairs(v, TILES, lambda i, u: finish(v, f, i, u, base))


def feed_forward0(nc, s, a):
    EH = HID // 2

    def load(sp, f):
        experts = [sp.value_load(s.expert_i[0:1, j:j + 1], min_val=0, max_val=EXPERTS - 1) for j in (0, 1)]
        with nc.allow_non_contiguous_dma(reason="biases, one to a partition"):
            for j, e in enumerate(experts):
                sp.dma_start(f.w1[:, :, j * EH:(j + 1) * EH],
                             a["L0_ffn_W1"][ds(e, 1), :, :].rearrange("o (k p) f -> p (o k) f", p=P)).then_inc(f.m_w, 16)
                sp.dma_start(f.w2[:, j * HB // 2:(j + 1) * HB // 2, :],
                             a["L0_ffn_W2"][ds(e, 1), :, :].rearrange("o (n p) d -> p (o n) d", p=P)).then_inc(f.m_w, 16)
                sp.dma_start(f.b1[:, j * HB // 2:(j + 1) * HB // 2],
                             a["L0_ffn_b1"][ds(e, 1), :].rearrange("o (n p) -> p (o n)", p=P)).then_inc(f.m_w, 16)
                sp.dma_start(f.vec[:, j, :], a["L0_ffn_b2"][ds(e, 1), :].partition_broadcast(P)).then_inc(f.m_w, 16)
        for j, n in enumerate(("L0_ffn_gamma", "L0_ffn_beta")):
            sp.dma_start(f.vec[:, 2 + j, :], a[n].partition_broadcast(P)).then_inc(f.m_w, 16)

    def prepare(v, f):
        link = linker(v, f.m_v, 0)
        v.wait_ge(f.m_w, 16 * 10)
        for j in (0, 1):
            w2 = f.w2[:, j * HB // 2:(j + 1) * HB // 2, :]
            link(v.tensor_scalar(w2, w2, s.wexp[:, j:j + 1], None, ALU.mult))
            link(v.tensor_scalar(f.vec[:, j, :], f.vec[:, j, :], s.wexp[:, j:j + 1], None, ALU.mult))
        link(v.tensor_tensor(f.vec[:, 0, :], f.vec[:, 0, :], f.vec[:, 1, :], ALU.add))
        return link.count[0]

    LINKS = 7

    def finish(v, f, i, u, base):
        t = 2 * i + u
        link = linker(v, f.m_v, base + t * LINKS)
        t1 = f.t1[:, u, :]
        v.wait_ge(f.m_y, t + 1)
        v.tensor_tensor(t1, f.pY[u][:, :], f.vec[:, 0, :], ALU.add).then_inc(f.m_yr, 1)
        v.wait_ge(f.m_yr, t + 1)
        link(v.tensor_tensor(t1, t1, f.xrow[:, u, 1, :], ALU.add))
        norm_stats(v, link, s.passed, t1, f.st[:, u, :], f.mv[:, u, :])
        v.tensor_scalar(f.ve[:, u:u + 1], f.mv[:, u, 1:2], EPS, None, ALU.add).then_inc(f.m_var, 1)
        v.wait_ge(f.m_rs, t + 1)
        link(v.tensor_scalar(t1, t1, f.mv[:, u, 0:1], f.rs[:, u:u + 1], ALU.subtract, ALU.mult))
        link(v.tensor_tensor(t1, t1, f.vec[:, 2, :], ALU.mult))
        link(v.tensor_tensor(t1, t1, f.vec[:, 3, :], ALU.add))
        if not first(i):
            v.wait_ge(f.m_st[u], 16 * i)
        link(v.tensor_tensor(f.o[:, u, :], t1, f.xrow[:, u, 0, :], ALU.add))
        v.sem_inc(f.m_o, 1)
        assert link.count[0] == LINKS, link.count

    def store(act, f, i, u, last):
        act.wait_ge(f.m_o, 2 * i + u + 1)
        act.dma_start(s.x2_d[ds((2 * i + u) * P, P), :], f.o[:, u, :]).then_inc(f.m_st[u], 16)

    feed_forward(nc, s, "g", ACT.Gelu, s.x1_d, load, prepare, finish, True, store)


def feed_forward1(nc, s, a, out):
    def load(sp, f):
        sp.dma_start(f.w1[:, :, :], a["L1_ffn_w1"].rearrange("(k p) f -> p k f", p=P)).then_inc(f.m_w, 16)
        sp.dma_start(f.w2[:, :, :], a["L1_ffn_w2"].rearrange("(n p) d -> p n d", p=P)).then_inc(f.m_w, 16)
        with nc.allow_non_contiguous_dma(reason="biases, one to a partition"):
            sp.dma_start(f.b1[:, :], a["L1_ffn_b1"].rearrange("(n p) -> p n", p=P)).then_inc(f.m_w, 16)
        sp.dma_start(f.vec[:, 0, :], a["L1_ffn_b2"].partition_broadcast(P)).then_inc(f.m_w, 16)

    def prepare(v, f):
        v.wait_ge(f.m_w, 16 * 4)
        return 0

    LINKS = 2

    def finish(v, f, i, u, base):
        t = 2 * i + u
        link = linker(v, f.m_v, base + t * LINKS)
        v.wait_ge(f.m_y, t + 1)
        v.tensor_tensor(f.t1[:, u, :], f.pY[u][:, :], f.vec[:, 0, :], ALU.add).then_inc(f.m_yr, 1)
        v.wait_ge(f.m_yr, t + 1)
        link(v.scalar_tensor_tensor(f.t1[:, u, :], f.t1[:, u, :], s.wcol[:, ds(t, 1)], f.xrow[:, u, 1, :],
                                    ALU.mult, ALU.add))
        if not first(i):
            v.wait_ge(f.m_st[u], 16 * i)
        link(v.tensor_tensor(f.o[:, u, :], f.t1[:, u, :], f.xrow[:, u, 0, :], ALU.add))
        v.sem_inc(f.m_o, 1)
        assert link.count[0] == LINKS

    def store(act, f, i, u, last):
        act.wait_ge(f.m_o, 2 * i + u + 1)
        rows = LAST if last else P
        act.dma_start(out[ds((2 * i + u) * P, rows), :], f.o[0:rows, u, :]).then_inc(f.m_st[u], 16)

    feed_forward(nc, s, "j", ACT.Gelu_apprx_tanh, s.x3_d, load, prepare, finish, False, store)


def project1(nc, s, a):
    with ExitStack() as ctx:
        def sb(name, shape, dt=F32):
            return ctx.enter_context(nc.sbuf_tensor(name, shape, dt))

        w = sb("p_w", [P, KD, 3 * D])
        bias = sb("p_bias", [P, 3 * D])
        xin = sb("p_xin", [P, 2, D])
        st, mv, ve, rs = sb("p_st", [P, 2, 6]), sb("p_mv", [P, 2, 2]), sb("p_ve", [P, 2]), sb("p_rs", [P, 2])
        xn = sb("p_xn", [P, 2, D])
        xT = sb("p_xT", [P, 2, KD, P])
        qvk = sb("p_qvk", [P, 2, 3 * D])
        pT = [ctx.enter_context(nc.psum_tensor(f"p_pT{u}", [P, KD, P], F32)) for u in (0, 1)]
        pQV = [ctx.enter_context(nc.psum_tensor(f"p_pQV{u}", [P, 2 * D], F32)) for u in (0, 1)]
        pKK = [ctx.enter_context(nc.psum_tensor(f"p_pKK{u}", [P, D], F32)) for u in (0, 1)]
        m_w = s.sem("p_w")
        m_x = [s.sem(f"p_x{u}") for u in (0, 1)]
        m_v, m_var, m_rs, m_xn, m_T, m_xT, m_h, m_o = (s.sem("p_" + n) for n in
                                                        ("v", "var", "rs", "xn", "T", "xT", "h", "o"))
        m_st = [s.sem(f"p_st{u}") for u in (0, 1)]
        LINKS = 2

        with nc.Block() as block:
            @block.sync
            def _(sp):
                for j, n in enumerate(("q", "v", "k")):
                    sp.dma_start(w[:, :, j * D:(j + 1) * D],
                                 a["L1_gnn_W" + n].rearrange("(k p) n -> p k n", p=P)).then_inc(m_w, 16)
                    sp.dma_start(bias[:, j * D:(j + 1) * D], a["L1_gnn_b" + n].partition_broadcast(P)).then_inc(m_w, 16)

                def load(i, u):
                    if not first(i):
                        sp.wait_ge(m_xn, 2 * i + u - 1)
                    sp.dma_start(xin[:, u, :], s.x2_d[ds((2 * i + u) * P, P), :]).then_inc(m_x[u], 16)

                pairs(sp, TILES, load)

            @block.gpsimd
            def _(g):
                def root(i, u):
                    g.wait_ge(m_var, 2 * i + u + 1)
                    g.tensor_tensor(rs[:, u:u + 1], ve[:, u:u + 1], s.half[:, :], ALU.pow).then_inc(m_rs, 1)

                pairs(g, TILES, root)

            @block.tensor
            def _(pe):
                def transposes(i, u):
                    pe.wait_ge(m_xn, 2 * i + u + 1)
                    if not first(i):
                        pe.wait_ge(m_xT, 2 * i + u - 1)
                    for k in range(KD):
                        last = pe.transpose(pT[u][:, k, :], xn[:, u, k * P:(k + 1) * P], s.ident[:, :])
                    last.then_inc(m_T, 1)

                def product(i, u):
                    pe.wait_ge(m_xT, 2 * i + u + 1)
                    if not first(i):
                        pe.wait_ge(m_o, 2 * i + u - 1)
                    for k in range(KD):
                        pe.matmul(pQV[u][:, :], xT[:, u, k, :], w[:, k, 0:2 * D], start=k == 0, stop=k == KD - 1)
                    for k in range(KD):
                        last = pe.matmul(pKK[u][:, :], xT[:, u, k, :], w[:, k, 2 * D:], start=k == 0, stop=k == KD - 1)
                    last.then_inc(m_h, 1)

                def step(i, u):
                    transposes(i, u)
                    if before(i, u):
                        product(*before(i, u))

                pe.wait_ge(m_w, 16 * 6)
                pairs(pe, TILES, step)
                product(TILES // 2 - 1, 1)

            @block.scalar
            def _(act):
                def turned(i, u):
                    act.wait_ge(m_T, 2 * i + u + 1)
                    if not first(i):
                        act.wait_ge(m_h, 2 * i + u - 1)
                    act.copy(xT[:, u, :, :], pT[u][:, :, :]).then_inc(m_xT, 1)

                def store(i, u):
                    act.wait_ge(m_o, 2 * i + u + 1)
                    rows = ds((2 * i + u) * P, P)
                    act.dma_start(s.qv_d[rows, :], qvk[:, u, 0:2 * D]).then_inc(m_st[u], 16)
                    act.dma_start(s.k_d[rows, :], qvk[:, u, 2 * D:]).then_inc(m_st[u], 16)

                def step(i, u):
                    turned(i, u)
                    if before(i, u):
                        store(*before(i, u))

                pairs(act, TILES, step)
                store(TILES // 2 - 1, 1)
                for u in (0, 1):
                    act.wait_ge(m_st[u], 32 * (TILES // 2))

            @block.vector
            def _(v):
                def normalise(i, u):
                    t = 2 * i + u
                    link = linker(v, m_v, t * LINKS)
                    v.wait_ge(m_x[u], 16 * (i + 1))
                    norm_stats(v, link, s.passed, xin[:, u, :], st[:, u, :], mv[:, u, :])
                    v.tensor_scalar(ve[:, u:u + 1], mv[:, u, 1:2], EPS, None, ALU.add).then_inc(m_var, 1)
                    if not first(i):
                        v.wait_ge(m_T, t - 1)
                    v.wait_ge(m_rs, t + 1)
                    v.tensor_scalar(xn[:, u, :], xin[:, u, :], mv[:, u, 0:1], rs[:, u:u + 1], ALU.subtract,
                                    ALU.mult).then_inc(m_xn, 1)

                def finish(i, u):
                    v.wait_ge(m_h, 2 * i + u + 1)
                    if not first(i):
                        v.wait_ge(m_st[u], 32 * i)
                    v.tensor_tensor(qvk[:, u, 0:2 * D], pQV[u][:, :], bias[:, 0:2 * D], ALU.add)
                    v.tensor_tensor(qvk[:, u, 2 * D:], pKK[u][:, :], bias[:, 2 * D:], ALU.add).then_inc(m_o, 1)

                def step(i, u):
                    normalise(i, u)
                    if before(i, u):
                        finish(*before(i, u))

                v.wait_ge(m_w, 16 * 6)
                v.memset(s.acc[:, :, 0:D], 0.0)
                pairs(v, TILES, step)
                finish(TILES // 2 - 1, 1)


def edges1(nc, s):
    with ExitStack() as ctx:
        def sb(name, shape, dt=F32):
            return ctx.enter_context(nc.sbuf_tensor(name, shape, dt))

        R = sb("h_R", [P, 2, GROUP, CH, 2 * D])
        idx = sb("h_idx", [P, 4, COLS], I32)
        drow = sb("h_drow", [P, 2, GROUP, EROW], BF16)
        kt = sb("h_kt", [P, 2, GROUP, D])
        OHT = sb("h_OHT", [P, 2, GROUP, EROW])
        OH = sb("h_OH", [P, 2, COLS, P])
        dcol = sb("h_dcol", [P, 2, COLS])
        prod = sb("h_prod", [P, 3, CH, D])
        sc = sb("h_sc", [P, COLS, HEADS])
        smax = sb("h_smax", [P, COLS])
        ex = sb("h_ex", [P, COLS, HEADS])
        ssum = sb("h_ssum", [P, COLS])
        at = sb("h_at", [P, COLS, HEADS])
        pK = [ctx.enter_context(nc.psum_tensor(f"h_pK{n}", [P, CH, D], F32)) for n in range(GROUP)]
        pA = ctx.enter_context(nc.psum_tensor("h_pA", [P, GROUP, 512], F32))
        m_idx = s.sem("h_idx")
        m_g = [s.sem(f"h_g{u}") for u in (0, 1)]
        m_row = [s.sem(f"h_row{u}") for u in (0, 1)]
        m_kt = [s.sem(f"h_kt{u}") for u in (0, 1)]
        m_v, m_rowdist, m_coldist, m_oht, m_dcol, m_oh, m_k, m_pr, m_d, m_ex, m_V, m_agg, m_acc = (
            s.sem("h_" + n) for n in ("v", "rowdist", "coldist", "oht", "dcol", "oh", "k", "pr", "d", "ex", "V", "agg", "acc"))
        LINKS = 5

        with nc.Block() as block:
            @block.gpsimd
            def _(g):
                def gather(i, u):
                    b = 4 * i + u
                    h = u % 2
                    g.tensor_copy(idx[:, u, :], s.src_t[:, ds(b * GROUP, GROUP), :]).then_inc(m_idx, 1)
                    g.wait_ge(m_idx, b + 1)
                    g.sem_inc(s.passed, 1)
                    for n in range(COLS):
                        if n % (2 * CH) == 0 and not (first(i) and u < 2):
                            g.wait_ge(m_agg, (b - 2) * GROUP + n // CH + 2)
                            g.sem_inc(s.passed, 1)
                        g.indirect_dma_start(R[:, h, n // CH, n % CH, :], None, s.qv_d[:, :],
                                             bass.IndirectOffsetOnAxis(ap=idx[:, u, n:n + 1], axis=0)
                                             ).then_inc(m_g[h], 16)

                turns(g, GROUPS, 4, gather)

            @block.sync
            def _(sp):
                def load(i, u):
                    b = 2 * i + u
                    if not first(i):
                        sp.wait_ge(m_oht, b - 1)
                    sp.dma_start(drow[:, u, :, :], s.drow_d[ds(b * GROUP, GROUP), :].partition_broadcast(P)
                                 ).then_inc(m_row[u], 16)
                    tiles = load_tiles(nc, s, ENGINE.SP, b)
                    if not first(i):
                        sp.wait_ge(m_k, (b - 1) * GROUP)
                    for n in range(GROUP):
                        sp.dma_start(kt[:, u, n, :], s.k_d[ds(tiles[n] * P, P), :]).then_inc(m_kt[u], 16)

                turns(sp, GROUPS, 2, load)

            @block.tensor
            def _(pe):
                def expand(i, u):
                    b = 2 * i + u
                    pe.wait_ge(m_kt[u], 16 * GROUP * (i + 1))
                    pe.wait_ge(m_oht, b + 1)
                    for n in range(GROUP):
                        if not (first(i) and u == 0):
                            pe.wait_ge(m_pr, (b - 1) * GROUP + n + 1)
                        for j in range(CH):
                            last = pe.matmul(pK[n][:, j, :], OHT[:, u, n, j * P:(j + 1) * P], kt[:, u, n, :],
                                             start=True, stop=True)
                        last.then_inc(m_k, 1)

                def collect(i, u):
                    b = 2 * i + u
                    pe.wait_ge(m_oh, b + 1)
                    for n in range(GROUP):
                        pe.wait_ge(m_V, b * GROUP + n + 1)
                        if before(i, u):
                            pe.wait_ge(m_acc, (b - 1) * GROUP + n + 1)
                        for j in range(CH):
                            last = pe.matmul(pA[:, n, 0:D], OH[:, u, n * CH + j, :], R[:, u, n, j, D:], start=j == 0,
                                             stop=j == CH - 1)
                        last.then_inc(m_agg, 1)

                def step(i, u, left=None):
                    if before(i, u):
                        collect(*before(i, u))
                    if left != 0:
                        expand(*after(i, u, 2))

                expand(0, 0)
                turns(pe, GROUPS, 2, step, peel_last=True)
                collect(GROUPS // 2 - 1, 1)

            @block.scalar
            def _(act):
                def row_distances(i, u):
                    act.wait_ge(m_row[u], 16 * (i + 1))
                    if not first(i):
                        act.wait_ge(m_k, (2 * i + u - 1) * GROUP)
                    act.activation(OHT[:, u, :, :], drow[:, u, :, :], ACT.Abs, bias=s.part[:, 0:1], scale=-1.0
                                   ).then_inc(m_rowdist, 1)

                def select_rows(i, u):
                    act.wait_ge(m_rowdist, 2 * i + u + 1)
                    act.activation(OHT[:, u, :, :], OHT[:, u, :, :], ACT.Relu, bias=s.ones[:, 0:1], scale=-1.0
                                   ).then_inc(m_oht, 1)

                def column_distances(i, u):
                    act.wait_ge(m_dcol, 2 * i + u + 1)
                    if not first(i):
                        act.wait_ge(m_agg, (2 * i + u - 1) * GROUP)
                    for n in range(COLS):
                        last = act.activation(OH[:, u, n, :], s.iota[:, :], ACT.Abs, bias=dcol[:, u, n:n + 1],
                                              scale=-1.0)
                    last.then_inc(m_coldist, 1)

                def select_columns(i, u):
                    act.wait_ge(m_coldist, 2 * i + u + 1)
                    act.activation(OH[:, u, :, :], OH[:, u, :, :], ACT.Relu, bias=s.ones[:, 0:1], scale=-1.0
                                   ).then_inc(m_oh, 1)

                def step(i, u, left=None):
                    b = 2 * i + u
                    act.copy(dcol[:, u, :], s.dst_t[:, ds(b * GROUP, GROUP), :]).then_inc(m_dcol, 1)
                    if left is None:
                        row_distances(*after(i, u, 2, 2))
                    column_distances(i, u)
                    if left is None:
                        select_rows(*after(i, u, 2, 2))
                    select_columns(i, u)
                    act.wait_ge(m_d, b + 1)
                    act.activation(ex[:, :, :], sc[:, :, :], ACT.Exp, scale=float(HD) ** -0.5).then_inc(m_ex, 1)

                for u in (0, 1):
                    row_distances(0, u)
                    select_rows(0, u)
                turns(act, GROUPS, 2, step, peel_last=True)

            @block.vector
            def _(v):
                def product(i, u, n):
                    v.wait_ge(m_k, (2 * i + u) * GROUP + n + 1)
                    if n >= 3:
                        v.wait_ge(m_pr, (2 * i + u) * GROUP + n)
                    v.tensor_tensor(prod[:, n % 3, :, :], pK[n][:, :, :], R[:, u, n, :, 0:D], ALU.mult
                                    ).then_inc(m_pr, 1)

                def score(i, u, n):
                    v.wait_ge(m_pr, (2 * i + u) * GROUP + n + 1)
                    return v.tensor_reduce(sc[:, n * CH:(n + 1) * CH, :],
                                           prod[:, n % 3, :, :].rearrange("p c (h d) -> p (c h) d", d=HD), X, ALU.add)

                def weighted(i, u, at_made):
                    v.wait_ge(m_v, at_made)
                    for n in range(GROUP):
                        rv = R[:, u, n, :, D:].rearrange("p c (h d) -> p c h d", d=HD)
                        v.tensor_tensor(rv, rv, at[:, n * CH:(n + 1) * CH, :].unsqueeze(3)
                                        .to_broadcast([P, CH, HEADS, HD]), ALU.mult).then_inc(m_V, 1)

                def add(i, u, tiles, n):
                    count = (2 * i + u) * GROUP + n
                    v.wait_ge(m_agg, count + 1)
                    if n or before(i, u):
                        v.wait_ge(m_acc, count)
                    acc = s.acc[:, ds(tiles[n], 1), 0:D]
                    v.tensor_tensor(acc, acc, pA[:, n:n + 1, 0:D], ALU.add).then_inc(m_acc, 1)

                def step(i, u):
                    b = 2 * i + u
                    past = before(i, u)
                    if past:
                        weighted(*past, b * LINKS)
                        tiles = load_tiles(nc, s, ENGINE.DVE, b - 1)
                    v.wait_ge(m_g[u], 16 * COLS * (i + 1))
                    product(i, u, 0)
                    for n in range(1, GROUP):
                        product(i, u, n)
                        score(i, u, n - 1)
                    if past:
                        add(*past, tiles, 0)
                    score(i, u, GROUP - 1).then_inc(m_v, 1)
                    if past:
                        add(*past, tiles, 1)
                    v.wait_ge(m_v, b * LINKS + 1)
                    v.tensor_reduce(smax[:, :], sc[:, :, :], X, ALU.max).then_inc(m_v, 1)
                    if past:
                        add(*past, tiles, 2)
                    v.wait_ge(m_v, b * LINKS + 2)
                    v.tensor_tensor(sc[:, :, :], sc[:, :, :], smax[:, :].unsqueeze(2).to_broadcast([P, COLS, HEADS]),
                                    ALU.subtract).then_inc(m_d, 1)
                    if past:
                        add(*past, tiles, 3)
                    v.wait_ge(m_ex, b + 1)
                    v.tensor_reduce(ssum[:, :], ex[:, :, :], X, ALU.add).then_inc(m_v, 1)
                    v.wait_ge(m_v, b * LINKS + 3)
                    v.reciprocal(ssum[:, :], ssum[:, :]).then_inc(m_v, 1)
                    v.wait_ge(m_v, b * LINKS + 4)
                    v.tensor_tensor(at[:, :, :], ex[:, :, :], ssum[:, :].unsqueeze(2).to_broadcast([P, COLS, HEADS]),
                                    ALU.mult).then_inc(m_v, 1)

                turns(v, GROUPS, 2, step)
                end = (GROUPS // 2 - 1, 1)
                weighted(*end, GROUPS * LINKS)
                tiles = load_tiles(nc, s, ENGINE.DVE, GROUPS - 1)
                for n in range(GROUP):
                    add(*end, tiles, n)


def finish1(nc, s, a):
    with ExitStack() as ctx:
        def sb(name, shape, dt=F32):
            return ctx.enter_context(nc.sbuf_tensor(name, shape, dt))

        w = sb("o_w", [P, KD, D])
        rows = sb("o_rows", [P, 2, D])
        br = sb("o_br", [P, 1])
        g = sb("o_g", [P, 2, D])
        gT = sb("o_gT", [P, 2, KD, P])
        xin = sb("o_xin", [P, 2, D])
        o = sb("o_o", [P, 2, 2, D])
        junk = sb("o_junk", [P, D])
        dot = sb("o_dot", [P, 2])
        st, mv, ve, rs = sb("o_st", [P, 2, 6]), sb("o_mv", [P, 2, 2]), sb("o_ve", [P, 2]), sb("o_rs", [P, 2])
        pT = [ctx.enter_context(nc.psum_tensor(f"o_pT{u}", [P, KD, P], F32)) for u in (0, 1)]
        pO = [ctx.enter_context(nc.psum_tensor(f"o_pO{u}", [P, D], F32)) for u in (0, 1)]
        m_w = s.sem("o_w")
        m_x = [s.sem(f"o_x{u}") for u in (0, 1)]
        m_st = [s.sem(f"o_st{u}") for u in (0, 1)]
        m_v, m_g, m_T, m_gT, m_p, m_pr, m_var, m_rs, m_o = (
            s.sem("o_" + n) for n in ("v", "g", "T", "gT", "p", "pr", "var", "rs", "out"))
        LINKS = 5

        with nc.Block() as block:
            @block.sync
            def _(sp):
                sp.dma_start(w[:, :, :], a["L1_gnn_Wo"].rearrange("(k p) n -> p k n", p=P)).then_inc(m_w, 16)
                sp.dma_start(rows[:, 0, :], a["L1_gnn_bo"].partition_broadcast(P)).then_inc(m_w, 16)
                sp.dma_start(rows[:, 1, :], a["L1_ffn_wr"].rearrange("d o -> (d o)").partition_broadcast(P)).then_inc(m_w, 16)
                sp.dma_start(br[:, :], a["L1_ffn_br"].partition_broadcast(P)).then_inc(m_w, 16)

                def load(i, u):
                    if not first(i):
                        sp.wait_ge(m_var, 2 * i + u - 1)
                    sp.dma_start(xin[:, u, :], s.x2_d[ds((2 * i + u) * P, P), :]).then_inc(m_x[u], 16)

                pairs(sp, TILES, load)

            @block.gpsimd
            def _(gp):
                def root(i, u):
                    gp.wait_ge(m_var, 2 * i + u + 1)
                    gp.tensor_tensor(rs[:, u:u + 1], ve[:, u:u + 1], s.half[:, :], ALU.pow).then_inc(m_rs, 1)

                pairs(gp, TILES, root)

            @block.tensor
            def _(pe):
                def transposes(i, u):
                    pe.wait_ge(m_g, 2 * i + u + 1)
                    if not first(i):
                        pe.wait_ge(m_gT, 2 * i + u - 1)
                    for k in range(KD):
                        last = pe.transpose(pT[u][:, k, :], g[:, u, k * P:(k + 1) * P], s.ident[:, :])
                    last.then_inc(m_T, 1)

                def product(i, u):
                    pe.wait_ge(m_gT, 2 * i + u + 1)
                    if not first(i):
                        pe.wait_ge(m_pr, 2 * i + u - 1)
                    for k in range(KD):
                        last = pe.matmul(pO[u][:, :], gT[:, u, k, :], w[:, k, :], start=k == 0, stop=k == KD - 1)
                    last.then_inc(m_p, 1)

                def step(i, u):
                    transposes(i, u)
                    if before(i, u):
                        product(*before(i, u))

                pe.wait_ge(m_w, 16 * 4)
                pairs(pe, TILES, step)
                product(TILES // 2 - 1, 1)

            @block.scalar
            def _(act):
                def stage(i, u):
                    if not first(i):
                        act.wait_ge(m_T, 2 * i + u - 1)
                    act.copy(g[:, u:u + 1, :], s.acc[:, ds(2 * i + u, 1), 0:D]).then_inc(m_g, 1)

                def turned(i, u):
                    act.wait_ge(m_T, 2 * i + u + 1)
                    if not first(i):
                        act.wait_ge(m_p, 2 * i + u - 1)
                    act.copy(gT[:, u, :, :], pT[u][:, :, :]).then_inc(m_gT, 1)

                def store(i, u):
                    act.wait_ge(m_o, 2 * i + u + 1)
                    act.dma_start(s.x3_d[ds((2 * i + u) * P, P), :], o[:, u, :, :]).then_inc(m_st[u], 16)

                def step(i, u):
                    stage(i, u)
                    turned(i, u)
                    if before(i, u) and before(*before(i, u)):
                        store(*before(*before(i, u)))

                pairs(act, TILES, step)
                store(TILES // 2 - 1, 0)
                store(TILES // 2 - 1, 1)
                for u in (0, 1):
                    act.wait_ge(m_st[u], 16 * (TILES // 2))

            @block.vector
            def _(v):
                v.wait_ge(m_w, 16 * 4)

                def finish(i, u):
                    t = 2 * i + u
                    link = linker(v, m_v, t * LINKS)
                    v.wait_ge(m_p, t + 1)
                    if not first(i):
                        v.wait_ge(m_st[u], 16 * i)
                    v.tensor_tensor(o[:, u, 0, :], pO[u][:, :], rows[:, 0, :], ALU.add).then_inc(m_pr, 1)
                    v.wait_ge(m_pr, t + 1)
                    v.wait_ge(m_x[u], 16 * (i + 1))
                    link(v.tensor_tensor(o[:, u, 0, :], o[:, u, 0, :], xin[:, u, :], ALU.add))
                    norm_stats(v, link, s.passed, o[:, u, 0, :], st[:, u, :], mv[:, u, :])
                    v.tensor_scalar(ve[:, u:u + 1], mv[:, u, 1:2], EPS, None, ALU.add).then_inc(m_var, 1)
                    v.wait_ge(m_rs, t + 1)
                    link(v.tensor_scalar(o[:, u, 1, :], o[:, u, 0, :], mv[:, u, 0:1], rs[:, u:u + 1], ALU.subtract,
                                         ALU.mult))
                    v.sem_inc(m_o, 1)
                    link(v.tensor_tensor_reduce(junk[:, :], o[:, u, 1, :], rows[:, 1, :], 1.0, 0.0, ALU.mult,
                                                ALU.add, dot[:, u:u + 1]))
                    v.tensor_scalar(s.wcol[:, ds(t, 1)], dot[:, u:u + 1], br[:, 0:1], None, ALU.add)
                    assert link.count[0] == LINKS

                pairs(v, TILES, finish)


def select1(nc, s):
    with ExitStack() as ctx:
        def sb(name, shape, dt=F32):
            return ctx.enter_context(nc.sbuf_tensor(name, shape, dt))

        bits = sb("s_bits", [P, TILES], I32)
        hi_i = sb("s_hi_i", [P, TILES], I32)
        lo_i = sb("s_lo_i", [P, TILES], I32)
        hi, lo, neg, tmp = sb("s_hi", [P, TILES]), sb("s_lo", [P, TILES]), sb("s_neg", [P, TILES]), sb("s_tmp", [P, TILES])
        real, chosen = sb("s_real", [P, TILES]), sb("s_chosen", [P, TILES])
        need, low, cand, bit, cnt, got = (sb("s_" + n, [P, 1]) for n in ("need", "low", "cand", "bit", "cnt", "got"))
        pc = ctx.enter_context(nc.psum_tensor("s_pc", [P, 1], F32))
        m_v, m_cnt, m_sum = s.sem("s_v"), s.sem("s_cnt"), s.sem("s_sum")
        BITS = (16, 16, 14)
        sums = sum(BITS) + 2

        with nc.Block() as block:
            @block.tensor
            def _(pe):
                with pe.Fori(0, sums) as i:
                    pe.wait_ge(m_cnt, i + 1)
                    pe.matmul(pc[:, :], s.ones[:, :], cnt[:, :], start=True, stop=True).then_inc(m_sum, 1)

            @block.vector
            def _(v):
                link = linker(v, m_v, 0)
                link(v.tensor_copy(bits[:, :], s.wcol[:, :].bitcast(I32)))
                link(v.tensor_scalar(hi_i[:, :], bits[:, :], 16, 0xFFFF, ALU.logical_shift_right, ALU.bitwise_and))
                link(v.tensor_scalar(lo_i[:, :], bits[:, :], 0xFFFF, None, ALU.bitwise_and))
                link(v.tensor_copy(hi[:, :], hi_i[:, :]))
                link(v.tensor_copy(lo[:, :], lo_i[:, :]))
                link(v.tensor_scalar(neg[:, :], hi[:, :], 32768.0, None, ALU.is_ge))
                link(v.tensor_scalar(tmp[:, :], lo[:, :], -2.0, 65535.0, ALU.mult, ALU.add))
                link(v.tensor_tensor(tmp[:, :], tmp[:, :], neg[:, :], ALU.mult))
                link(v.tensor_tensor(lo[:, :], lo[:, :], tmp[:, :], ALU.add))
                link(v.tensor_scalar(tmp[:, :], hi[:, :], -2.0, 32767.0, ALU.mult, ALU.add))
                link(v.tensor_tensor(tmp[:, :], tmp[:, :], neg[:, :], ALU.mult))
                link(v.tensor_scalar(hi[:, :], hi[:, :], 32768.0, None, ALU.add))
                link(v.tensor_tensor(hi[:, :], hi[:, :], tmp[:, :], ALU.add))
                link(v.tensor_scalar(real[:, :], s.node[:, :], float(N), None, ALU.is_lt))

                def masked(digit, mask):
                    link(v.tensor_scalar(digit, digit, 1.0, None, ALU.add))
                    link(v.tensor_tensor(digit, digit, mask, ALU.mult))
                    link(v.tensor_scalar(digit, digit, -1.0, None, ALU.add))

                masked(hi[:, :], real[:, :])
                link(v.memset(need[:, :], float(TOPK)))
                link(v.memset(chosen[:, :], 0.0))
                at, summed = link.count[0], 0

                def search(digit, nbits):
                    v.memset(low[:, :], 0.0).then_inc(m_v, 1)
                    v.memset(bit[:, :], float(2 ** (nbits - 1))).then_inc(m_v, 1)
                    v.wait_ge(m_v, at + 2)
                    with v.Fori(0, nbits) as i:
                        step = linker(v, m_v, i * 5 + (at + 2))
                        step(v.tensor_tensor(cand[:, :], low[:, :], bit[:, :], ALU.add))
                        step(v.tensor_scalar(tmp[:, :], digit, cand[:, 0:1], None, ALU.is_ge))
                        v.tensor_reduce(cnt[:, :], tmp[:, :], X, ALU.add).then_inc(m_cnt, 1)
                        v.wait_ge(m_sum, i + (summed + 1))
                        step(v.tensor_tensor(got[:, :], pc[:, :], need[:, :], ALU.is_ge))
                        step(v.scalar_tensor_tensor(low[:, :], got[:, :], bit[:, 0:1], low[:, :], ALU.mult, ALU.add))
                        step(v.tensor_scalar(bit[:, :], bit[:, :], 0.5, None, ALU.mult))
                    return at + 2 + 5 * nbits, summed + nbits

                def settle(digit, following):
                    step = linker(v, m_v, at)
                    step(v.tensor_scalar(tmp[:, :], digit, low[:, 0:1], None, ALU.is_gt))
                    step(v.tensor_tensor(chosen[:, :], chosen[:, :], tmp[:, :], ALU.add))
                    v.tensor_reduce(cnt[:, :], tmp[:, :], X, ALU.add).then_inc(m_cnt, 1)
                    v.wait_ge(m_sum, summed + 1)
                    step(v.tensor_tensor(need[:, :], need[:, :], pc[:, :], ALU.subtract))
                    step(v.tensor_scalar(tmp[:, :], digit, low[:, 0:1], None, ALU.is_equal))
                    step(v.tensor_scalar(following, following, 1.0, None, ALU.add))
                    step(v.tensor_tensor(following, following, tmp[:, :], ALU.mult))
                    step(v.tensor_scalar(following, following, -1.0, None, ALU.add))
                    return at + step.count[0], summed + 1

                at, summed = search(hi[:, :], BITS[0])
                at, summed = settle(hi[:, :], lo[:, :])
                at, summed = search(lo[:, :], BITS[1])
                v.tensor_scalar(neg[:, :], s.node[:, :], -1.0, float(2 ** BITS[2] - 1), ALU.mult, ALU.add).then_inc(m_v, 1)
                at += 1
                v.wait_ge(m_v, at)
                at, summed = settle(lo[:, :], neg[:, :])
                at, summed = search(neg[:, :], BITS[2])
                step = linker(v, m_v, at)
                step(v.tensor_scalar(tmp[:, :], neg[:, :], low[:, 0:1], None, ALU.is_ge))
                step(v.tensor_tensor(chosen[:, :], chosen[:, :], tmp[:, :], ALU.add))
                step(v.tensor_tensor(s.wcol[:, :], s.wcol[:, :], chosen[:, :], ALU.mult))


def build(nc, x, src2, dst2, a, out):
    with ExitStack() as ctx:
        s = Shared()

        def sb(name, shape, dt=F32):
            return ctx.enter_context(nc.sbuf_tensor(name, shape, dt))

        s.sem = lambda name: ctx.enter_context(nc.semaphore(name))
        s.passed = s.sem("passed")
        s.acc = sb("acc", [P, TILES, ACOLS])
        s.iota = sb("iota", [P, P])
        s.iota_b = sb("iota_b", [P, P], BF16)
        s.part_i = sb("part_i", [P, 1], I32)
        s.part = sb("part", [P, 1])
        s.node_i = sb("node_i", [P, TILES], I32)
        s.node = sb("node", [P, TILES])
        s.ones = sb("ones", [P, P])
        s.half = sb("half", [P, 1])
        s.ident = sb("ident", [P, P])
        s.tile_i = sb("tile_i", [1, IPAD], I32)
        s.src_t = sb("src_t", [P, IPAD, CH], I32)
        s.dst_t = sb("dst_t", [P, IPAD, CH])
        s.xsum = sb("xsum", [P, D])
        s.expert_i = sb("expert_i", [1, 2], I32)
        s.wexp = sb("wexp", [P, 2])
        s.wcol = sb("wcol", [P, TILES])
        s.drow_d = nc.dram_tensor("drow_d", [IPAD, EROW], BF16).ap()
        s.seg_d = nc.dram_tensor("seg_d", [IPAD, EROW + 1], F32).ap()
        s.hq_d = nc.dram_tensor("hq_d", [NPAD, D + 1], F32).ap()
        s.qv_d = nc.dram_tensor("qv_d", [NPAD, 2 * D], F32).ap()
        s.k_d = nc.dram_tensor("k_d", [NPAD, D], F32).ap()
        s.x1_d = nc.dram_tensor("x1_d", [NPAD, 2 * D], F32).ap()
        s.x2_d = nc.dram_tensor("x2_d", [NPAD, D], F32).ap()
        s.x3_d = nc.dram_tensor("x3_d", [NPAD, 2 * D], F32).ap()
        with ExitStack() as layer0:
            def sb0(name, shape, dt=F32):
                return layer0.enter_context(nc.sbuf_tensor(name, shape, dt))

            s.iota_i = sb0("iota_i", [P, IPAD], I32)
            s.item_no = sb0("item_no", [P, IPAD])
            s.fresh = sb0("fresh", [P, IPAD])
            s.kf = sb0("kf", [P, TILES])
            s.k0 = sb0("k0", [P, TILES, KPARTS], BF16)
            constants(nc, s)
            item_tables(nc, s, src2, dst2)
            project0(nc, s, x, a["L0_gnn_Wv"], a["L0_gnn_bv"], a["L0_gnn_wq"], a["L0_gnn_bq"], a["L0_gnn_wk"],
                     a["L0_gnn_bk"])
            edges0(nc, s)
        finish0(nc, s, x)
        route0(nc, s, a)
        feed_forward0(nc, s, a)
        project1(nc, s, a)
        edges1(nc, s)
        finish1(nc, s, a)
        select1(nc, s)
        feed_forward1(nc, s, a, out)


_WEIGHTS = ['L0_gnn_Wv', 'L0_gnn_bv', 'L0_gnn_wq', 'L0_gnn_bq', 'L0_gnn_wk', 'L0_gnn_bk', 'L0_ffn_Wr', 'L0_ffn_br',
            'L0_ffn_W1', 'L0_ffn_b1', 'L0_ffn_W2', 'L0_ffn_b2', 'L0_ffn_gamma', 'L0_ffn_beta', 'L1_gnn_Wq', 'L1_gnn_bq',
            'L1_gnn_Wk', 'L1_gnn_bk', 'L1_gnn_Wv', 'L1_gnn_bv', 'L1_gnn_Wo', 'L1_gnn_bo', 'L1_ffn_wr', 'L1_ffn_br',
            'L1_ffn_w1', 'L1_ffn_b1', 'L1_ffn_w2', 'L1_ffn_b2']


def kernel(**inputs):
    import numpy as np
    import concourse.bacc as bacc
    from concourse.bass_utils import run_bass_kernel_spmd

    nc = bacc.Bacc("TRN2", target_bir_lowering=False, num_devices=1)
    arrays, args = {}, {}
    laid = {"x": np.pad(np.asarray(inputs["x"]), ((0, NPAD - N), (0, 0)))}
    laid["src2"] = np.pad(np.asarray(inputs["src"]), (0, EROWS * EROW - EDGES)).reshape(EROWS, EROW)
    laid["dst2"] = np.pad(np.asarray(inputs["dst"]), (0, EROWS * EROW - EDGES),
                          constant_values=2 * NPAD).reshape(EROWS, EROW)
    for name in _WEIGHTS:
        w = np.asarray(inputs[name])
        if name in ("L1_gnn_Wq", "L1_gnn_Wk", "L1_gnn_Wv", "L1_gnn_Wo"):
            w = w.T
        laid[name] = w.reshape(1) if w.ndim == 0 else w
    for name, value in laid.items():
        value = np.ascontiguousarray(value)
        arrays["in_" + name] = value
        args[name] = nc.dram_tensor("in_" + name, value.shape, mybir.dt.from_np(value.dtype), kind="ExternalInput").ap()
    out = nc.dram_tensor("out", (N, D), F32, kind="ExternalOutput").ap()
    build(nc, args.pop("x"), args.pop("src2"), args.pop("dst2"), args, out)
    return run_bass_kernel_spmd(nc, [arrays], core_ids=[0]).results[0]["out"]
```

```python
from contextlib import ExitStack

import concourse.bass as bass
from concourse import mybir

F32 = mybir.dt.float32
BF16 = mybir.dt.bfloat16
I32 = mybir.dt.int32
ALU = mybir.AluOpType
ACT = mybir.ActivationFunctionType
ENGINE = mybir.EngineType
X = mybir.AxisListType.X

P = 128
N = 12500
D = 256
TILES = (N + P - 1) // P
NPAD = TILES * P
LAST = N - (TILES - 1) * P
EDGES = 212500
EROW = 256
EROWS = (EDGES + EROW - 1) // EROW
ITEMS = EROWS + TILES - 1
GROUP = 4
GROUPS = ITEMS // GROUP
IBLOCKS = (ITEMS + P - 1) // P
IPAD = IBLOCKS * P
CH = EROW // P
COLS = GROUP * CH
RING = 4
UNROLL = 4
DEPTH = 4
LAST_TILE = (TILES // DEPTH, TILES % DEPTH - 1)
LAST_TURN = (GROUPS // RING - 1, RING - 1)
KPARTS = 3
HEADS = 8
HD = D // HEADS
EXPERTS = 8
HID = 1024
HB = HID // P
KD = D // P
EPS = 1e-5
BIG = 1e30
TOPK = N // 2 - 1
CAPACITY = float(-(-N * 5 // (4 * EXPERTS)))
QCOL, ONECOL, SCOL, HCOLS = D, D + 1, D + 2, D + 3
ACOLS = D + 1
assert ITEMS % (RING * GROUP) == 0 and TILES % DEPTH >= 1


def ds(start, size):
    return bass.ds(start, size)


def turns(eng, n, width, body, peel_last=False):
    def run(i, peeled):
        for u in range(width):
            if peeled:
                body(i, u, left=width - 1 - u)
            else:
                body(i, u)

    run(0, False)
    with eng.Fori(1, n // width - int(peel_last)) as i:
        run(i, False)
    if peel_last:
        run(n // width - 1, True)
    for u in range(n % width):
        body(n // width, u)


def before(i, u, width=2):
    if u:
        return i, u - 1
    return None if isinstance(i, int) and i == 0 else (i - 1, width - 1)


def back(i, u, steps):
    if u >= steps:
        return i, u - steps
    return None if first(i) else (i - 1, u - steps + DEPTH)


def tiles_pipelined(v, run):
    turns(v, TILES, DEPTH, lambda i, u: run((i, u), back(i, u, 1), back(i, u, 3)))
    i, u = TILES // DEPTH, TILES % DEPTH
    run(None, back(i, u, 1), back(i, u, 3))
    run(None, None, back(i, u, 2))
    run(None, None, back(i, u, 1))


def wait_stores(eng, sems):
    for u in range(DEPTH):
        eng.wait_ge(sems[u], 16 * ((TILES - u + DEPTH - 1) // DEPTH))


def after(i, u, width, steps=1):
    return (i, u + steps) if u + steps < width else (i + 1, u + steps - width)


def load_tiles(nc, s, engine, b, groups=1):
    return nc.values_load_multi_w_load_instructions(s.tile_i[0:1, ds(b * GROUP, groups * GROUP)], engines=(engine,),
                                                    min_val=0, max_val=TILES - 1)[1]


def first(i):
    return isinstance(i, int) and i == 0


def linker(eng, sem, base):
    count = [0]

    def link(ins):
        count[0] += 1
        ins.then_inc(sem, 1)
        eng.wait_ge(sem, base + count[0])

    link.count = count
    return link


class Shared:
    pass


def constants(nc, s):
    sem_iota, sem_c = s.sem("c_iota"), s.sem("c_made")
    with nc.Block() as block:
        @block.gpsimd
        def _(g):
            g.iota(s.iota_i[:, :], pattern=[[1, IPAD]], base=0, channel_multiplier=0).then_inc(sem_iota, 1)
            g.iota(s.part_i[:, :], pattern=[[0, 1]], base=0, channel_multiplier=1).then_inc(sem_iota, 1)
            g.iota(s.node_i[:, :], pattern=[[P, TILES]], base=0, channel_multiplier=1).then_inc(sem_iota, 1)

        @block.vector
        def _(v):
            link = linker(v, sem_c, 0)
            v.memset(s.ones[:, :], 1.0)
            v.memset(s.half[:, :], -0.5)
            v.memset(s.acc[:, :, :], 0.0)
            v.wait_ge(sem_iota, 3)
            v.tensor_copy(s.item_no[:, :], s.iota_i[:, :])
            v.tensor_copy(s.iota[:, :], s.iota_i[:, 0:P])
            v.tensor_copy(s.iota_b[:, :], s.iota_i[:, 0:P])
            v.tensor_copy(s.node[:, :], s.node_i[:, :])
            link(v.tensor_copy(s.part[:, :], s.part_i[:, :]))
            link(v.tensor_scalar(s.ident[:, :], s.iota[:, :], s.part[:, 0:1], None, ALU.is_equal))


def item_tables(nc, s, src2, dst2):
    with ExitStack() as ctx:
        def sb(name, shape, dt):
            return ctx.enter_context(nc.sbuf_tensor(name, shape, dt))

        def ps(name, shape, dt=F32):
            return ctx.enter_context(nc.psum_tensor(name, shape, dt))

        first_f = sb("t_first_f", [1, EROWS], F32)
        below = sb("t_below", [P, EROWS], F32)
        cnt = sb("t_cnt", [P, 1], F32)
        begins = sb("t_begins", [P, 1], F32)
        bound = sb("t_bound", [P, 1], F32)
        valid = sb("t_valid", [P, P], BF16)
        vcol = sb("t_vcol", [P, 2], F32)
        step = sb("t_step", [P, IPAD], BF16)
        tcol = sb("t_tcol", [P, IBLOCKS], F32)
        tbase = sb("t_tbase", [P, IBLOCKS], F32)
        grow = sb("t_grow", [P, IBLOCKS], F32)
        growi = sb("t_growi", [P, IBLOCKS], I32)
        srcb = sb("t_srcb", [P, 2, EROW], I32)
        dstb = sb("t_dstb", [P, 2, EROW], I32)
        srcf = sb("t_srcf", [P, 2, EROW], F32)
        dloc = sb("t_dloc", [P, 2, EROW], F32)
        dlocb = sb("t_dlocb", [P, 2, EROW], BF16)
        seg = sb("t_seg", [P, 2, EROW + 1], F32)
        trep = sb("t_trep", [P, IPAD], F32)
        bc = [ps(f"t_bc{i}", [P, 512]) for i in range(2)]
        pt = [ps(f"t_pt{i}", [P, 512]) for i in range(2)]
        pc = ps("t_pc", [P, 512])
        px = [ps(f"t_px{i}", [P, 2, CH, P]) for i in range(2)]
        m_ff, m_bc, m_v = s.sem("t_ff"), s.sem("t_bc"), s.sem("t_v")
        m_step, m_t, m_idx = s.sem("t_step"), s.sem("t_t"), s.sem("t_idx")
        m_rows = [s.sem(f"t_rows{u}") for u in (0, 1)]
        m_loc, m_x, m_done = s.sem("t_loc"), s.sem("t_x"), s.sem("t_done")
        m_st = [s.sem(f"t_st{u}") for u in (0, 1)]
        half = EROWS // 2

        with nc.Block() as block:
            @block.sync
            def _(sp):
                for b in range(IBLOCKS):
                    u = b % 2
                    sp.wait_ge(m_loc, b + 1)
                    sp.dma_start(s.drow_d[b * P:(b + 1) * P, :], dlocb[:, u, :]).then_inc(m_st[u], 16)
                    sp.dma_start(s.seg_d[b * P:(b + 1) * P, :], seg[:, u, :]).then_inc(m_st[u], 16)
                for u in (0, 1):
                    sp.wait_ge(m_st[u], 32 * (IBLOCKS // 2))

            @block.tensor
            def _(pe):
                pe.wait_ge(m_ff, 1)
                pe.matmul(bc[0][:, 0:half], s.ones[0:1, :], first_f[:, 0:half], start=True, stop=True)
                pe.matmul(bc[1][:, 0:EROWS - half], s.ones[0:1, :], first_f[:, half:], start=True,
                          stop=True).then_inc(m_bc, 1)
                pe.wait_ge(m_step, 1)
                for k in range(2):
                    pe.matmul(pt[k][:, :], valid[:, :], step[:, k * 512:(k + 1) * 512], start=True, stop=True)
                for b in range(IBLOCKS):
                    last = pe.matmul(pc[:, b:b + 1], step[:, b * P:(b + 1) * P], valid[:, 0:1], start=True, stop=True)
                last.then_inc(m_t, 1)
                for b in range(IBLOCKS):
                    u = b % 2
                    pe.wait_ge(m_loc, b + 1)
                    if b >= 2:
                        pe.wait_ge(m_done, b - 1)
                    for c in range(CH):
                        pe.transpose(px[u][:, 0, c, :], srcf[:, u, c * P:(c + 1) * P], s.ident[:, :])
                        last = pe.transpose(px[u][:, 1, c, :], dloc[:, u, c * P:(c + 1) * P], s.ident[:, :])
                    last.then_inc(m_x, 1)

            @block.gpsimd
            def _(g):
                g.wait_ge(m_idx, 1)
                for b in range(IBLOCKS):
                    u = b % 2
                    if b >= 2:
                        g.wait_ge(m_loc, b - 1)
                    for buf, table in ((srcb, src2), (dstb, dst2)):
                        g.indirect_dma_start(buf[:, u, :], None, table,
                                             bass.IndirectOffsetOnAxis(ap=growi[:, b:b + 1], axis=0)
                                             ).then_inc(m_rows[u], 16)

            @block.vector
            def _(v):
                link = linker(v, m_v, 0)
                v.wait_ge(s.m_first, 16)
                v.tensor_copy(first_f[:, :], s.first_i[:, :]).then_inc(m_ff, 1)
                link(v.tensor_scalar(bound[:, :], s.part[:, :], float(P), None, ALU.mult))
                link(v.tensor_scalar(vcol[:, 0:1], s.part[:, :], 1.0, None, ALU.is_ge))
                link(v.tensor_scalar(vcol[:, 1:2], s.part[:, :], float(TILES), None, ALU.is_lt))
                link(v.tensor_tensor(vcol[:, 0:1], vcol[:, 0:1], vcol[:, 1:2], ALU.mult))
                link(v.tensor_scalar(valid[:, :], s.ones[:, :], vcol[:, 0:1], None, ALU.mult))
                v.wait_ge(m_bc, 1)
                link(v.tensor_scalar(below[:, 0:half], bc[0][:, 0:half], bound[:, 0:1], None, ALU.is_lt))
                link(v.tensor_scalar(below[:, half:], bc[1][:, 0:EROWS - half], bound[:, 0:1], None, ALU.is_lt))
                link(v.tensor_reduce(cnt[:, :], below[:, 1:EROWS], X, ALU.add))
                link(v.tensor_tensor(begins[:, :], cnt[:, :], s.part[:, :], ALU.add))
                link(v.tensor_scalar(step[:, :], s.item_no[:, :], begins[:, 0:1], None, ALU.is_ge))
                v.sem_inc(m_step, 1)
                v.wait_ge(m_t, 1)
                for k in range(2):
                    v.tensor_copy(s.tile_i[:, k * 512:(k + 1) * 512], pt[k][0:1, :])
                    link(v.tensor_copy(trep[:, k * 512:(k + 1) * 512], pt[k][:, :]))
                link(v.memset(s.fresh[:, 0:1], 1.0))
                link(v.tensor_tensor(s.fresh[:, 1:IPAD], trep[:, 1:IPAD], trep[:, 0:IPAD - 1], ALU.not_equal))
                link(v.tensor_scalar(s.fresh[:, :], s.fresh[:, :], -BIG, None, ALU.mult))
                link(v.tensor_copy(tcol[:, :], pc[:, 0:IBLOCKS]))
                link(v.tensor_scalar(tbase[:, :], tcol[:, :], float(P), None, ALU.mult))
                link(v.tensor_scalar(grow[:, :], s.item_no[:, 0:IPAD:P], s.part[:, 0:1], None, ALU.add))
                link(v.tensor_tensor(grow[:, :], grow[:, :], tcol[:, :], ALU.subtract))
                link(v.tensor_scalar(grow[:, :], grow[:, :], float(EROWS - 1), None, ALU.min))
                v.tensor_copy(growi[:, :], grow[:, :]).then_inc(m_idx, 1)
                link(v.memset(seg[:, :, :], 0.0))

                def tables(b):
                    u = b % 2
                    v.wait_ge(m_x, b + 1)
                    v.tensor_copy(s.src_t[:, b * P:(b + 1) * P, :], px[u][:, 0, :, :].rearrange("p c i -> p i c"))
                    v.tensor_copy(s.dst_t[:, b * P:(b + 1) * P, :],
                                  px[u][:, 1, :, :].rearrange("p c i -> p i c")).then_inc(m_done, 1)

                for b in range(IBLOCKS):
                    u = b % 2
                    v.wait_ge(m_rows[u], 32 * (b // 2 + 1))
                    if b >= 2:
                        v.wait_ge(m_st[u], 32 * (b // 2))
                        v.wait_ge(m_x, b - 1)
                    v.tensor_copy(srcf[:, u, :], srcb[:, u, :])
                    link(v.tensor_scalar(dloc[:, u, :], dstb[:, u, :], tbase[:, b:b + 1], None, ALU.subtract))
                    link(v.tensor_tensor(seg[:, u, 1:EROW], dstb[:, u, 1:EROW], dstb[:, u, 0:EROW - 1], ALU.not_equal))
                    link(v.tensor_scalar(seg[:, u, :], seg[:, u, :], -BIG, None, ALU.mult))
                    link(v.tensor_copy(dlocb[:, u, :], dloc[:, u, :]))
                    v.sem_inc(m_loc, 1)
                    if b >= 1:
                        tables(b - 1)
                tables(IBLOCKS - 1)


def statistics(v, passed, x, st, mv, ve, m_bn, m_mv, m_var, tile, fill):
    v.bn_stats(st, x).then_inc(m_bn, 1)
    fill(0)
    v.wait_ge(m_bn, tile + 1)
    v.sem_inc(passed, 1)
    v.bn_aggr(mv, st).then_inc(m_mv, 1)
    fill(1)
    v.wait_ge(m_mv, tile + 1)
    v.tensor_scalar(ve, mv[:, 1:2], EPS, None, ALU.add).then_inc(m_var, 1)


def roots(g, half, ve, rs, m_var, m_rs):
    def root(i, u):
        g.wait_ge(m_var, DEPTH * i + u + 1)
        g.tensor_tensor(rs[:, u:u + 1], ve[:, u:u + 1], half[:, :], ALU.pow).then_inc(m_rs, 1)

    turns(g, TILES, DEPTH, root)


def project0(nc, s, x, dst2, Wv, bv, wq, bq, wk, bk):
    with ExitStack() as ctx:
        def sb(name, shape, dt=F32):
            return ctx.enter_context(nc.sbuf_tensor(name, shape, dt))

        w = sb("a_w", [P, KD, D])
        rows = sb("a_rows", [P, 3, D])
        bqk = sb("a_bqk", [P, 2])
        kcol = sb("a_kcol", [P, DEPTH])
        xin = sb("a_xin", [P, DEPTH, D])
        st = sb("a_st", [P, DEPTH, 6])
        mv = sb("a_mv", [P, DEPTH, 2])
        ve = sb("a_ve", [P, DEPTH])
        rs = sb("a_rs", [P, DEPTH])
        xn = sb("a_xn", [P, DEPTH, D])
        xT = sb("a_xT", [P, DEPTH, KD, P])
        hq = sb("a_hq", [P, DEPTH, D + 1])
        junk = sb("a_junk", [P, 2, D])
        pT = [ctx.enter_context(nc.psum_tensor(f"a_pT{u}", [P, KD, P], F32)) for u in (0, 1)]
        pH = [ctx.enter_context(nc.psum_tensor(f"a_pH{u}", [P, D], F32)) for u in (0, 1)]
        m_w = s.sem("a_w")
        m_x = [s.sem(f"a_x{u}") for u in range(DEPTH)]
        m_st = [s.sem(f"a_st{u}") for u in range(DEPTH)]
        m_bn, m_mv, m_var, m_rs, m_xn, m_T, m_xT, m_h, m_hb, m_dot, m_hq, m_k = (
            s.sem("a_" + n) for n in ("bn", "mv", "var", "rs", "xn", "T", "xT", "h", "hb", "dot", "hq", "k"))

        with nc.Block() as block:
            @block.sync
            def _(sp):
                sp.dma_start(w[:, :, :], Wv.rearrange("(k p) n -> p k n", p=P)).then_inc(m_w, 16)
                for j, row in enumerate((bv, wq, wk)):
                    sp.dma_start(rows[:, j, :], row.partition_broadcast(P)).then_inc(m_w, 16)
                for j, one in enumerate((bq, bk)):
                    sp.dma_start(bqk[:, j:j + 1], one.partition_broadcast(P)).then_inc(m_w, 16)
                with nc.allow_non_contiguous_dma(reason="one element of each edge row"):
                    sp.dma_start(s.first_i[:, :], dst2[:, 0:1].rearrange("r o -> o r")).then_inc(s.m_first, 16)

                def load(i, u):
                    if not first(i):
                        sp.wait_ge(m_xn, DEPTH * i + u - DEPTH + 1)
                    sp.dma_start(xin[:, u, :], x[ds((DEPTH * i + u) * P, P), :]).then_inc(m_x[u], 16)

                turns(sp, TILES, DEPTH, load)

            @block.gpsimd
            def _(g):
                roots(g, s.half, ve, rs, m_var, m_rs)

            @block.tensor
            def _(pe):
                def transposes(i, u):
                    pe.wait_ge(m_xn, DEPTH * i + u + 1)
                    if back(i, u, 2):
                        pe.wait_ge(m_xT, DEPTH * i + u - 1)
                    for k in range(KD):
                        last = pe.transpose(pT[u % 2][:, k, :], xn[:, u, k * P:(k + 1) * P], s.ident[:, :])
                    last.then_inc(m_T, 1)

                def product(i, u):
                    pe.wait_ge(m_xT, DEPTH * i + u + 1)
                    if back(i, u, 2):
                        pe.wait_ge(m_hb, DEPTH * i + u - 1)
                    for k in range(KD):
                        last = pe.matmul(pH[u % 2][:, :], xT[:, u, k, :], w[:, k, :], start=k == 0, stop=k == KD - 1)
                    last.then_inc(m_h, 1)

                def step(i, u):
                    transposes(i, u)
                    if back(i, u, 1):
                        product(*back(i, u, 1))

                pe.wait_ge(m_w, 16 * 6)
                turns(pe, TILES, DEPTH, step)
                product(*LAST_TILE)

            @block.scalar
            def _(act):
                def copy(i, u):
                    act.wait_ge(m_T, DEPTH * i + u + 1)
                    if not first(i):
                        act.wait_ge(m_h, DEPTH * i + u - DEPTH + 1)
                    act.copy(xT[:, u, :, :], pT[u % 2][:, :, :]).then_inc(m_xT, 1)

                def store(i, u):
                    act.wait_ge(m_hq, DEPTH * i + u + 1)
                    act.dma_start(s.hq_d[ds((DEPTH * i + u) * P, P), :], hq[:, u, :]).then_inc(m_st[u], 16)

                def step(i, u):
                    copy(i, u)
                    if back(i, u, 3):
                        store(*back(i, u, 3))

                turns(act, TILES, DEPTH, step)
                for n in (2, 1, 0):
                    store(*back(*LAST_TILE, n))
                wait_stores(act, m_st)

            @block.vector
            def _(v):
                v.wait_ge(m_w, 16 * 6)

                def normalise(i, u):
                    v.wait_ge(m_rs, DEPTH * i + u + 1)
                    if not first(i):
                        v.wait_ge(m_T, DEPTH * i + u - DEPTH + 1)
                    v.tensor_scalar(xn[:, u, :], xin[:, u, :], mv[:, u, 0:1], rs[:, u:u + 1], ALU.subtract,
                                    ALU.mult).then_inc(m_xn, 1)

                def bias(i, u):
                    v.wait_ge(m_h, DEPTH * i + u + 1)
                    if not first(i):
                        v.wait_ge(m_st[u], 16 * i)
                    v.tensor_tensor(hq[:, u, 0:D], pH[u % 2][:, :], rows[:, 0, :], ALU.add).then_inc(m_hb, 1)

                def dots(i, u):
                    t = DEPTH * i + u
                    v.wait_ge(m_hb, t + 1)
                    if back(i, u, 1):
                        v.wait_ge(m_k, t)
                    v.tensor_tensor_reduce(junk[:, 0, :], hq[:, u, 0:D], rows[:, 1, :], 1.0, 0.0, ALU.mult,
                                           ALU.add, hq[:, u, D:D + 1])
                    v.tensor_tensor_reduce(junk[:, 1, :], hq[:, u, 0:D], rows[:, 2, :], 1.0, 0.0, ALU.mult,
                                           ALU.add, kcol[:, u:u + 1]).then_inc(m_dot, 1)
                    v.wait_ge(m_dot, t + 1)
                    v.tensor_scalar(hq[:, u, D:D + 1], hq[:, u, D:D + 1], bqk[:, 0:1], None, ALU.add).then_inc(m_hq, 1)
                    v.tensor_scalar(s.kf[:, ds(t, 1)], kcol[:, u:u + 1], bqk[:, 1:2], None, ALU.add).then_inc(m_k, 1)

                def run(now, last, old):
                    def fill(gap):
                        if gap == 0 and last:
                            normalise(*last)
                        if gap == 1 and old:
                            bias(*old)

                    if now:
                        i, u = now
                        v.wait_ge(m_x[u], 16 * (i + 1))
                        statistics(v, s.passed, xin[:, u, :], st[:, u, :], mv[:, u, :], ve[:, u:u + 1], m_bn, m_mv,
                                   m_var, DEPTH * i + u, fill)
                    else:
                        fill(0)
                        fill(1)
                    if old:
                        dots(*old)

                tiles_pipelined(v, run)
                v.wait_ge(m_k, TILES)
                link = linker(v, m_k, TILES)
                link(v.tensor_copy(s.k0[:, :, 0], s.kf[:, :]))
                for c in range(1, KPARTS):
                    link(v.tensor_tensor(s.kf[:, :], s.kf[:, :], s.k0[:, :, c - 1], ALU.subtract))
                    link(v.tensor_copy(s.k0[:, :, c], s.kf[:, :]))


def edges0(nc, s):
    with ExitStack() as ctx:
        def sb(name, shape, dt=F32):
            return ctx.enter_context(nc.sbuf_tensor(name, shape, dt))

        R = sb("e_R", [P, RING, GROUP, CH, HCOLS])
        idx = sb("e_idx", [P, RING, COLS], I32)
        drow = sb("e_drow", [P, 2, GROUP, EROW], BF16)
        seg = sb("e_seg", [GROUP, 2, EROW + 1])
        OHT = sb("e_OHT", [P, 2, GROUP, EROW], BF16)
        OH = sb("e_OH", [P, 2, COLS, P], BF16)
        W = sb("e_W", [P, 2, COLS, P])
        fwd = sb("e_fwd", [GROUP, EROW])
        bwd = sb("e_bwd", [GROUP, EROW])
        mx = sb("e_mx", [GROUP, EROW])
        dcol = sb("e_dcol", [P, 2, COLS])
        kS = sb("e_kS", [P, GROUP, CH])
        z = sb("e_z", [P, 2, GROUP, CH])
        c = sb("e_c", [P, 2, GROUP, CH])
        dd = sb("e_dd", [P, COLS])
        w = sb("e_w", [P, 2, COLS])
        rl = sb("e_rl", [P, GROUP])
        ltmp = sb("e_ltmp", [P, 2, GROUP])
        none = sb("e_none", [P, GROUP])
        sn = sb("e_sn", [P, GROUP])
        run = sb("e_run", [P, GROUP + 1])
        old = sb("e_old", [P, GROUP])
        dab = sb("e_dab", [P, 2, GROUP])
        ab = sb("e_ab", [P, 2, 2, GROUP])
        tmp = sb("e_tmp", [P, 2, GROUP, ACOLS])

        pA = ctx.enter_context(nc.psum_tensor("e_pA", [P, 2, GROUP // 2, 2, D], F32))
        pL = ctx.enter_context(nc.psum_tensor("e_pL", [P, GROUP, 2], F32))
        pS = ctx.enter_context(nc.psum_tensor("e_pS", [P, 512], F32))
        pK = pS[:, 0:COLS * KPARTS]
        pM = ctx.enter_context(nc.psum_tensor("e_pM", [P, 512], F32))[:, 0:COLS]
        pQ = pS[0:GROUP, 128:128 + EROW]
        m_idx = s.sem("e_idx")
        m_g = [s.sem(f"e_g{u}") for u in range(RING)]
        m_row = [s.sem(f"e_row{u}") for u in (0, 1)]
        (m_v, m_one, m_oh, m_oht, m_q, m_mx, m_mxe, m_dd, m_w, m_W, m_l, m_sum, m_dab, m_ab, m_tmp, m_done, m_old, m_z) = (
            s.sem("e_" + n) for n in ("v", "one", "oh", "oht", "q", "mx", "mxe", "dd", "w", "W", "l", "sum", "dab",
                                      "ab", "tmp", "done", "old", "z"))
        LINKS_S, LINKS_M, LINKS_C = 3, 7, GROUP
        LINKS = LINKS_S + LINKS_M + LINKS_C

        with nc.Block() as block:
            @block.gpsimd
            def _(g):
                def gather(i, u):
                    b = RING * i + u
                    if not first(i):
                        g.wait_ge(m_sum, 2 * (b - RING + 1))
                    g.tensor_copy(idx[:, u, :], s.src_t[:, ds(b * GROUP, GROUP), :]).then_inc(m_idx, 1)
                    g.wait_ge(m_idx, b + 1)
                    g.sem_inc(s.passed, 1)
                    for n in range(COLS):
                        g.indirect_dma_start(R[:, u, n // CH, n % CH, 0:D + 1], None, s.hq_d[:, :],
                                             bass.IndirectOffsetOnAxis(ap=idx[:, u, n:n + 1], axis=0)
                                             ).then_inc(m_g[u], 16)

                g.wait_ge(m_one, 1)
                turns(g, GROUPS, RING, gather)

            @block.sync
            def _(sp):
                def load(i, u):
                    b = 2 * i + u
                    if not first(i):
                        sp.wait_ge(m_mx, b - 1)
                    sp.dma_start(drow[:, u, :, :], s.drow_d[ds(b * GROUP, GROUP), :].partition_broadcast(P)
                                 ).then_inc(m_row[u], 16)
                    sp.dma_start(seg[:, u, :], s.seg_d[ds(b * GROUP, GROUP), :]).then_inc(m_row[u], 16)

                turns(sp, GROUPS, 2, load)

            @block.tensor
            def _(pe):
                def edge_values(i, u):
                    b = RING * i + u
                    tiles = load_tiles(nc, s, ENGINE.PE, b)
                    if before(i, u, RING):
                        pe.wait_ge(m_dd, b)
                    pe.wait_ge(m_oht, b + 1)
                    for n in range(COLS):
                        pe.matmul(pK[:, n * KPARTS:(n + 1) * KPARTS],
                                  OHT[:, u % 2, n // CH, (n % CH) * P:(n % CH + 1) * P],
                                  s.k0[:, ds(tiles[n // CH], 1), :], start=True, stop=True)
                    pe.wait_ge(m_g[u], 16 * COLS * (i + 1))
                    for j in range(CH):
                        last = pe.transpose(pQ[:, j * P:(j + 1) * P], R[:, u, :, j, QCOL], s.ident[:, :])
                    last.then_inc(m_q, 1)

                def turn_maxima(i, u):
                    pe.wait_ge(m_mx, RING * i + u + 1)
                    pe.sem_inc(s.passed, 1)
                    for j in range(CH):
                        last = pe.transpose(pM[:, j * GROUP:(j + 1) * GROUP], mx[:, j * P:(j + 1) * P],
                                            s.ident[0:GROUP, 0:GROUP])
                    last.then_inc(m_mxe, 1)

                def totals(i, u):
                    b = RING * i + u
                    for n in range(COLS):
                        pe.wait_ge(m_W, COLS * b + n + 1)
                        if n == 0 and before(i, u, RING):
                            pe.wait_ge(m_dab, b)
                        last = pe.matmul(pL[:, n // CH, :], W[:, u % 2, n, :], R[:, u, n // CH, n % CH, ONECOL:HCOLS],
                                         start=n % CH == 0, stop=n % CH == CH - 1)
                    last.then_inc(m_l, 1)

                def sums(i, u, half):
                    b = RING * i + u
                    if not first(i) or u >= 2:
                        pe.wait_ge(m_tmp, (b - 2) * GROUP + 2 * half + 2)
                    for n in (2 * half, 2 * half + 1):
                        for j in range(CH):
                            last = pe.matmul(pA[:, u % 2, half, n % 2, :], W[:, u % 2, n * CH + j, :],
                                             R[:, u, n, j, 0:D], start=j == 0, stop=j == CH - 1)
                    last.then_inc(m_sum, 1)

                def step(i, u, left=None):
                    if left != 0:
                        edge_values(*after(i, u, RING))
                    totals(i, u)
                    if left != 0:
                        turn_maxima(*after(i, u, RING))
                    sums(i, u, 0)
                    sums(i, u, 1)

                edge_values(0, 0)
                turn_maxima(0, 0)
                turns(pe, GROUPS, RING, step, peel_last=True)

            @block.scalar
            def _(act):
                def weights(i, u):
                    b = RING * i + u
                    act.wait_ge(m_dd, b + 1)
                    if not first(i) or u >= 2:
                        act.wait_ge(m_sum, 2 * (b - 1))
                    act.activation(w[:, u % 2, :], dd[:, :], ACT.Exp).then_inc(m_w, 1)
                    act.wait_ge(m_w, b + 1)
                    act.wait_ge(m_oh, b + 1)
                    for n in range(COLS):
                        act.activation(W[:, u % 2, n, :], OH[:, u % 2, n, :], ACT.Copy, scale=w[:, u % 2, n:n + 1]
                                       ).then_inc(m_W, 1)

                def factors(i, u):
                    b = RING * i + u
                    act.wait_ge(m_dab, b + 1)
                    if not first(i) or u >= 2:
                        act.wait_ge(m_done, b - 1)
                    act.activation(ab[:, u % 2, :, :], dab[:, :, :], ACT.Exp).then_inc(m_ab, 1)

                def rescale(i, u):
                    b = RING * i + u
                    act.wait_ge(m_ab, b + 1)
                    for n in range(GROUP):
                        if n % 2 == 0:
                            act.wait_ge(m_sum, 2 * b + n // 2 + 1)
                        act.activation(tmp[:, u % 2, n, 0:D], pA[:, u % 2, n // 2, n % 2, :], ACT.Copy,
                                       scale=ab[:, u % 2, 1, n:n + 1]
                                       ).then_inc(m_tmp, 1)

                def step(i, u, left=None):
                    factors(i, u)
                    if left != 0:
                        weights(*after(i, u, RING))
                    rescale(i, u)

                weights(0, 0)
                turns(act, GROUPS, RING, step, peel_last=True)

            @block.vector
            def _(v):
                v.memset(run[:, 0:1], -BIG)
                v.memset(R[:, :, :, :, ONECOL], 1.0).then_inc(m_one, 1)

                def copy_destinations(i, u):
                    v.tensor_copy(dcol[:, u % 2, :], s.dst_t[:, ds((RING * i + u) * GROUP, GROUP), :]).then_inc(m_old, 1)

                def select_rows(i, u):
                    b = RING * i + u
                    h = u % 2
                    v.wait_ge(m_row[h], 32 * (i * (RING // 2) + u // 2 + 1))
                    if not first(i) or u >= 2:
                        v.wait_ge(m_q, b - 1)
                        v.wait_ge(m_W, COLS * (b - 1))
                    v.tensor_scalar(OHT[:, h, :, :], drow[:, h, :, :], s.part[:, 0:1], None,
                                    ALU.is_equal).then_inc(m_oht, 1)

                def select_columns(i, u, columns):
                    v.wait_ge(m_old, RING * i + u + 1)
                    for n in columns:
                        last = v.tensor_scalar(OH[:, u % 2, n, :], s.iota_b[:, :], dcol[:, u % 2, n:n + 1], None,
                                               ALU.is_equal)
                    if n == COLS - 1:
                        last.then_inc(m_oh, 1)

                def scans(i, u, base):
                    b = RING * i + u
                    h = u % 2
                    v.wait_ge(m_q, b + 1)
                    v.tensor_tensor_scan(fwd[:, :], seg[:, h, 0:EROW], pQ, -BIG, ALU.add, ALU.max)
                    v.tensor_tensor_scan(bwd[:, ::-1], seg[:, h, 1:EROW + 1][:, ::-1], pQ[:, ::-1], -BIG,
                                         ALU.add, ALU.max).then_inc(m_v, 1)
                    v.tensor_reduce(kS[:, :, :], pK.rearrange("p (n j c) -> p n j c", j=CH, c=KPARTS), X, ALU.add
                                    ).then_inc(m_v, 1)
                    v.wait_ge(m_v, base + 1)
                    v.tensor_tensor(mx[:, :], fwd[:, :], bwd[:, :], ALU.max).then_inc(m_mx, 1)
                    v.wait_ge(m_v, base + 2)
                    v.tensor_tensor(z[:, 0, :, :], R[:, u, :, :, QCOL], kS[:, :, :], ALU.add).then_inc(m_v, 1)

                def shifts(i, u, base, part):
                    b = RING * i + u
                    if part == 0:
                        v.wait_ge(m_mxe, b + 1)
                        v.wait_ge(m_v, base)
                        v.tensor_tensor(z[:, 1, :, :], pM.rearrange("p (j n) -> p n j", j=CH), kS[:, :, :], ALU.add
                                        ).then_inc(m_z, 1)
                    elif part == 1:
                        v.wait_ge(m_z, 2 * b + 1)
                        v.scalar_tensor_tensor(c[:, :, :, :], z[:, :, :, :], 0.2, z[:, :, :, :], ALU.mult, ALU.max
                                               ).then_inc(m_z, 1)
                    else:
                        v.wait_ge(m_z, 2 * b + 2)
                        v.tensor_copy(R[:, u, :, :, SCOL], c[:, 1, :, :])
                        v.tensor_tensor(dd[:, :], c[:, 0, :, :], c[:, 1, :, :], ALU.subtract).then_inc(m_dd, 1)

                def maxima(i, u, base, fill):
                    b = RING * i + u
                    v.wait_ge(m_l, b + 1)
                    v.tensor_scalar(rl[:, :], pL[:, :, 0], 1e-30, None, ALU.max).then_inc(m_v, 1)
                    v.tensor_scalar(none[:, :], pL[:, :, 0], 0.5, -BIG, ALU.is_lt, ALU.mult)
                    fill(0)
                    v.wait_ge(m_v, base + 1)
                    v.reciprocal(rl[:, :], rl[:, :]).then_inc(m_v, 1)
                    fill(1)
                    v.wait_ge(m_v, base + 2)
                    v.tensor_tensor(sn[:, :], pL[:, :, 1], rl[:, :], ALU.mult).then_inc(m_v, 1)
                    fill(2)
                    v.wait_ge(m_v, base + 3)
                    v.tensor_tensor(sn[:, :], sn[:, :], none[:, :], ALU.add).then_inc(m_v, 1)
                    fill(3)
                    v.wait_ge(m_v, base + 4)
                    v.tensor_tensor_scan(run[:, 1:GROUP + 1], s.fresh[:, ds(b * GROUP, GROUP)], sn[:, :],
                                         run[:, 0:1], ALU.add, ALU.max).then_inc(m_v, 1)
                    v.tensor_copy(ltmp[:, u % 2, :], pL[:, :, 0])
                    v.wait_ge(m_v, base + 5)
                    v.tensor_tensor(old[:, :], run[:, 0:GROUP], s.fresh[:, ds(b * GROUP, GROUP)], ALU.add
                                    ).then_inc(m_v, 1)
                    fill(4)
                    v.wait_ge(m_v, base + 6)
                    v.tensor_tensor(dab[:, 0, :], old[:, :], run[:, 1:GROUP + 1], ALU.subtract)
                    v.tensor_tensor(dab[:, 1, :], sn[:, :], run[:, 1:GROUP + 1], ALU.subtract).then_inc(m_dab, 1)
                    v.tensor_copy(run[:, 0:1], run[:, GROUP:GROUP + 1]).then_inc(m_v, 1)

                def merge(i, u, base, tiles, between=None):
                    b = RING * i + u
                    h = u % 2
                    v.wait_ge(m_ab, b + 1)
                    v.tensor_tensor(tmp[:, h, :, D], ltmp[:, h, :], ab[:, h, 1, :], ALU.mult).then_inc(m_v, 1)
                    for n in range(GROUP):
                        if between:
                            between(n)
                        v.wait_ge(m_tmp, b * GROUP + n + 1)
                        v.wait_ge(m_v, base + 1 + n)
                        if n == 0 and before(i, u, RING):
                            v.wait_ge(m_done, b)
                        a = s.acc[:, ds(tiles[n], 1), :]
                        v.scalar_tensor_tensor(a, a, ab[:, h, 0, n:n + 1], tmp[:, h, n:n + 1, :], ALU.mult,
                                               ALU.add).then_inc(m_v if n < GROUP - 1 else m_done, 1)

                def step(i, u, left=None):
                    b = RING * i + u
                    past = before(i, u, RING)
                    following = after(i, u, RING) if left != 0 else None
                    ahead = after(i, u, RING, 2) if left is None or left > 1 else None
                    base = LINKS_S + b * (LINKS_S + LINKS_M) + ((b - 1) * LINKS_C if past else 0)
                    if following:
                        scans(*following, base)
                        base = base + LINKS_S

                    tiles = []

                    def fill(gap):
                        if past and gap == 0:
                            tiles.extend(load_tiles(nc, s, ENGINE.DVE, b - 1))
                        if following and gap < 3:
                            shifts(*following, base, gap)
                        if ahead and gap == 3:
                            copy_destinations(*ahead)
                        if ahead and gap == 4:
                            select_rows(*ahead)

                    maxima(i, u, base, fill)
                    base = base + LINKS_M
                    if ahead:
                        select_columns(*ahead, range(COLS - GROUP))
                    if past:
                        def between(n):
                            if ahead:
                                select_columns(*ahead, (COLS - GROUP + n,))
                        merge(*past, base, tiles, between)
                    else:
                        select_columns(*ahead, range(COLS - GROUP, COLS))

                for u in (0, 1):
                    copy_destinations(0, u)
                    select_rows(0, u)
                    select_columns(0, u, range(COLS))
                scans(0, 0, 0)
                for part in range(3):
                    shifts(0, 0, LINKS_S, part)
                turns(v, GROUPS, RING, step, peel_last=True)
                merge(*LAST_TURN, (GROUPS - 1) * LINKS + LINKS_S + LINKS_M, load_tiles(nc, s, ENGINE.DVE, GROUPS - 1))


def finish0(nc, s, x):
    with ExitStack() as ctx:
        def sb(name, shape, dt=F32):
            return ctx.enter_context(nc.sbuf_tensor(name, shape, dt))

        xin = sb("f_xin", [P, DEPTH, D])
        x1 = sb("f_x1", [P, DEPTH, 2, D])
        rd = sb("f_rd", [P, TILES])
        st = sb("f_st", [P, DEPTH, 6])
        mv = sb("f_mv", [P, DEPTH, 2])
        ve = sb("f_ve", [P, DEPTH])
        rs = sb("f_rs", [P, DEPTH])
        m_x = [s.sem(f"f_x{u}") for u in range(DEPTH)]
        m_st = [s.sem(f"f_st{u}") for u in range(DEPTH)]
        m_rd, m_x1, m_bn, m_mv, m_var, m_rs, m_xn, m_sum = (
            s.sem("f_" + n) for n in ("rd", "res", "bn", "mv", "var", "rs", "xn", "sum"))

        with nc.Block() as block:
            @block.sync
            def _(sp):
                def load(i, u):
                    if not first(i):
                        sp.wait_ge(m_x1, DEPTH * i + u - DEPTH + 1)
                    sp.dma_start(xin[:, u, :], x[ds((DEPTH * i + u) * P, P), :]).then_inc(m_x[u], 16)

                turns(sp, TILES, DEPTH, load)

            @block.scalar
            def _(act):
                def store(i, u):
                    act.wait_ge(m_xn, DEPTH * i + u + 1)
                    act.dma_start(s.x1_d[ds((DEPTH * i + u) * P, P), :], x1[:, u, :, :]).then_inc(m_st[u], 16)

                turns(act, TILES, DEPTH, store)
                wait_stores(act, m_st)

            @block.gpsimd
            def _(g):
                roots(g, s.half, ve, rs, m_var, m_rs)

            @block.vector
            def _(v):
                v.memset(s.xsum[:, :], 0.0).then_inc(m_sum, 1)
                link = linker(v, m_rd, 0)
                link(v.tensor_scalar(rd[:, :], s.acc[:, :, D], 1e-30, None, ALU.max))
                link(v.reciprocal(rd[:, :], rd[:, :]))

                def residual(i, u):
                    t = DEPTH * i + u
                    v.wait_ge(m_x[u], 16 * (i + 1))
                    if not first(i):
                        v.wait_ge(m_st[u], 16 * i)
                        v.wait_ge(m_sum, t - DEPTH + 2)
                    v.scalar_tensor_tensor(x1[:, u, 0:1, :], s.acc[:, ds(t, 1), 0:D], rd[:, ds(t, 1)],
                                           xin[:, u:u + 1, :], ALU.mult, ALU.add).then_inc(m_x1, 1)

                def normalise(i, u):
                    v.wait_ge(m_rs, DEPTH * i + u + 1)
                    v.tensor_scalar(x1[:, u, 1, :], x1[:, u, 0, :], mv[:, u, 0:1], rs[:, u:u + 1],
                                    ALU.subtract, ALU.mult).then_inc(m_xn, 1)

                def total(i, u):
                    t = DEPTH * i + u
                    v.wait_ge(m_xn, t + 1)
                    v.wait_ge(m_sum, t + 1)
                    v.tensor_tensor(s.xsum[:, :], s.xsum[:, :], x1[:, u, 1, :], ALU.add).then_inc(m_sum, 1)

                def run(now, last, old):
                    def fill(gap):
                        if gap == 0 and last:
                            total(*last)

                    if now:
                        residual(*now)
                    if last:
                        normalise(*last)
                    if now:
                        i, u = now
                        v.wait_ge(m_x1, DEPTH * i + u + 1)
                        statistics(v, s.passed, x1[:, u, 0, :], st[:, u, :], mv[:, u, :], ve[:, u:u + 1], m_bn, m_mv,
                                   m_var, DEPTH * i + u, fill)
                    else:
                        fill(0)

                tiles_pipelined(v, run)




def route0(nc, s, a):
    with ExitStack() as ctx:
        def sb(name, shape, dt=F32):
            return ctx.enter_context(nc.sbuf_tensor(name, shape, dt))

        wr = sb("r_wr", [P, KD, EXPERTS])
        br = sb("r_br", [1, EXPERTS])
        mean = sb("r_mean", [P, KD])
        row = sb("r_row", [1, EXPERTS])
        ex = sb("r_ex", [1, EXPERTS])
        sc = sb("r_sc", [1, EXPERTS])
        eq = sb("r_eq", [1, EXPERTS])
        one = sb("r_one", [1, 8])
        top = sb("r_top", [1, 2])
        tex = sb("r_tex", [1, 2])
        wtop = sb("r_wtop", [1, 2])
        pm = ctx.enter_context(nc.psum_tensor("r_pm", [P, KD], F32))
        pl = ctx.enter_context(nc.psum_tensor("r_pl", [1, EXPERTS], F32))
        pw = ctx.enter_context(nc.psum_tensor("r_pw", [P, 2], F32))
        m_w, m_pe, m_v, m_a, m_go, m_mean, m_top = (s.sem("r_" + n) for n in
                                                    ("w", "pe", "v", "a", "go", "mean", "wtop"))

        with nc.Block() as block:
            @block.sync
            def _(sp):
                sp.dma_start(wr[:, :, :], a["L0_ffn_Wr"].rearrange("(k p) e -> p k e", p=P)).then_inc(m_w, 16)
                sp.dma_start(br[:, :], a["L0_ffn_br"].partition_broadcast(1)).then_inc(m_w, 16)

            @block.tensor
            def _(pe):
                for k in range(KD):
                    last = pe.matmul(pm[:, k:k + 1], s.xsum[:, k * P:(k + 1) * P], s.ones[:, 0:1], start=True, stop=True)
                last.then_inc(m_pe, 1)
                pe.wait_ge(m_w, 32)
                pe.wait_ge(m_mean, 1)
                for k in range(KD):
                    last = pe.matmul(pl[:, :], mean[:, k:k + 1], wr[:, k, :], start=k == 0, stop=k == KD - 1)
                last.then_inc(m_pe, 1)
                pe.wait_ge(m_top, 1)
                pe.matmul(pw[:, :], s.ones[0:1, :], wtop[:, :], start=True, stop=True).then_inc(m_pe, 1)

            @block.scalar
            def _(act):
                for n, (dst, src) in enumerate(((ex, row), (ex, row), (tex, top))):
                    act.wait_ge(m_go, n + 1)
                    act.activation(dst[:, :], src[:, :], ACT.Exp).then_inc(m_a, 1)

            @block.vector
            def _(v):
                link = linker(v, m_v, 0)
                exps = [0]

                def softmax(row_, ex_, out_):
                    link(v.tensor_reduce(one[:, 0:1], row_, X, ALU.max))
                    v.tensor_scalar(row_, row_, one[:, 0:1], None, ALU.subtract).then_inc(m_go, 1)
                    exps[0] += 1
                    v.wait_ge(m_a, exps[0])
                    link(v.tensor_reduce(one[:, 1:2], ex_, X, ALU.add))
                    link(v.reciprocal(one[:, 2:3], one[:, 1:2]))
                    return v.tensor_scalar(out_, ex_, one[:, 2:3], None, ALU.mult)

                v.wait_ge(m_pe, 1)
                v.tensor_scalar(mean[:, :], pm[:, :], 1.0 / N, None, ALU.mult).then_inc(m_mean, 1)
                v.wait_ge(m_pe, 2)
                link(v.tensor_tensor(row[:, :], pl[:, :], br[:, :], ALU.add))
                link(softmax(row[:, :], ex[:, :], row[:, :]))
                link(v.tensor_scalar(sc[:, :], row[:, :], float(N), None, ALU.mult))
                link(v.tensor_scalar(sc[:, :], sc[:, :], CAPACITY, None, ALU.max))
                link(v.reciprocal(sc[:, :], sc[:, :]))
                link(v.tensor_scalar(sc[:, :], sc[:, :], CAPACITY, None, ALU.mult))
                link(v.tensor_tensor(row[:, :], row[:, :], sc[:, :], ALU.mult))
                link(softmax(row[:, :], ex[:, :], row[:, :]))
                for j in range(2):
                    link(v.tensor_reduce(top[:, j:j + 1], row[:, :], X, ALU.max))
                    link(v.tensor_scalar(eq[:, :], row[:, :], top[:, j:j + 1], None, ALU.is_equal))
                    link(v.tensor_scalar(sc[:, :], s.iota[0:1, 0:EXPERTS], float(-EXPERTS), None, ALU.add))
                    link(v.tensor_tensor(sc[:, :], sc[:, :], eq[:, :], ALU.mult))
                    link(v.tensor_reduce(one[:, 3:4], sc[:, :], X, ALU.min))
                    link(v.tensor_scalar(one[:, 4:5], one[:, 3:4], float(EXPERTS), None, ALU.add))
                    link(v.tensor_copy(s.expert_i[:, j:j + 1], one[:, 4:5]))
                    link(v.tensor_scalar(eq[:, :], s.iota[0:1, 0:EXPERTS], one[:, 4:5], -2.0, ALU.is_equal, ALU.mult))
                    link(v.tensor_tensor(row[:, :], row[:, :], eq[:, :], ALU.add))
                softmax(top[:, :], tex[:, :], wtop[:, :]).then_inc(m_top, 1)
                v.wait_ge(m_pe, 3)
                v.tensor_copy(s.wexp[:, :], pw[:, :])


def feed_forward(nc, s, name, func, table, load_weights, prepare, finish, normed, store):
    with ExitStack() as ctx:
        def sb(n, shape, dt=F32):
            return ctx.enter_context(nc.sbuf_tensor(name + n, shape, dt))

        def ps(n, shape):
            return ctx.enter_context(nc.psum_tensor(name + n, shape, F32))

        f = Shared()
        f.w1 = sb("w1", [P, KD, HID])
        f.b1 = sb("b1", [P, HB])
        f.w2 = sb("w2", [P, HB, D])
        f.vec = sb("vec", [P, 4, D])
        f.xrow = sb("xrow", [P, DEPTH, 2, D])
        f.o = sb("o", [P, DEPTH, D])
        f.t1 = sb("t1", [P, DEPTH, D])
        f.st, f.mv, f.ve, f.rs = (sb("st", [P, DEPTH, 6]), sb("mv", [P, DEPTH, 2]), sb("ve", [P, DEPTH]),
                                  sb("rs", [P, DEPTH]))
        xT = sb("xT", [P, 2, KD, P])
        h = sb("h", [P, HB, P])
        pT = ps("pT", [P, KD, P])
        pH = [ps(f"pH{n}", [P, 2, P]) for n in range(HB // 2)]
        f.pY = [ps(f"pY{n}", [P, D]) for n in (0, 1)]
        (f.m_w, f.m_v, m_T, m_xT, m_h, m_g, f.m_y, f.m_o, m_set, f.m_bn, f.m_mv, f.m_var, f.m_rs, f.m_yr, f.m_res,
         f.m_xn, f.m_scaled, f.m_shifted) = (
            s.sem(name + n) for n in ("w", "v", "T", "xT", "h", "g", "y", "o", "set", "bn", "mv", "var", "rs", "yread",
                                      "res", "xn", "scaled", "shifted"))
        m_row = [s.sem(f"{name}row{u}") for u in range(DEPTH)]
        f.m_st = [s.sem(f"{name}st{u}") for u in range(DEPTH)]

        with nc.Block() as block:
            @block.sync
            def _(sp):
                load_weights(sp, f)

                def rows(i, u):
                    if not first(i):
                        sp.wait_ge(f.m_o, DEPTH * i + u - DEPTH + 1)
                    sp.dma_start(f.xrow[:, u, :, :], table[ds((DEPTH * i + u) * P, P), :]).then_inc(m_row[u], 16)

                turns(sp, TILES, DEPTH, rows)

            if normed:
                @block.gpsimd
                def _(g):
                    roots(g, s.half, f.ve, f.rs, f.m_var, f.m_rs)

            @block.tensor
            def _(pe):
                def transposes(i, u):
                    pe.wait_ge(m_row[u], 16 * (i + 1))
                    if back(i, u, 1):
                        pe.wait_ge(m_xT, DEPTH * i + u)
                    for k in range(KD):
                        last = pe.transpose(pT[:, k, :], f.xrow[:, u, 1, k * P:(k + 1) * P], s.ident[:, :])
                    last.then_inc(m_T, 1)

                def hidden(i, u):
                    pe.wait_ge(m_xT, DEPTH * i + u + 1)
                    for n in range(HB):
                        for k in range(KD):
                            last = pe.matmul(pH[n // 2][:, n % 2, :], f.w1[:, k, n * P:(n + 1) * P], xT[:, u % 2, k, :],
                                             start=k == 0, stop=k == KD - 1)
                        if n % 2:
                            last.then_inc(m_h, 1)

                def output(i, u):
                    t = DEPTH * i + u
                    if back(i, u, 2):
                        pe.wait_ge(f.m_yr, t - 1)
                    for n in range(HB):
                        pe.wait_ge(m_g, t * HB + n + 1)
                        last = pe.matmul(f.pY[u % 2][:, :], h[:, n, :], f.w2[:, n, :], start=n == 0, stop=n == HB - 1)
                    last.then_inc(f.m_y, 1)

                def step(i, u):
                    if back(i, u, 1):
                        hidden(*back(i, u, 1))
                    transposes(i, u)
                    if back(i, u, 1):
                        output(*back(i, u, 1))

                pe.wait_ge(m_set, 1)
                turns(pe, TILES, DEPTH, step)
                hidden(*LAST_TILE)
                output(*LAST_TILE)

            @block.scalar
            def _(act):
                def turned(i, u):
                    act.wait_ge(m_T, DEPTH * i + u + 1)
                    if back(i, u, 2):
                        act.wait_ge(m_h, (DEPTH * i + u - 1) * (HB // 2))
                    act.copy(xT[:, u % 2, :, :], pT[:, :, :]).then_inc(m_xT, 1)

                def hidden(i, u):
                    t = DEPTH * i + u
                    for n in range(HB):
                        if n % 2 == 0:
                            act.wait_ge(m_h, t * (HB // 2) + n // 2 + 1)
                        if n == 0 and back(i, u, 1):
                            act.wait_ge(f.m_y, t)
                        act.activation(h[:, n, :], pH[n // 2][:, n % 2, :], func, bias=f.b1[:, n:n + 1]).then_inc(m_g, 1)

                def step(i, u):
                    if back(i, u, 1):
                        hidden(*back(i, u, 1))
                    turned(i, u)
                    if back(i, u, 3):
                        store(act, f, *back(i, u, 3), False)

                act.wait_ge(m_set, 1)
                turns(act, TILES, DEPTH, step)
                hidden(*LAST_TILE)
                for n in (2, 1, 0):
                    store(act, f, *back(*LAST_TILE, n), n == 0)
                wait_stores(act, f.m_st)

            @block.vector
            def _(v):
                prepare(v, f)
                v.sem_inc(m_set, 1)
                finish(v, f)


def feed_forward0(nc, s, a):
    EH = HID // 2

    def load(sp, f):
        experts = [sp.value_load(s.expert_i[0:1, j:j + 1], min_val=0, max_val=EXPERTS - 1) for j in (0, 1)]
        with nc.allow_non_contiguous_dma(reason="biases, one to a partition"):
            for j, e in enumerate(experts):
                sp.dma_start(f.w1[:, :, j * EH:(j + 1) * EH],
                             a["L0_ffn_W1"][ds(e, 1), :, :].rearrange("o (k p) f -> p (o k) f", p=P)).then_inc(f.m_w, 16)
                sp.dma_start(f.w2[:, j * HB // 2:(j + 1) * HB // 2, :],
                             a["L0_ffn_W2"][ds(e, 1), :, :].rearrange("o (n p) d -> p (o n) d", p=P)).then_inc(f.m_w, 16)
                sp.dma_start(f.b1[:, j * HB // 2:(j + 1) * HB // 2],
                             a["L0_ffn_b1"][ds(e, 1), :].rearrange("o (n p) -> p (o n)", p=P)).then_inc(f.m_w, 16)
                sp.dma_start(f.vec[:, j, :], a["L0_ffn_b2"][ds(e, 1), :].partition_broadcast(P)).then_inc(f.m_w, 16)
        for j, n in enumerate(("L0_ffn_gamma", "L0_ffn_beta")):
            sp.dma_start(f.vec[:, 2 + j, :], a[n].partition_broadcast(P)).then_inc(f.m_w, 16)

    def prepare(v, f):
        link = linker(v, f.m_v, 0)
        v.wait_ge(f.m_w, 16 * 10)
        for j in (0, 1):
            w2 = f.w2[:, j * HB // 2:(j + 1) * HB // 2, :]
            link(v.tensor_scalar(w2, w2, s.wexp[:, j:j + 1], None, ALU.mult))
            link(v.tensor_scalar(f.vec[:, j, :], f.vec[:, j, :], s.wexp[:, j:j + 1], None, ALU.mult))
        link(v.tensor_tensor(f.vec[:, 0, :], f.vec[:, 0, :], f.vec[:, 1, :], ALU.add))

    def finish(v, f):
        def residual(i, u):
            t = DEPTH * i + u
            v.wait_ge(f.m_y, t + 1)
            if not first(i):
                v.wait_ge(f.m_shifted, t - DEPTH + 1)
            v.tensor_tensor(f.t1[:, u, :], f.pY[u % 2][:, :], f.vec[:, 0, :], ALU.add).then_inc(f.m_yr, 1)

        def run(now, last, old):
            if now:
                residual(*now)
            if last:
                i, u = last
                v.wait_ge(f.m_rs, DEPTH * i + u + 1)
                v.tensor_scalar(f.t1[:, u, :], f.t1[:, u, :], f.mv[:, u, 0:1], f.rs[:, u:u + 1], ALU.subtract,
                                ALU.mult).then_inc(f.m_xn, 1)
            if now:
                i, u = now
                v.wait_ge(f.m_yr, DEPTH * i + u + 1)
                v.tensor_tensor(f.t1[:, u, :], f.t1[:, u, :], f.xrow[:, u, 1, :], ALU.add).then_inc(f.m_res, 1)
            if last:
                i, u = last
                v.wait_ge(f.m_xn, DEPTH * i + u + 1)
                v.tensor_tensor(f.t1[:, u, :], f.t1[:, u, :], f.vec[:, 2, :], ALU.mult).then_inc(f.m_scaled, 1)

            def fill(gap):
                if not last:
                    return
                i, u = last
                t = DEPTH * i + u
                if gap == 0:
                    v.wait_ge(f.m_scaled, t + 1)
                    v.tensor_tensor(f.t1[:, u, :], f.t1[:, u, :], f.vec[:, 3, :], ALU.add).then_inc(f.m_shifted, 1)
                else:
                    v.wait_ge(f.m_shifted, t + 1)
                    if not first(i):
                        v.wait_ge(f.m_st[u], 16 * i)
                    v.tensor_tensor(f.o[:, u, :], f.t1[:, u, :], f.xrow[:, u, 0, :], ALU.add).then_inc(f.m_o, 1)

            if now:
                i, u = now
                v.wait_ge(f.m_res, DEPTH * i + u + 1)
                statistics(v, s.passed, f.t1[:, u, :], f.st[:, u, :], f.mv[:, u, :], f.ve[:, u:u + 1], f.m_bn, f.m_mv,
                           f.m_var, DEPTH * i + u, fill)
            else:
                fill(0)
                fill(1)

        tiles_pipelined(v, run)

    def store(act, f, i, u, last):
        act.wait_ge(f.m_o, DEPTH * i + u + 1)
        act.dma_start(s.x2_d[ds((DEPTH * i + u) * P, P), :], f.o[:, u, :]).then_inc(f.m_st[u], 16)

    feed_forward(nc, s, "g", ACT.Gelu, s.x1_d, load, prepare, finish, True, store)


def feed_forward1(nc, s, a, out):
    def load(sp, f):
        sp.dma_start(f.w1[:, :, :], a["L1_ffn_w1"].rearrange("(k p) f -> p k f", p=P)).then_inc(f.m_w, 16)
        sp.dma_start(f.w2[:, :, :], a["L1_ffn_w2"].rearrange("(n p) d -> p n d", p=P)).then_inc(f.m_w, 16)
        with nc.allow_non_contiguous_dma(reason="biases, one to a partition"):
            sp.dma_start(f.b1[:, :], a["L1_ffn_b1"].rearrange("(n p) -> p n", p=P)).then_inc(f.m_w, 16)
        sp.dma_start(f.vec[:, 0, :], a["L1_ffn_b2"].partition_broadcast(P)).then_inc(f.m_w, 16)

    def prepare(v, f):
        v.wait_ge(f.m_w, 16 * 4)

    def finish(v, f):
        def one(i, u):
            t = DEPTH * i + u
            v.wait_ge(f.m_y, t + 1)
            if not first(i):
                v.wait_ge(f.m_o, t - DEPTH + 1)
            v.tensor_tensor(f.t1[:, u, :], f.pY[u % 2][:, :], f.vec[:, 0, :], ALU.add).then_inc(f.m_yr, 1)
            v.wait_ge(f.m_yr, t + 1)
            v.scalar_tensor_tensor(f.t1[:, u, :], f.t1[:, u, :], s.wcol[:, ds(t, 1)], f.xrow[:, u, 1, :],
                                   ALU.mult, ALU.add).then_inc(f.m_res, 1)
            v.wait_ge(f.m_res, t + 1)
            if not first(i):
                v.wait_ge(f.m_st[u], 16 * i)
            v.tensor_tensor(f.o[:, u, :], f.t1[:, u, :], f.xrow[:, u, 0, :], ALU.add).then_inc(f.m_o, 1)

        turns(v, TILES, DEPTH, one)

    def store(act, f, i, u, last):
        act.wait_ge(f.m_o, DEPTH * i + u + 1)
        rows = LAST if last else P
        act.dma_start(out[ds((DEPTH * i + u) * P, rows), :], f.o[0:rows, u, :]).then_inc(f.m_st[u], 16)

    feed_forward(nc, s, "j", ACT.Gelu_apprx_tanh, s.x3_d, load, prepare, finish, False, store)


def project1(nc, s, a):
    with ExitStack() as ctx:
        def sb(name, shape, dt=F32):
            return ctx.enter_context(nc.sbuf_tensor(name, shape, dt))

        w = sb("p_w", [P, KD, 3 * D])
        bias = sb("p_bias", [P, 3 * D])
        xin = sb("p_xin", [P, DEPTH, D])
        st, mv, ve, rs = sb("p_st", [P, DEPTH, 6]), sb("p_mv", [P, DEPTH, 2]), sb("p_ve", [P, DEPTH]), sb("p_rs", [P, DEPTH])
        xn = sb("p_xn", [P, DEPTH, D])
        xT = sb("p_xT", [P, DEPTH, KD, P])
        qvk = sb("p_qvk", [P, DEPTH, 3 * D])
        pT = [ctx.enter_context(nc.psum_tensor(f"p_pT{u}", [P, KD, P], F32)) for u in (0, 1)]
        pQV = [ctx.enter_context(nc.psum_tensor(f"p_pQV{u}", [P, 2 * D], F32)) for u in (0, 1)]
        pKK = [ctx.enter_context(nc.psum_tensor(f"p_pKK{u}", [P, D], F32)) for u in (0, 1)]
        m_w = s.sem("p_w")
        m_x = [s.sem(f"p_x{u}") for u in range(DEPTH)]
        m_bn, m_mv, m_var, m_rs, m_xn, m_T, m_xT, m_h, m_o = (
            s.sem("p_" + n) for n in ("bn", "mv", "var", "rs", "xn", "T", "xT", "h", "o"))
        m_st, m_stk = [s.sem(f"p_st{u}") for u in range(DEPTH)], [s.sem(f"p_stk{u}") for u in range(DEPTH)]

        with nc.Block() as block:
            @block.sync
            def _(sp):
                for j, n in enumerate(("q", "v", "k")):
                    sp.dma_start(w[:, :, j * D:(j + 1) * D],
                                 a["L1_gnn_W" + n].rearrange("(k p) n -> p k n", p=P)).then_inc(m_w, 16)
                    sp.dma_start(bias[:, j * D:(j + 1) * D], a["L1_gnn_b" + n].partition_broadcast(P)).then_inc(m_w, 16)

                def load(i, u):
                    if not first(i):
                        sp.wait_ge(m_xn, DEPTH * i + u - DEPTH + 1)
                    sp.dma_start(xin[:, u, :], s.x2_d[ds((DEPTH * i + u) * P, P), :]).then_inc(m_x[u], 16)

                turns(sp, TILES, DEPTH, load)

            @block.gpsimd
            def _(g):
                roots(g, s.half, ve, rs, m_var, m_rs)

            @block.tensor
            def _(pe):
                def transposes(i, u):
                    pe.wait_ge(m_xn, DEPTH * i + u + 1)
                    if back(i, u, 2):
                        pe.wait_ge(m_xT, DEPTH * i + u - 1)
                    for k in range(KD):
                        last = pe.transpose(pT[u % 2][:, k, :], xn[:, u, k * P:(k + 1) * P], s.ident[:, :])
                    last.then_inc(m_T, 1)

                def product(i, u):
                    pe.wait_ge(m_xT, DEPTH * i + u + 1)
                    if back(i, u, 2):
                        pe.wait_ge(m_o, DEPTH * i + u - 1)
                    for k in range(KD):
                        pe.matmul(pQV[u % 2][:, :], xT[:, u, k, :], w[:, k, 0:2 * D], start=k == 0, stop=k == KD - 1)
                    for k in range(KD):
                        last = pe.matmul(pKK[u % 2][:, :], xT[:, u, k, :], w[:, k, 2 * D:], start=k == 0,
                                         stop=k == KD - 1)
                    last.then_inc(m_h, 1)

                def step(i, u):
                    transposes(i, u)
                    if back(i, u, 1):
                        product(*back(i, u, 1))

                pe.wait_ge(m_w, 16 * 6)
                turns(pe, TILES, DEPTH, step)
                product(*LAST_TILE)

            @block.scalar
            def _(act):
                def turned(i, u):
                    act.wait_ge(m_T, DEPTH * i + u + 1)
                    if not first(i):
                        act.wait_ge(m_h, DEPTH * i + u - DEPTH + 1)
                    act.copy(xT[:, u, :, :], pT[u % 2][:, :, :]).then_inc(m_xT, 1)

                def store(i, u):
                    act.wait_ge(m_o, DEPTH * i + u + 1)
                    rows = ds((DEPTH * i + u) * P, P)
                    act.dma_start(s.qv_d[rows, :], qvk[:, u, 0:2 * D]).then_inc(m_st[u], 16)
                    act.dma_start(s.k_d[rows, :], qvk[:, u, 2 * D:]).then_inc(m_stk[u], 16)

                def step(i, u):
                    turned(i, u)
                    if back(i, u, 3):
                        store(*back(i, u, 3))

                turns(act, TILES, DEPTH, step)
                for n in (2, 1, 0):
                    store(*back(*LAST_TILE, n))
                wait_stores(act, m_st)
                wait_stores(act, m_stk)

            @block.vector
            def _(v):
                def normalise(i, u):
                    v.wait_ge(m_rs, DEPTH * i + u + 1)
                    if not first(i):
                        v.wait_ge(m_T, DEPTH * i + u - DEPTH + 1)
                    v.tensor_scalar(xn[:, u, :], xin[:, u, :], mv[:, u, 0:1], rs[:, u:u + 1], ALU.subtract,
                                    ALU.mult).then_inc(m_xn, 1)

                def run(now, last, old):
                    def fill(gap):
                        if gap == 0 and last:
                            normalise(*last)
                        if gap == 1 and old:
                            i, u = old
                            v.wait_ge(m_h, DEPTH * i + u + 1)
                            if not first(i):
                                v.wait_ge(m_st[u], 16 * i)
                                v.wait_ge(m_stk[u], 16 * i)
                            v.tensor_tensor(qvk[:, u, 0:2 * D], pQV[u % 2][:, :], bias[:, 0:2 * D], ALU.add)
                            v.tensor_tensor(qvk[:, u, 2 * D:], pKK[u % 2][:, :], bias[:, 2 * D:], ALU.add
                                            ).then_inc(m_o, 1)

                    if now:
                        i, u = now
                        v.wait_ge(m_x[u], 16 * (i + 1))
                        statistics(v, s.passed, xin[:, u, :], st[:, u, :], mv[:, u, :], ve[:, u:u + 1], m_bn, m_mv,
                                   m_var, DEPTH * i + u, fill)
                    else:
                        fill(0)
                        fill(1)

                v.wait_ge(m_w, 16 * 6)
                v.memset(s.acc[:, :, 0:D], 0.0)
                tiles_pipelined(v, run)


def edges1(nc, s):
    with ExitStack() as ctx:
        def sb(name, shape, dt=F32):
            return ctx.enter_context(nc.sbuf_tensor(name, shape, dt))

        R = sb("h_R", [P, 2, GROUP, CH, 2 * D])
        idx = sb("h_idx", [P, UNROLL, COLS], I32)
        drow = sb("h_drow", [P, 2, GROUP, EROW], BF16)
        kt = sb("h_kt", [P, 2, GROUP, D])
        OHT = sb("h_OHT", [P, 2, GROUP, EROW])
        OH = sb("h_OH", [P, 2, COLS, P])
        dcol = sb("h_dcol", [P, 2, COLS])
        prod = sb("h_prod", [P, 3, CH, D])
        sc = sb("h_sc", [P, COLS, HEADS])
        smax = sb("h_smax", [P, COLS])
        ex = sb("h_ex", [P, COLS, HEADS])
        ssum = sb("h_ssum", [P, COLS])
        minus = sb("h_minus", [P, COLS])
        pK = [ctx.enter_context(nc.psum_tensor(f"h_pK{n}", [P, CH, D], F32)) for n in range(GROUP)]
        pA = ctx.enter_context(nc.psum_tensor("h_pA", [P, GROUP, 512], F32))
        m_idx = s.sem("h_idx")
        m_g = [[s.sem(f"h_g{u}_{n}") for n in range(GROUP)] for u in (0, 1)]
        m_row = [s.sem(f"h_row{u}") for u in (0, 1)]
        m_kt = [s.sem(f"h_kt{u}") for u in (0, 1)]
        m_v, m_rowdist, m_coldist, m_oht, m_dcol, m_oh, m_k, m_pr, m_d, m_ex, m_V, m_agg, m_acc, m_r, m_minus = (
            s.sem("h_" + n) for n in ("v", "rowdist", "coldist", "oht", "dcol", "oh", "k", "pr", "d", "ex", "V", "agg", "acc",
                                      "r", "minus"))
        LINKS = 3

        def uses(i, u):
            return i * (UNROLL // 2) + u // 2 + 1

        with nc.Block() as block:
            @block.gpsimd
            def _(g):
                def gather(i, u):
                    b = UNROLL * i + u
                    h = u % 2
                    g.tensor_copy(idx[:, u, :], s.src_t[:, ds(b * GROUP, GROUP), :]).then_inc(m_idx, 1)
                    g.wait_ge(m_idx, b + 1)
                    g.sem_inc(s.passed, 1)
                    for n in range(COLS):
                        if n % CH == 0 and not (first(i) and u < 2):
                            g.wait_ge(m_agg, (b - 2) * GROUP + n // CH + 1)
                            g.sem_inc(s.passed, 1)
                        g.indirect_dma_start(R[:, h, n // CH, n % CH, :], None, s.qv_d[:, :],
                                             bass.IndirectOffsetOnAxis(ap=idx[:, u, n:n + 1], axis=0)
                                             ).then_inc(m_g[h][n // CH], 16)

                turns(g, GROUPS, UNROLL, gather)

            @block.sync
            def _(sp):
                def load(i, u):
                    b = UNROLL * i + u
                    if not (first(i) and u < 2):
                        sp.wait_ge(m_oht, b - 1)
                    sp.dma_start(drow[:, u % 2, :, :], s.drow_d[ds(b * GROUP, GROUP), :].partition_broadcast(P)
                                 ).then_inc(m_row[u % 2], 16)
                    tiles = load_tiles(nc, s, ENGINE.SP, b)
                    if not (first(i) and u < 2):
                        sp.wait_ge(m_k, (b - 1) * GROUP)
                    for n in range(GROUP):
                        sp.dma_start(kt[:, u % 2, n, :], s.k_d[ds(tiles[n] * P, P), :]).then_inc(m_kt[u % 2], 16)

                turns(sp, GROUPS, UNROLL, load)

            @block.tensor
            def _(pe):
                def expand(i, u):
                    b = UNROLL * i + u
                    pe.wait_ge(m_kt[u % 2], 16 * GROUP * uses(i, u))
                    pe.wait_ge(m_oht, b + 1)
                    for n in range(GROUP):
                        if not (first(i) and u == 0):
                            pe.wait_ge(m_pr, (b - 1) * GROUP + n + 1)
                        for j in range(CH):
                            last = pe.matmul(pK[n][:, j, :], OHT[:, u % 2, n, j * P:(j + 1) * P], kt[:, u % 2, n, :],
                                             start=True, stop=True)
                        last.then_inc(m_k, 1)

                def collect(i, u):
                    b = UNROLL * i + u
                    for n in range(GROUP):
                        pe.wait_ge(m_oh, b * GROUP + n + 1)
                        pe.wait_ge(m_V, b * GROUP + n + 1)
                        if before(i, u, UNROLL):
                            pe.wait_ge(m_acc, (b - 1) * GROUP + n + 1)
                        for j in range(CH):
                            last = pe.matmul(pA[:, n, 0:D], OH[:, u % 2, n * CH + j, :], R[:, u % 2, n, j, D:], start=j == 0,
                                             stop=j == CH - 1)
                        last.then_inc(m_agg, 1)

                def step(i, u, left=None):
                    if before(i, u, UNROLL):
                        collect(*before(i, u, UNROLL))
                    if left != 0:
                        expand(*after(i, u, UNROLL))

                expand(0, 0)
                turns(pe, GROUPS, UNROLL, step, peel_last=True)
                collect(GROUPS // UNROLL - 1, UNROLL - 1)

            @block.scalar
            def _(act):
                def row_distances(i, u):
                    act.wait_ge(m_row[u % 2], 16 * uses(i, u))
                    if not (first(i) and u < 2):
                        act.wait_ge(m_k, (UNROLL * i + u - 1) * GROUP)
                    act.activation(OHT[:, u % 2, :, :], drow[:, u % 2, :, :], ACT.Abs, bias=s.part[:, 0:1], scale=-1.0
                                   ).then_inc(m_rowdist, 1)

                def select_rows(i, u):
                    act.wait_ge(m_rowdist, UNROLL * i + u + 1)
                    act.activation(OHT[:, u % 2, :, :], OHT[:, u % 2, :, :], ACT.Relu, bias=s.ones[:, 0:1], scale=-1.0
                                   ).then_inc(m_oht, 1)

                def column_distances(i, u):
                    act.wait_ge(m_dcol, UNROLL * i + u + 1)
                    if not (first(i) and u < 2):
                        act.wait_ge(m_agg, (UNROLL * i + u - 1) * GROUP)
                    for n in range(COLS):
                        last = act.activation(OH[:, u % 2, n, :], s.iota[:, :], ACT.Abs, bias=dcol[:, u % 2, n:n + 1],
                                              scale=-1.0)
                    last.then_inc(m_coldist, 1)

                def select_columns(i, u):
                    b = UNROLL * i + u
                    act.wait_ge(m_coldist, b + 1)
                    act.wait_ge(m_r, b + 1)
                    act.activation(minus[:, :], ssum[:, :], ACT.Copy, scale=-1.0).then_inc(m_minus, 1)
                    act.wait_ge(m_minus, b + 1)
                    for n in range(COLS):
                        last = act.activation(OH[:, u % 2, n, :], OH[:, u % 2, n, :], ACT.Relu, bias=ssum[:, n:n + 1],
                                              scale=minus[:, n:n + 1])
                        if n % CH == CH - 1:
                            last.then_inc(m_oh, 1)

                def step(i, u, left=None):
                    b = UNROLL * i + u
                    act.copy(dcol[:, u % 2, :], s.dst_t[:, ds(b * GROUP, GROUP), :]).then_inc(m_dcol, 1)
                    ahead = left is None or left > 1
                    if ahead:
                        row_distances(*after(i, u, UNROLL, 2))
                    column_distances(i, u)
                    if ahead:
                        select_rows(*after(i, u, UNROLL, 2))
                    act.wait_ge(m_d, b + 1)
                    act.activation(ex[:, :, :], sc[:, :, :], ACT.Exp, scale=float(HD) ** -0.5).then_inc(m_ex, 1)
                    select_columns(i, u)

                for u in (0, 1):
                    row_distances(0, u)
                    select_rows(0, u)
                turns(act, GROUPS, UNROLL, step, peel_last=True)

            @block.vector
            def _(v):
                def product(i, u, n):
                    v.wait_ge(m_g[u % 2][n], 16 * CH * uses(i, u))
                    v.wait_ge(m_k, (UNROLL * i + u) * GROUP + n + 1)
                    if n >= 3:
                        v.wait_ge(m_pr, (UNROLL * i + u) * GROUP + n)
                    v.tensor_tensor(prod[:, n % 3, :, :], pK[n][:, :, :], R[:, u % 2, n, :, 0:D], ALU.mult
                                    ).then_inc(m_pr, 1)

                def score(i, u, n):
                    v.wait_ge(m_pr, (UNROLL * i + u) * GROUP + n + 1)
                    return v.tensor_reduce(sc[:, n * CH:(n + 1) * CH, :],
                                           prod[:, n % 3, :, :].rearrange("p c (h d) -> p (c h) d", d=HD), X, ALU.add)

                def weighted(i, u):
                    for n in range(GROUP):
                        rv = R[:, u % 2, n, :, D:].rearrange("p c (h d) -> p c h d", d=HD)
                        v.tensor_tensor(rv, rv, ex[:, n * CH:(n + 1) * CH, :].unsqueeze(3)
                                        .to_broadcast([P, CH, HEADS, HD]), ALU.mult).then_inc(m_V, 1)

                def add(i, u, tiles, n):
                    count = (UNROLL * i + u) * GROUP + n
                    v.wait_ge(m_agg, count + 1)
                    if n or before(i, u, UNROLL):
                        v.wait_ge(m_acc, count)
                    acc = s.acc[:, ds(tiles[n], 1), 0:D]
                    v.tensor_tensor(acc, acc, pA[:, n:n + 1, 0:D], ALU.add).then_inc(m_acc, 1)

                def step(i, u):
                    b = UNROLL * i + u
                    past = before(i, u, UNROLL)
                    if past:
                        weighted(*past)
                        tiles = load_tiles(nc, s, ENGINE.DVE, b - 1)
                    product(i, u, 0)
                    for n in range(1, GROUP):
                        product(i, u, n)
                        score(i, u, n - 1)
                    def fill(n):
                        if past:
                            add(*past, tiles, n)

                    score(i, u, GROUP - 1).then_inc(m_v, 1)
                    fill(0)
                    v.wait_ge(m_v, b * LINKS + 1)
                    v.tensor_reduce(smax[:, :], sc[:, :, :], X, ALU.max).then_inc(m_v, 1)
                    fill(1)
                    v.wait_ge(m_v, b * LINKS + 2)
                    v.tensor_tensor(sc[:, :, :], sc[:, :, :], smax[:, :].unsqueeze(2).to_broadcast([P, COLS, HEADS]),
                                    ALU.subtract).then_inc(m_d, 1)
                    fill(2)
                    v.wait_ge(m_ex, b + 1)
                    if past:
                        v.wait_ge(m_oh, b * GROUP)
                    v.tensor_reduce(ssum[:, :], ex[:, :, :], X, ALU.add).then_inc(m_v, 1)
                    fill(3)
                    v.wait_ge(m_v, b * LINKS + 3)
                    v.reciprocal(ssum[:, :], ssum[:, :]).then_inc(m_r, 1)

                turns(v, GROUPS, UNROLL, step)
                end = (GROUPS // UNROLL - 1, UNROLL - 1)
                weighted(*end)
                tiles = load_tiles(nc, s, ENGINE.DVE, GROUPS - 1)
                for n in range(GROUP):
                    add(*end, tiles, n)


def finish1(nc, s, a):
    with ExitStack() as ctx:
        def sb(name, shape, dt=F32):
            return ctx.enter_context(nc.sbuf_tensor(name, shape, dt))

        w = sb("o_w", [P, KD, D])
        rows = sb("o_rows", [P, 2, D])
        br = sb("o_br", [P, 1])
        g = sb("o_g", [P, 2, D])
        gT = sb("o_gT", [P, 2, KD, P])
        xin = sb("o_xin", [P, DEPTH, D])
        o = sb("o_o", [P, DEPTH, 2, D])
        junk = sb("o_junk", [P, D])
        dot = sb("o_dot", [P, DEPTH])
        st, mv, ve, rs = sb("o_st", [P, DEPTH, 6]), sb("o_mv", [P, DEPTH, 2]), sb("o_ve", [P, DEPTH]), sb("o_rs", [P, DEPTH])
        pT = [ctx.enter_context(nc.psum_tensor(f"o_pT{u}", [P, KD, P], F32)) for u in (0, 1)]
        pO = [ctx.enter_context(nc.psum_tensor(f"o_pO{u}", [P, D], F32)) for u in (0, 1)]
        m_w = s.sem("o_w")
        m_x = [s.sem(f"o_x{u}") for u in range(DEPTH)]
        m_st = [s.sem(f"o_st{u}") for u in range(DEPTH)]
        m_g, m_T, m_gT, m_p, m_pr, m_res, m_bn, m_mv, m_var, m_rs, m_o, m_dot = (
            s.sem("o_" + n) for n in ("g", "T", "gT", "p", "pr", "res", "bn", "mv", "var", "rs", "out", "dot"))

        with nc.Block() as block:
            @block.sync
            def _(sp):
                sp.dma_start(w[:, :, :], a["L1_gnn_Wo"].rearrange("(k p) n -> p k n", p=P)).then_inc(m_w, 16)
                sp.dma_start(rows[:, 0, :], a["L1_gnn_bo"].partition_broadcast(P)).then_inc(m_w, 16)
                sp.dma_start(rows[:, 1, :], a["L1_ffn_wr"].rearrange("d o -> (d o)").partition_broadcast(P)).then_inc(m_w, 16)
                sp.dma_start(br[:, :], a["L1_ffn_br"].partition_broadcast(P)).then_inc(m_w, 16)

                def load(i, u):
                    if not first(i):
                        sp.wait_ge(m_res, DEPTH * i + u - DEPTH + 1)
                    sp.dma_start(xin[:, u, :], s.x2_d[ds((DEPTH * i + u) * P, P), :]).then_inc(m_x[u], 16)

                turns(sp, TILES, DEPTH, load)

            @block.gpsimd
            def _(gp):
                roots(gp, s.half, ve, rs, m_var, m_rs)

            @block.tensor
            def _(pe):
                def transposes(i, u):
                    pe.wait_ge(m_g, DEPTH * i + u + 1)
                    if back(i, u, 2):
                        pe.wait_ge(m_gT, DEPTH * i + u - 1)
                    for k in range(KD):
                        last = pe.transpose(pT[u % 2][:, k, :], g[:, u % 2, k * P:(k + 1) * P], s.ident[:, :])
                    last.then_inc(m_T, 1)

                def product(i, u):
                    pe.wait_ge(m_gT, DEPTH * i + u + 1)
                    if back(i, u, 2):
                        pe.wait_ge(m_pr, DEPTH * i + u - 1)
                    for k in range(KD):
                        last = pe.matmul(pO[u % 2][:, :], gT[:, u % 2, k, :], w[:, k, :], start=k == 0, stop=k == KD - 1)
                    last.then_inc(m_p, 1)

                def step(i, u):
                    transposes(i, u)
                    if back(i, u, 1):
                        product(*back(i, u, 1))

                pe.wait_ge(m_w, 16 * 4)
                turns(pe, TILES, DEPTH, step)
                product(*LAST_TILE)

            @block.scalar
            def _(act):
                def stage(i, u):
                    if back(i, u, 2):
                        act.wait_ge(m_T, DEPTH * i + u - 1)
                    act.copy(g[:, u % 2:u % 2 + 1, :], s.acc[:, ds(DEPTH * i + u, 1), 0:D]).then_inc(m_g, 1)

                def turned(i, u):
                    act.wait_ge(m_T, DEPTH * i + u + 1)
                    if back(i, u, 2):
                        act.wait_ge(m_p, DEPTH * i + u - 1)
                    act.copy(gT[:, u % 2, :, :], pT[u % 2][:, :, :]).then_inc(m_gT, 1)

                def store(i, u):
                    act.wait_ge(m_o, DEPTH * i + u + 1)
                    act.dma_start(s.x3_d[ds((DEPTH * i + u) * P, P), :], o[:, u, :, :]).then_inc(m_st[u], 16)

                def step(i, u):
                    stage(i, u)
                    if back(i, u, 1):
                        turned(*back(i, u, 1))
                    if back(i, u, 3):
                        store(*back(i, u, 3))

                turns(act, TILES, DEPTH, step)
                turned(*LAST_TILE)
                for n in (2, 1, 0):
                    store(*back(*LAST_TILE, n))
                wait_stores(act, m_st)

            @block.vector
            def _(v):
                def bias(i, u):
                    t = DEPTH * i + u
                    v.wait_ge(m_p, t + 1)
                    if not first(i):
                        v.wait_ge(m_st[u], 16 * i)
                        v.wait_ge(m_dot, t - DEPTH + 1)
                    v.tensor_tensor(o[:, u, 0, :], pO[u % 2][:, :], rows[:, 0, :], ALU.add).then_inc(m_pr, 1)

                def residual(i, u):
                    v.wait_ge(m_pr, DEPTH * i + u + 1)
                    v.wait_ge(m_x[u], 16 * (i + 1))
                    v.tensor_tensor(o[:, u, 0, :], o[:, u, 0, :], xin[:, u, :], ALU.add).then_inc(m_res, 1)

                def normalise(i, u):
                    v.wait_ge(m_rs, DEPTH * i + u + 1)
                    v.tensor_scalar(o[:, u, 1, :], o[:, u, 0, :], mv[:, u, 0:1], rs[:, u:u + 1], ALU.subtract,
                                    ALU.mult).then_inc(m_o, 1)

                def weight(i, u):
                    t = DEPTH * i + u
                    v.wait_ge(m_o, t + 1)
                    if back(i, u, 1):
                        v.wait_ge(m_dot, t)
                    v.tensor_tensor_reduce(junk[:, :], o[:, u, 1, :], rows[:, 1, :], 1.0, 0.0, ALU.mult,
                                           ALU.add, dot[:, u:u + 1]).then_inc(m_dot, 1)

                def run(now, last, old):
                    def fill(gap):
                        if gap == 0 and last:
                            weight(*last)
                        if gap == 1 and last:
                            i, u = last
                            t = DEPTH * i + u
                            v.wait_ge(m_dot, t + 1)
                            v.tensor_scalar(s.wcol[:, ds(t, 1)], dot[:, u:u + 1], br[:, 0:1], None, ALU.add)

                    if now:
                        bias(*now)
                    if last:
                        normalise(*last)
                    if now:
                        residual(*now)
                        i, u = now
                        v.wait_ge(m_res, DEPTH * i + u + 1)
                        statistics(v, s.passed, o[:, u, 0, :], st[:, u, :], mv[:, u, :], ve[:, u:u + 1], m_bn, m_mv,
                                   m_var, DEPTH * i + u, fill)
                    else:
                        fill(0)
                        fill(1)

                v.wait_ge(m_w, 16 * 4)
                tiles_pipelined(v, run)


def select1(nc, s):
    BITS = (16, 16, 14)
    DIGIT = 3
    with ExitStack() as ctx:
        def sb(name, shape, dt=F32):
            return ctx.enter_context(nc.sbuf_tensor(name, shape, dt))

        bits = sb("s_bits", [P, TILES], I32)
        hi_i = sb("s_hi_i", [P, TILES], I32)
        lo_i = sb("s_lo_i", [P, TILES], I32)
        hi, lo, neg, tmp = sb("s_hi", [P, TILES]), sb("s_lo", [P, TILES]), sb("s_neg", [P, TILES]), sb("s_tmp", [P, TILES])
        real, chosen = sb("s_real", [P, TILES]), sb("s_chosen", [P, TILES])
        need, low, bit, hits = (sb("s_" + n, [P, 1]) for n in ("need", "low", "bit", "hits"))
        cand, cnt, got = (sb("s_" + n, [P, DIGIT]) for n in ("cand", "cnt", "got"))
        over = sb("s_over", [P, DIGIT, TILES])
        pc = ctx.enter_context(nc.psum_tensor("s_pc", [P, DIGIT], F32))
        m_v, m_cnt, m_sum = s.sem("s_v"), s.sem("s_cnt"), s.sem("s_sum")
        sums = sum(BITS) // 2 + 2

        with nc.Block() as block:
            @block.tensor
            def _(pe):
                with pe.Fori(0, sums) as i:
                    pe.wait_ge(m_cnt, i + 1)
                    pe.matmul(pc[:, :], s.ones[:, :], cnt[:, :], start=True, stop=True).then_inc(m_sum, 1)

            @block.vector
            def _(v):
                link = linker(v, m_v, 0)
                link(v.tensor_copy(bits[:, :], s.wcol[:, :].bitcast(I32)))
                link(v.tensor_scalar(hi_i[:, :], bits[:, :], 16, 0xFFFF, ALU.logical_shift_right, ALU.bitwise_and))
                link(v.tensor_scalar(lo_i[:, :], bits[:, :], 0xFFFF, None, ALU.bitwise_and))
                link(v.tensor_copy(hi[:, :], hi_i[:, :]))
                link(v.tensor_copy(lo[:, :], lo_i[:, :]))
                link(v.tensor_scalar(neg[:, :], hi[:, :], 32768.0, None, ALU.is_ge))
                link(v.tensor_scalar(tmp[:, :], lo[:, :], -2.0, 65535.0, ALU.mult, ALU.add))
                link(v.tensor_tensor(tmp[:, :], tmp[:, :], neg[:, :], ALU.mult))
                link(v.tensor_tensor(lo[:, :], lo[:, :], tmp[:, :], ALU.add))
                link(v.tensor_scalar(tmp[:, :], hi[:, :], -2.0, 32767.0, ALU.mult, ALU.add))
                link(v.tensor_tensor(tmp[:, :], tmp[:, :], neg[:, :], ALU.mult))
                link(v.tensor_scalar(hi[:, :], hi[:, :], 32768.0, None, ALU.add))
                link(v.tensor_tensor(hi[:, :], hi[:, :], tmp[:, :], ALU.add))
                link(v.tensor_scalar(real[:, :], s.node[:, :], float(N), None, ALU.is_lt))

                def masked(digit, mask):
                    link(v.tensor_scalar(digit, digit, 1.0, None, ALU.add))
                    link(v.tensor_tensor(digit, digit, mask, ALU.mult))
                    link(v.tensor_scalar(digit, digit, -1.0, None, ALU.add))

                masked(hi[:, :], real[:, :])
                link(v.memset(need[:, :], float(TOPK)))
                link(v.memset(chosen[:, :], 0.0))
                at, summed = link.count[0], 0

                link(v.memset(cnt[:, :], 0.0))
                at = link.count[0]

                def search(digit, nbits):
                    v.memset(low[:, :], 0.0).then_inc(m_v, 1)
                    v.memset(bit[:, :], float(2 ** (nbits - 2))).then_inc(m_v, 1)
                    v.wait_ge(m_v, at + 2)
                    with v.Fori(0, nbits // 2) as i:
                        step = linker(v, m_v, i * 6 + (at + 2))
                        step(v.tensor_scalar(cand[:, :], s.iota[:, 1:1 + DIGIT], bit[:, 0:1], low[:, 0:1], ALU.mult,
                                             ALU.add))
                        for c in range(DIGIT):
                            last = v.tensor_scalar(over[:, c, :], digit, cand[:, c:c + 1], None, ALU.is_ge)
                        step(last)
                        v.tensor_reduce(cnt[:, :], over[:, :, :], X, ALU.add).then_inc(m_cnt, 1)
                        v.wait_ge(m_sum, i + (summed + 1))
                        step(v.tensor_scalar(got[:, :], pc[:, :], need[:, 0:1], None, ALU.is_ge))
                        step(v.tensor_reduce(hits[:, :], got[:, :], X, ALU.add))
                        step(v.scalar_tensor_tensor(low[:, :], hits[:, :], bit[:, 0:1], low[:, :], ALU.mult, ALU.add))
                        step(v.tensor_scalar(bit[:, :], bit[:, :], 0.25, None, ALU.mult))
                    return at + 2 + 6 * (nbits // 2), summed + nbits // 2

                def settle(digit, following):
                    step = linker(v, m_v, at)
                    step(v.tensor_scalar(tmp[:, :], digit, low[:, 0:1], None, ALU.is_gt))
                    step(v.tensor_tensor(chosen[:, :], chosen[:, :], tmp[:, :], ALU.add))
                    v.tensor_reduce(cnt[:, 0:1], tmp[:, :], X, ALU.add).then_inc(m_cnt, 1)
                    v.wait_ge(m_sum, summed + 1)
                    step(v.tensor_tensor(need[:, :], need[:, :], pc[:, 0:1], ALU.subtract))
                    step(v.tensor_scalar(tmp[:, :], digit, low[:, 0:1], None, ALU.is_equal))
                    step(v.tensor_scalar(following, following, 1.0, None, ALU.add))
                    step(v.tensor_tensor(following, following, tmp[:, :], ALU.mult))
                    step(v.tensor_scalar(following, following, -1.0, None, ALU.add))
                    return at + step.count[0], summed + 1

                at, summed = search(hi[:, :], BITS[0])
                at, summed = settle(hi[:, :], lo[:, :])
                at, summed = search(lo[:, :], BITS[1])
                v.tensor_scalar(neg[:, :], s.node[:, :], -1.0, float(2 ** BITS[2] - 1), ALU.mult, ALU.add).then_inc(m_v, 1)
                at += 1
                v.wait_ge(m_v, at)
                at, summed = settle(lo[:, :], neg[:, :])
                at, summed = search(neg[:, :], BITS[2])
                step = linker(v, m_v, at)
                step(v.tensor_scalar(tmp[:, :], neg[:, :], low[:, 0:1], None, ALU.is_ge))
                step(v.tensor_tensor(chosen[:, :], chosen[:, :], tmp[:, :], ALU.add))
                step(v.tensor_tensor(s.wcol[:, :], s.wcol[:, :], chosen[:, :], ALU.mult))


def build(nc, x, src2, dst2, a, out):
    with ExitStack() as ctx:
        s = Shared()

        def sb(name, shape, dt=F32):
            return ctx.enter_context(nc.sbuf_tensor(name, shape, dt))

        used = []

        def sem(name):
            used.append(nc.alloc_semaphore(name))
            return used[-1]

        def release_semaphores():
            nc.all_engine_barrier()
            nc.clear_and_free_semaphores(used)
            nc.all_engine_barrier()
            used.clear()

        s.sem = sem
        s.passed = nc.alloc_semaphore("passed")
        s.acc = sb("acc", [P, TILES, ACOLS])
        s.iota = sb("iota", [P, P])
        s.iota_b = sb("iota_b", [P, P], BF16)
        s.part_i = sb("part_i", [P, 1], I32)
        s.part = sb("part", [P, 1])
        s.node_i = sb("node_i", [P, TILES], I32)
        s.node = sb("node", [P, TILES])
        s.ones = sb("ones", [P, P])
        s.half = sb("half", [P, 1])
        s.ident = sb("ident", [P, P])
        s.tile_i = sb("tile_i", [1, IPAD], I32)
        s.src_t = sb("src_t", [P, IPAD, CH], I32)
        s.dst_t = sb("dst_t", [P, IPAD, CH])
        s.xsum = sb("xsum", [P, D])
        s.expert_i = sb("expert_i", [1, 2], I32)
        s.wexp = sb("wexp", [P, 2])
        s.wcol = sb("wcol", [P, TILES])
        s.drow_d = nc.dram_tensor("drow_d", [IPAD, EROW], BF16).ap()
        s.seg_d = nc.dram_tensor("seg_d", [IPAD, EROW + 1], F32).ap()
        s.hq_d = nc.dram_tensor("hq_d", [NPAD, D + 1], F32).ap()
        s.qv_d = nc.dram_tensor("qv_d", [NPAD, 2 * D], F32).ap()
        s.k_d = nc.dram_tensor("k_d", [NPAD, D], F32).ap()
        s.x1_d = nc.dram_tensor("x1_d", [NPAD, 2 * D], F32).ap()
        s.x2_d = nc.dram_tensor("x2_d", [NPAD, D], F32).ap()
        s.x3_d = nc.dram_tensor("x3_d", [NPAD, 2 * D], F32).ap()
        with ExitStack() as layer0:
            def sb0(name, shape, dt=F32):
                return layer0.enter_context(nc.sbuf_tensor(name, shape, dt))

            s.iota_i = sb0("iota_i", [P, IPAD], I32)
            s.item_no = sb0("item_no", [P, IPAD])
            s.fresh = sb0("fresh", [P, IPAD])
            s.first_i = sb0("first_i", [1, EROWS], I32)
            s.m_first = s.sem("t_first")
            s.kf = sb0("kf", [P, TILES])
            s.k0 = sb0("k0", [P, TILES, KPARTS], BF16)
            constants(nc, s)
            project0(nc, s, x, dst2, a["L0_gnn_Wv"], a["L0_gnn_bv"], a["L0_gnn_wq"], a["L0_gnn_bq"], a["L0_gnn_wk"],
                     a["L0_gnn_bk"])
            item_tables(nc, s, src2, dst2)
            edges0(nc, s)
        finish0(nc, s, x)
        route0(nc, s, a)
        feed_forward0(nc, s, a)
        release_semaphores()
        project1(nc, s, a)
        edges1(nc, s)
        finish1(nc, s, a)
        select1(nc, s)
        feed_forward1(nc, s, a, out)


_WEIGHTS = ['L0_gnn_Wv', 'L0_gnn_bv', 'L0_gnn_wq', 'L0_gnn_bq', 'L0_gnn_wk', 'L0_gnn_bk', 'L0_ffn_Wr', 'L0_ffn_br',
            'L0_ffn_W1', 'L0_ffn_b1', 'L0_ffn_W2', 'L0_ffn_b2', 'L0_ffn_gamma', 'L0_ffn_beta', 'L1_gnn_Wq', 'L1_gnn_bq',
            'L1_gnn_Wk', 'L1_gnn_bk', 'L1_gnn_Wv', 'L1_gnn_bv', 'L1_gnn_Wo', 'L1_gnn_bo', 'L1_ffn_wr', 'L1_ffn_br',
            'L1_ffn_w1', 'L1_ffn_b1', 'L1_ffn_w2', 'L1_ffn_b2']


def kernel(**inputs):
    import numpy as np
    import concourse.bacc as bacc
    from concourse.bass_utils import run_bass_kernel_spmd

    nc = bacc.Bacc("TRN2", target_bir_lowering=False, num_devices=1)
    arrays, args = {}, {}
    laid = {"x": np.pad(np.asarray(inputs["x"]), ((0, NPAD - N), (0, 0)))}
    laid["src2"] = np.pad(np.asarray(inputs["src"]), (0, EROWS * EROW - EDGES)).reshape(EROWS, EROW)
    laid["dst2"] = np.pad(np.asarray(inputs["dst"]), (0, EROWS * EROW - EDGES),
                          constant_values=2 * NPAD).reshape(EROWS, EROW)
    for name in _WEIGHTS:
        w = np.asarray(inputs[name])
        if name in ("L1_gnn_Wq", "L1_gnn_Wk", "L1_gnn_Wv", "L1_gnn_Wo"):
            w = w.T
        laid[name] = w.reshape(1) if w.ndim == 0 else w
    for name, value in laid.items():
        value = np.ascontiguousarray(value)
        arrays["in_" + name] = value
        args[name] = nc.dram_tensor("in_" + name, value.shape, mybir.dt.from_np(value.dtype), kind="ExternalInput").ap()
    out = nc.dram_tensor("out", (N, D), F32, kind="ExternalOutput").ap()
    build(nc, args.pop("x"), args.pop("src2"), args.pop("dst2"), args, out)
    return run_bass_kernel_spmd(nc, [arrays], core_ids=[0]).results[0]["out"]
```
